# Optimizing a Trainium2 kernel written in Bass

```python
import numpy as np
import jax
import jax.numpy as jnp

def _softmax(x, axis=-1):
    return jax.nn.softmax(x, axis=axis)

def _gelu(x):
    return jax.nn.gelu(x, approximate=True)

def _silu(x):
    return jax.nn.silu(x)

def _sigmoid(x):
    return jax.nn.sigmoid(x)

def _layernorm(x, axis=-1, eps=1e-05):
    m = jnp.mean(x, axis=axis, keepdims=True)
    v = jnp.var(x, axis=axis, keepdims=True)
    return (x - m) / jnp.sqrt(v + eps)

def _scatter_add(tgt, idx, src, axis=0):
    return tgt.at[idx].add(src)

def _segment_sum(src, seg, n):
    return jax.ops.segment_sum(src, seg, n)
kernel_name = 'mk_metaformer_d4_conv_nhwc384_r4_c60a18'

def setup_inputs(seed: int=0):
    np.random.seed(seed)
    _w = jnp.asarray

    def _rec_inputs():
        import jax
        import jax.numpy as jnp
        _gk = jax.random.key(seed)
        x = -4.65e-05 + 0.9999 * jax.random.normal(jax.random.fold_in(_gk, 1), (16, 16, 16, 96), jnp.float32)
        return x
    x = _rec_inputs()

    def _L0_conv_setup():
        import jax, jax.numpy as jnp
        import numpy as np
        IN_CH = 96
        HEAD_DIM = 32
        MAX_SEQ = 16
        N_HEADS = IN_CH // HEAD_DIM
        PART = int(np.sqrt(MAX_SEQ))
        SCALE = HEAD_DIM ** (-0.5)

        def _relative_position_index():
            h = np.arange(PART)
            coords = np.stack(np.meshgrid(h, h, indexing='ij')).reshape(2, -1)
            rel = coords[:, :, None] - coords[:, None, :]
            rel = rel.transpose(1, 2, 0).astype(np.int64)
            rel[:, :, 0] += PART - 1
            rel[:, :, 1] += PART - 1
            rel[:, :, 0] *= 2 * PART - 1
            return rel.sum(-1).reshape(-1)
        REL_IDX = jnp.asarray(_relative_position_index())
        key = jax.random.key(seed)
        ks = jax.random.split(key, 6)
        B, G, P, D = (32, 16, MAX_SEQ, IN_CH)
        x = jax.random.normal(ks[0], (B, G, P, D), dtype=jnp.float32)
        Wqkv = jax.random.normal(ks[1], (D, 3 * D), dtype=jnp.float32) * D ** (-0.5)
        bqkv = jnp.zeros((3 * D,), dtype=jnp.float32)
        Wm = jax.random.normal(ks[2], (D, D), dtype=jnp.float32) * D ** (-0.5)
        bm = jnp.zeros((D,), dtype=jnp.float32)
        rel_table = jax.random.normal(ks[3], ((2 * PART - 1) ** 2, N_HEADS), dtype=jnp.float32) * 0.02
        return {'x': x, 'Wqkv': Wqkv, 'bqkv': bqkv, 'Wm': Wm, 'bm': bm, 'rel_table': rel_table}
    _L0_conv_all = _L0_conv_setup()
    _L0_conv_in = {k: v for k, v in _L0_conv_all.items() if k in ('Wqkv', 'bqkv', 'Wm', 'bm', 'rel_table')}
    del _L0_conv_all

    def _L0_ffn_setup():
        import jax, jax.numpy as jnp
        import numpy as np
        NUM_GROUPS = 5
        EPS = 1e-05
        QB = 128.0

        def _binarize_weights_groupwise(W):
            n_out = W.shape[0]
            gs = n_out // NUM_GROUPS
            Wb = jnp.zeros_like(W)
            for g in range(NUM_GROUPS):
                wg = W[g * gs:(g + 1) * gs]
                z = wg - wg.mean()
                ste = z + jax.lax.stop_gradient(jnp.sign(z) - z)
                Wb = Wb.at[g * gs:(g + 1) * gs].set(ste)
            return Wb

        def _quantize_activations_groupwise(x):
            n = x.shape[0]
            gs = n // NUM_GROUPS
            xq = jnp.zeros_like(x)
            for g in range(NUM_GROUPS):
                ag = x[g * gs:(g + 1) * gs]
                gamma = jnp.max(jnp.abs(ag))
                xq = xq.at[g * gs:(g + 1) * gs].set(jnp.clip(ag * QB / (gamma + EPS), -QB + EPS, QB - EPS))
            return xq

        def _bitlinear(x, W, b):
            Wb = _binarize_weights_groupwise(W)
            y = jnp.einsum('btc,oc->bto', x, Wb) + b
            return _quantize_activations_groupwise(y)
        key = jax.random.key(seed)
        k1, k2, k3, k4, k5 = jax.random.split(key, 5)
        B, T, C = (10, 512, 96)
        H = 4 * C
        lim1 = 1.0 / np.sqrt(C)
        lim2 = 1.0 / np.sqrt(H)
        x = jax.random.normal(k1, (B, T, C), dtype=jnp.float32)
        W1 = jax.random.uniform(k2, (H, C), minval=-lim1, maxval=lim1, dtype=jnp.float32)
        b1 = jax.random.uniform(k3, (H,), minval=-lim1, maxval=lim1, dtype=jnp.float32)
        W2 = jax.random.uniform(k4, (C, H), minval=-lim2, maxval=lim2, dtype=jnp.float32)
        b2 = jax.random.uniform(k5, (C,), minval=-lim2, maxval=lim2, dtype=jnp.float32)
        return {'x': x, 'W1': W1, 'b1': b1, 'W2': W2, 'b2': b2}
    _L0_ffn_all = _L0_ffn_setup()
    _L0_ffn_in = {k: v for k, v in _L0_ffn_all.items() if k in ('W1', 'b1', 'W2', 'b2')}
    del _L0_ffn_all

    def _L1_conv_setup():
        import jax, jax.numpy as jnp
        import numpy as np
        DIM = 96
        DIM_HEAD = 32
        HEADS = DIM // DIM_HEAD
        INNER = HEADS * DIM_HEAD
        WSZ = 8
        WSZ2 = 8
        SCALE = DIM_HEAD ** (-0.5)
        key = jax.random.key(seed)
        k1, k2, k3, k4 = jax.random.split(key, 4)
        B, H, W = (32, 16, 16)
        x = jax.random.normal(k1, (B, H, W, DIM), dtype=jnp.float32)
        w_qkv = jax.random.normal(k2, (DIM, 3 * INNER), dtype=jnp.float32) * DIM ** (-0.5)
        w_out = jax.random.normal(k3, (INNER, DIM), dtype=jnp.float32) * INNER ** (-0.5)
        b_out = jax.random.normal(k4, (DIM,), dtype=jnp.float32) * 0.02
        return {'x': x, 'w_qkv': w_qkv, 'w_out': w_out, 'b_out': b_out}
    _L1_conv_all = _L1_conv_setup()
    _L1_conv_in = {k: v for k, v in _L1_conv_all.items() if k in ('w_qkv', 'w_out', 'b_out')}
    del _L1_conv_all

    def _L1_ffn_setup():
        import jax, jax.numpy as jnp
        import numpy as np
        NUM_EXPERTS = 4
        TOP_K = 2
        DIM = 96
        HID = 4 * DIM
        key = jax.random.key(seed)
        ks = jax.random.split(key, 5)
        B, S = (16, 512)
        scale_in = 1.0 / np.sqrt(DIM)
        scale_hid = 1.0 / np.sqrt(HID)
        return {'x': jax.random.normal(ks[0], (B, S, DIM), dtype=jnp.float32), 'gate_w': jax.random.normal(ks[1], (DIM, NUM_EXPERTS), dtype=jnp.float32) * scale_in, 'gate_b': jnp.zeros((NUM_EXPERTS,), dtype=jnp.float32), 'w1': jax.random.normal(ks[2], (NUM_EXPERTS, DIM, HID), dtype=jnp.float32) * scale_in, 'b1': jnp.zeros((NUM_EXPERTS, HID), dtype=jnp.float32), 'w2': jax.random.normal(ks[3], (NUM_EXPERTS, HID, DIM), dtype=jnp.float32) * scale_hid, 'b2': jnp.zeros((NUM_EXPERTS, DIM), dtype=jnp.float32)}
    _L1_ffn_all = _L1_ffn_setup()
    _L1_ffn_in = {k: v for k, v in _L1_ffn_all.items() if k in ('gate_w', 'gate_b', 'w1', 'b1', 'w2', 'b2')}
    del _L1_ffn_all

    def _L2_conv_setup():
        import jax, jax.numpy as jnp
        import numpy as np
        NUM_BLOCKS = 8
        LAMBDA = 0.01

        def softshrink(x, lam):
            return jnp.sign(x) * jnp.maximum(jnp.abs(x) - lam, 0.0)
        key = jax.random.key(seed)
        ks = jax.random.split(key, 8)
        B, H, W, C = (32, 56, 56, 96)
        med = 192
        nb, bs = (NUM_BLOCKS, med // NUM_BLOCKS)
        scale = 0.02
        return {'x': jax.random.normal(ks[0], (B, H, W, C), dtype=jnp.float32), 'w_pw1': jax.random.normal(ks[1], (C, med), dtype=jnp.float32) * 0.02, 'star_scale': jnp.ones((1,), dtype=jnp.float32), 'star_bias': jnp.zeros((1,), dtype=jnp.float32), 'w1': scale * jax.random.normal(ks[2], (2, nb, bs, bs), dtype=jnp.float32), 'b1': scale * jax.random.normal(ks[3], (2, nb, bs), dtype=jnp.float32), 'w2': scale * jax.random.normal(ks[4], (2, nb, bs, bs), dtype=jnp.float32), 'b2': scale * jax.random.normal(ks[5], (2, nb, bs), dtype=jnp.float32), 'w_pw2': jax.random.normal(ks[6], (med, C), dtype=jnp.float32) * 0.02}
    _L2_conv_all = _L2_conv_setup()
    _L2_conv_in = {k: v for k, v in _L2_conv_all.items() if k in ('w_pw1', 'star_scale', 'star_bias', 'w1', 'b1', 'w2', 'b2', 'w_pw2')}
    del _L2_conv_all

    def _L2_ffn_setup():
        import jax, jax.numpy as jnp
        import numpy as np
        NUM_EXPERTS = 4
        TOP_K = 2
        DIM = 96
        HID = 4 * DIM
        key = jax.random.key(seed)
        ks = jax.random.split(key, 5)
        B, S = (16, 512)
        scale_in = 1.0 / np.sqrt(DIM)
        scale_hid = 1.0 / np.sqrt(HID)
        return {'x': jax.random.normal(ks[0], (B, S, DIM), dtype=jnp.float32), 'gate_w': jax.random.normal(ks[1], (DIM, NUM_EXPERTS), dtype=jnp.float32) * scale_in, 'gate_b': jnp.zeros((NUM_EXPERTS,), dtype=jnp.float32), 'w1': jax.random.normal(ks[2], (NUM_EXPERTS, DIM, HID), dtype=jnp.float32) * scale_in, 'b1': jnp.zeros((NUM_EXPERTS, HID), dtype=jnp.float32), 'w2': jax.random.normal(ks[3], (NUM_EXPERTS, HID, DIM), dtype=jnp.float32) * scale_hid, 'b2': jnp.zeros((NUM_EXPERTS, DIM), dtype=jnp.float32)}
    _L2_ffn_all = _L2_ffn_setup()
    _L2_ffn_in = {k: v for k, v in _L2_ffn_all.items() if k in ('gate_w', 'gate_b', 'w1', 'b1', 'w2', 'b2')}
    del _L2_ffn_all

    def _L3_conv_setup():
        import jax, jax.numpy as jnp
        import numpy as np
        A = -0.75

        def _cubic(t):
            at = jnp.abs(t)
            w1 = ((A + 2.0) * at - (A + 3.0)) * at * at + 1.0
            w2 = A * (((at - 5.0) * at + 8.0) * at - 4.0)
            return jnp.where(at <= 1.0, w1, jnp.where(at < 2.0, w2, 0.0))

        def _resize_axis(x, new, axis):
            old = x.shape[axis]
            pos = jnp.arange(new, dtype=jnp.float32) * ((old - 1) / (new - 1))
            i0 = jnp.floor(pos).astype(jnp.int32)
            frac = pos - i0.astype(jnp.float32)
            offs = jnp.array([-1, 0, 1, 2], dtype=jnp.int32)
            idx = jnp.clip(i0[None, :] + offs[:, None], 0, old - 1)
            w = _cubic(frac[None, :] - offs[:, None].astype(jnp.float32))
            g = jnp.take(x, idx, axis=axis)
            wshape = [1] * g.ndim
            wshape[axis] = 4
            wshape[axis + 1] = new
            return jnp.sum(g * w.reshape(wshape), axis=axis)

        def _bicubic_ac(x, new_h, new_w):
            return _resize_axis(_resize_axis(x, new_h, 0), new_w, 1)
        key = jax.random.key(seed)
        ks = jax.random.split(key, 6)
        B, H, W, dim = (16, 56, 56, 96)
        med = 2 * dim
        hid = int(0.25 * dim)
        nf = 4
        return {'x': jax.random.normal(ks[0], (B, H, W, dim), jnp.float32), 'pwconv1_w': jax.random.normal(ks[1], (dim, med), jnp.float32) / np.sqrt(dim), 'act1_scale': jnp.ones((1,), jnp.float32), 'act1_bias': jnp.zeros((1,), jnp.float32), 'fc1_w': jax.random.normal(ks[2], (dim, hid), jnp.float32) / np.sqrt(dim), 'mlp_scale': jnp.ones((1,), jnp.float32), 'mlp_bias': jnp.zeros((1,), jnp.float32), 'fc2_w': jax.random.normal(ks[3], (hid, nf * med), jnp.float32) / np.sqrt(hid), 'complex_weights': jax.random.normal(ks[4], (14, 8, nf, 2), jnp.float32) * 0.02, 'pwconv2_w': jax.random.normal(ks[5], (med, dim), jnp.float32) / np.sqrt(med)}
    _L3_conv_all = _L3_conv_setup()
    _L3_conv_in = {k: v for k, v in _L3_conv_all.items() if k in ('pwconv1_w', 'act1_scale', 'act1_bias', 'fc1_w', 'mlp_scale', 'mlp_bias', 'fc2_w', 'complex_weights', 'pwconv2_w')}
    del _L3_conv_all

    def _L3_ffn_setup():
        import jax, jax.numpy as jnp
        import numpy as np
        NUM_EXPERTS = 4
        TOP_K = 2
        DIM = 96
        HID = 4 * DIM
        key = jax.random.key(seed)
        ks = jax.random.split(key, 5)
        B, S = (16, 512)
        scale_in = 1.0 / np.sqrt(DIM)
        scale_hid = 1.0 / np.sqrt(HID)
        return {'x': jax.random.normal(ks[0], (B, S, DIM), dtype=jnp.float32), 'gate_w': jax.random.normal(ks[1], (DIM, NUM_EXPERTS), dtype=jnp.float32) * scale_in, 'gate_b': jnp.zeros((NUM_EXPERTS,), dtype=jnp.float32), 'w1': jax.random.normal(ks[2], (NUM_EXPERTS, DIM, HID), dtype=jnp.float32) * scale_in, 'b1': jnp.zeros((NUM_EXPERTS, HID), dtype=jnp.float32), 'w2': jax.random.normal(ks[3], (NUM_EXPERTS, HID, DIM), dtype=jnp.float32) * scale_hid, 'b2': jnp.zeros((NUM_EXPERTS, DIM), dtype=jnp.float32)}
    _L3_ffn_all = _L3_ffn_setup()
    _L3_ffn_in = {k: v for k, v in _L3_ffn_all.items() if k in ('gate_w', 'gate_b', 'w1', 'b1', 'w2', 'b2')}
    del _L3_ffn_all
    return {'x': x, 'L0_conv_Wqkv': _L0_conv_in['Wqkv'], 'L0_conv_bqkv': _L0_conv_in['bqkv'], 'L0_conv_Wm': _L0_conv_in['Wm'], 'L0_conv_bm': _L0_conv_in['bm'], 'L0_conv_rel_table': _L0_conv_in['rel_table'], 'L0_ffn_W1': _L0_ffn_in['W1'], 'L0_ffn_b1': _L0_ffn_in['b1'], 'L0_ffn_W2': _L0_ffn_in['W2'], 'L0_ffn_b2': _L0_ffn_in['b2'], 'L1_conv_w_qkv': _L1_conv_in['w_qkv'], 'L1_conv_w_out': _L1_conv_in['w_out'], 'L1_conv_b_out': _L1_conv_in['b_out'], 'L1_ffn_gate_w': _L1_ffn_in['gate_w'], 'L1_ffn_gate_b': _L1_ffn_in['gate_b'], 'L1_ffn_w1': _L1_ffn_in['w1'], 'L1_ffn_b1': _L1_ffn_in['b1'], 'L1_ffn_w2': _L1_ffn_in['w2'], 'L1_ffn_b2': _L1_ffn_in['b2'], 'L2_conv_w_pw1': _L2_conv_in['w_pw1'], 'L2_conv_star_scale': _L2_conv_in['star_scale'], 'L2_conv_star_bias': _L2_conv_in['star_bias'], 'L2_conv_w1': _L2_conv_in['w1'], 'L2_conv_b1': _L2_conv_in['b1'], 'L2_conv_w2': _L2_conv_in['w2'], 'L2_conv_b2': _L2_conv_in['b2'], 'L2_conv_w_pw2': _L2_conv_in['w_pw2'], 'L2_ffn_gate_w': _L2_ffn_in['gate_w'], 'L2_ffn_gate_b': _L2_ffn_in['gate_b'], 'L2_ffn_w1': _L2_ffn_in['w1'], 'L2_ffn_b1': _L2_ffn_in['b1'], 'L2_ffn_w2': _L2_ffn_in['w2'], 'L2_ffn_b2': _L2_ffn_in['b2'], 'L3_conv_pwconv1_w': _L3_conv_in['pwconv1_w'], 'L3_conv_act1_scale': _L3_conv_in['act1_scale'], 'L3_conv_act1_bias': _L3_conv_in['act1_bias'], 'L3_conv_fc1_w': _L3_conv_in['fc1_w'], 'L3_conv_mlp_scale': _L3_conv_in['mlp_scale'], 'L3_conv_mlp_bias': _L3_conv_in['mlp_bias'], 'L3_conv_fc2_w': _L3_conv_in['fc2_w'], 'L3_conv_complex_weights': _L3_conv_in['complex_weights'], 'L3_conv_pwconv2_w': _L3_conv_in['pwconv2_w'], 'L3_ffn_gate_w': _L3_ffn_in['gate_w'], 'L3_ffn_gate_b': _L3_ffn_in['gate_b'], 'L3_ffn_w1': _L3_ffn_in['w1'], 'L3_ffn_b1': _L3_ffn_in['b1'], 'L3_ffn_w2': _L3_ffn_in['w2'], 'L3_ffn_b2': _L3_ffn_in['b2']}

def reference(x, L0_conv_Wqkv, L0_conv_bqkv, L0_conv_Wm, L0_conv_bm, L0_conv_rel_table, L0_ffn_W1, L0_ffn_b1, L0_ffn_W2, L0_ffn_b2, L1_conv_w_qkv, L1_conv_w_out, L1_conv_b_out, L1_ffn_gate_w, L1_ffn_gate_b, L1_ffn_w1, L1_ffn_b1, L1_ffn_w2, L1_ffn_b2, L2_conv_w_pw1, L2_conv_star_scale, L2_conv_star_bias, L2_conv_w1, L2_conv_b1, L2_conv_w2, L2_conv_b2, L2_conv_w_pw2, L2_ffn_gate_w, L2_ffn_gate_b, L2_ffn_w1, L2_ffn_b1, L2_ffn_w2, L2_ffn_b2, L3_conv_pwconv1_w, L3_conv_act1_scale, L3_conv_act1_bias, L3_conv_fc1_w, L3_conv_mlp_scale, L3_conv_mlp_bias, L3_conv_fc2_w, L3_conv_complex_weights, L3_conv_pwconv2_w, L3_ffn_gate_w, L3_ffn_gate_b, L3_ffn_w1, L3_ffn_b1, L3_ffn_w2, L3_ffn_b2):
    import jax
    import jax.numpy as jnp

    def _L0_conv_ref(x, Wqkv, bqkv, Wm, bm, rel_table):
        import jax, jax.numpy as jnp
        import numpy as np
        IN_CH = 96
        HEAD_DIM = 32
        MAX_SEQ = 16
        N_HEADS = IN_CH // HEAD_DIM
        PART = int(np.sqrt(MAX_SEQ))
        SCALE = HEAD_DIM ** (-0.5)

        def _relative_position_index():
            h = np.arange(PART)
            coords = np.stack(np.meshgrid(h, h, indexing='ij')).reshape(2, -1)
            rel = coords[:, :, None] - coords[:, None, :]
            rel = rel.transpose(1, 2, 0).astype(np.int64)
            rel[:, :, 0] += PART - 1
            rel[:, :, 1] += PART - 1
            rel[:, :, 0] *= 2 * PART - 1
            return rel.sum(-1).reshape(-1)
        REL_IDX = jnp.asarray(_relative_position_index())
        B, G, P, D = x.shape
        H, DH = (N_HEADS, HEAD_DIM)
        qkv = x @ Wqkv + bqkv
        q, k, v = jnp.split(qkv, 3, axis=-1)
        q = q.reshape(B, G, P, H, DH) * SCALE
        k = k.reshape(B, G, P, H, DH)
        v = v.reshape(B, G, P, H, DH)
        attn = jnp.einsum('bgihd,bgjhd->bghij', q, k)
        bias = rel_table[REL_IDX].reshape(P, P, H).transpose(2, 0, 1)
        attn = jax.nn.softmax(attn + bias[None, None], axis=-1)
        out = jnp.einsum('bghij,bgjhd->bgihd', attn, v)
        out = out.reshape(B, G, P, D)
        return out @ Wm + bm

    def _L0_ffn_ref(x, W1, b1, W2, b2):
        import jax, jax.numpy as jnp
        import numpy as np
        NUM_GROUPS = 5
        EPS = 1e-05
        QB = 128.0

        def _binarize_weights_groupwise(W):
            n_out = W.shape[0]
            gs = n_out // NUM_GROUPS
            Wb = jnp.zeros_like(W)
            for g in range(NUM_GROUPS):
                wg = W[g * gs:(g + 1) * gs]
                z = wg - wg.mean()
                ste = z + jax.lax.stop_gradient(jnp.sign(z) - z)
                Wb = Wb.at[g * gs:(g + 1) * gs].set(ste)
            return Wb

        def _quantize_activations_groupwise(x):
            n = x.shape[0]
            gs = n // NUM_GROUPS
            xq = jnp.zeros_like(x)
            for g in range(NUM_GROUPS):
                ag = x[g * gs:(g + 1) * gs]
                gamma = jnp.max(jnp.abs(ag))
                xq = xq.at[g * gs:(g + 1) * gs].set(jnp.clip(ag * QB / (gamma + EPS), -QB + EPS, QB - EPS))
            return xq

        def _bitlinear(x, W, b):
            Wb = _binarize_weights_groupwise(W)
            y = jnp.einsum('btc,oc->bto', x, Wb) + b
            return _quantize_activations_groupwise(y)
        h = _bitlinear(x, W1, b1)
        h = jax.nn.gelu(h, approximate=False)
        out = _bitlinear(h, W2, b2)
        return out

    def _L1_conv_ref(x, w_qkv, w_out, b_out):
        import jax, jax.numpy as jnp
        import numpy as np
        DIM = 96
        DIM_HEAD = 32
        HEADS = DIM // DIM_HEAD
        INNER = HEADS * DIM_HEAD
        WSZ = 8
        WSZ2 = 8
        SCALE = DIM_HEAD ** (-0.5)
        B, H, W, D = x.shape
        nh, nw = (H // WSZ, W // WSZ2)
        S = WSZ * WSZ2
        xw = x.reshape(B, nh, WSZ, nw, WSZ2, D).transpose(0, 1, 3, 2, 4, 5).reshape(B * nh * nw, S, D)
        qkv = xw @ w_qkv
        q, k, v = jnp.split(qkv, 3, axis=-1)

        def split_heads(t):
            N = t.shape[0]
            return t.reshape(N, S, HEADS, DIM_HEAD).transpose(0, 2, 1, 3)
        q, k, v = map(split_heads, (q, k, v))
        sim = jnp.einsum('nhid,nhjd->nhij', q * SCALE, k)
        attn = jax.nn.softmax(sim, axis=-1)
        out = jnp.einsum('nhij,nhjd->nhid', attn, v)
        out = out.transpose(0, 2, 1, 3).reshape(-1, S, INNER)
        out = out @ w_out + b_out
        out = out.reshape(B, nh, nw, WSZ, WSZ2, D).transpose(0, 1, 3, 2, 4, 5).reshape(B, H, W, D)
        return out

    def _L1_ffn_ref(x, gate_w, gate_b, w1, b1, w2, b2):
        import jax, jax.numpy as jnp
        import numpy as np
        NUM_EXPERTS = 4
        TOP_K = 2
        DIM = 96
        HID = 4 * DIM
        scores = jnp.einsum('bsd,de->bse', x, gate_w) + gate_b
        probs = jax.nn.softmax(scores, axis=-1)
        topk_vals, topk_idx = jax.lax.top_k(probs, TOP_K)
        mask = jnp.sum(jax.nn.one_hot(topk_idx, NUM_EXPERTS, dtype=probs.dtype), axis=-2)
        masked = probs * mask
        masked = masked / (jnp.sum(masked, axis=-1, keepdims=True) + 1e-09)
        h = jax.nn.gelu(jnp.einsum('bsd,edh->ebsh', x, w1) + b1[:, None, None, :], approximate=False)
        y = jnp.einsum('ebsh,ehd->ebsd', h, w2) + b2[:, None, None, :]
        out = jnp.einsum('bse,ebsd->bsd', masked, y)
        return out

    def _L2_conv_ref(x, w_pw1, star_scale, star_bias, w1, b1, w2, b2, w_pw2):
        import jax, jax.numpy as jnp
        import numpy as np
        NUM_BLOCKS = 8
        LAMBDA = 0.01

        def softshrink(x, lam):
            return jnp.sign(x) * jnp.maximum(jnp.abs(x) - lam, 0.0)
        h = jnp.einsum('bhwc,cm->bhwm', x, w_pw1)
        h = star_scale * jnp.maximum(h, 0.0) ** 2 + star_bias
        h = h.astype(jnp.float32)
        skip = h
        B, H, W, C = h.shape
        nb = NUM_BLOCKS
        bs = C // nb
        Wf = W // 2 + 1
        xf = jnp.fft.rfft2(h, axes=(1, 2), norm='ortho')
        xf = xf.reshape(B, H, Wf, nb, bs)
        xr, xi = (jnp.real(xf), jnp.imag(xf))
        ein = lambda t, w: jnp.einsum('bhwki,kio->bhwko', t, w)
        o1r = jax.nn.relu(ein(xr, w1[0]) - ein(xi, w1[1]) + b1[0])
        o1i = jax.nn.relu(ein(xi, w1[0]) + ein(xr, w1[1]) + b1[1])
        o2r = ein(o1r, w2[0]) - ein(o1i, w2[1]) + b2[0]
        o2i = ein(o1i, w2[0]) + ein(o1r, w2[1]) + b2[1]
        o2r = softshrink(o2r, LAMBDA)
        o2i = softshrink(o2i, LAMBDA)
        xc = (o2r + 1j * o2i).reshape(B, H, Wf, C)
        out = jnp.fft.irfft2(xc, s=(H, W), axes=(1, 2), norm='ortho')
        out = out + skip
        out = jnp.einsum('bhwm,mc->bhwc', out, w_pw2)
        return out

    def _L2_ffn_ref(x, gate_w, gate_b, w1, b1, w2, b2):
        import jax, jax.numpy as jnp
        import numpy as np
        NUM_EXPERTS = 4
        TOP_K = 2
        DIM = 96
        HID = 4 * DIM
        scores = jnp.einsum('bsd,de->bse', x, gate_w) + gate_b
        probs = jax.nn.softmax(scores, axis=-1)
        topk_vals, topk_idx = jax.lax.top_k(probs, TOP_K)
        mask = jnp.sum(jax.nn.one_hot(topk_idx, NUM_EXPERTS, dtype=probs.dtype), axis=-2)
        masked = probs * mask
        masked = masked / (jnp.sum(masked, axis=-1, keepdims=True) + 1e-09)
        h = jax.nn.gelu(jnp.einsum('bsd,edh->ebsh', x, w1) + b1[:, None, None, :], approximate=False)
        y = jnp.einsum('ebsh,ehd->ebsd', h, w2) + b2[:, None, None, :]
        out = jnp.einsum('bse,ebsd->bsd', masked, y)
        return out

    def _L3_conv_ref(x, pwconv1_w, act1_scale, act1_bias, fc1_w, mlp_scale, mlp_bias, fc2_w, complex_weights, pwconv2_w):
        import jax, jax.numpy as jnp
        import numpy as np
        A = -0.75

        def _cubic(t):
            at = jnp.abs(t)
            w1 = ((A + 2.0) * at - (A + 3.0)) * at * at + 1.0
            w2 = A * (((at - 5.0) * at + 8.0) * at - 4.0)
            return jnp.where(at <= 1.0, w1, jnp.where(at < 2.0, w2, 0.0))

        def _resize_axis(x, new, axis):
            old = x.shape[axis]
            pos = jnp.arange(new, dtype=jnp.float32) * ((old - 1) / (new - 1))
            i0 = jnp.floor(pos).astype(jnp.int32)
            frac = pos - i0.astype(jnp.float32)
            offs = jnp.array([-1, 0, 1, 2], dtype=jnp.int32)
            idx = jnp.clip(i0[None, :] + offs[:, None], 0, old - 1)
            w = _cubic(frac[None, :] - offs[:, None].astype(jnp.float32))
            g = jnp.take(x, idx, axis=axis)
            wshape = [1] * g.ndim
            wshape[axis] = 4
            wshape[axis + 1] = new
            return jnp.sum(g * w.reshape(wshape), axis=axis)

        def _bicubic_ac(x, new_h, new_w):
            return _resize_axis(_resize_axis(x, new_h, 0), new_w, 1)
        B, H, W, C = x.shape
        nf = complex_weights.shape[2]
        med = pwconv1_w.shape[1]
        pooled = x.mean(axis=(1, 2))
        h = pooled @ fc1_w
        h = mlp_scale * jnp.square(jax.nn.relu(h)) + mlp_bias
        routeing = jax.nn.softmax((h @ fc2_w).reshape(B, nf, med), axis=1)
        xp = x @ pwconv1_w
        xp = act1_scale * jnp.square(jax.nn.relu(xp)) + act1_bias
        xf = jnp.fft.rfft2(xp.astype(jnp.float32), axes=(1, 2), norm='ortho')
        Wf = xf.shape[2]
        cw = complex_weights.reshape(complex_weights.shape[0], complex_weights.shape[1], -1)
        cw = _bicubic_ac(cw, H, Wf).reshape(H, Wf, nf, 2)
        wc = jax.lax.complex(cw[..., 0], cw[..., 1])
        weight = jnp.einsum('bfc,hwf->bhwc', routeing.astype(jnp.complex64), wc)
        xo = jnp.fft.irfft2(xf * weight, s=(H, W), axes=(1, 2), norm='ortho')
        return xo @ pwconv2_w

    def _L3_ffn_ref(x, gate_w, gate_b, w1, b1, w2, b2):
        import jax, jax.numpy as jnp
        import numpy as np
        NUM_EXPERTS = 4
        TOP_K = 2
        DIM = 96
        HID = 4 * DIM
        scores = jnp.einsum('bsd,de->bse', x, gate_w) + gate_b
        probs = jax.nn.softmax(scores, axis=-1)
        topk_vals, topk_idx = jax.lax.top_k(probs, TOP_K)
        mask = jnp.sum(jax.nn.one_hot(topk_idx, NUM_EXPERTS, dtype=probs.dtype), axis=-2)
        masked = probs * mask
        masked = masked / (jnp.sum(masked, axis=-1, keepdims=True) + 1e-09)
        h = jax.nn.gelu(jnp.einsum('bsd,edh->ebsh', x, w1) + b1[:, None, None, :], approximate=False)
        y = jnp.einsum('ebsh,ehd->ebsd', h, w2) + b2[:, None, None, :]
        out = jnp.einsum('bse,ebsd->bsd', masked, y)
        return out

    def _gn(v, G=32, eps=1e-05):
        B_, H_, W_, C_ = v.shape
        g = v.reshape(B_, H_, W_, G, C_ // G)
        m = jnp.mean(g, axis=(1, 2, 4), keepdims=True)
        s = jnp.var(g, axis=(1, 2, 4), keepdims=True)
        return ((g - m) / jnp.sqrt(s + eps)).reshape(v.shape)

    def _ln_c(v, eps=1e-06):
        m = jnp.mean(v, axis=-1, keepdims=True)
        s = jnp.var(v, axis=-1, keepdims=True)
        return (v - m) / jnp.sqrt(s + eps)

    def _ln_t(v, eps=1e-05):
        m = jnp.mean(v, axis=-1, keepdims=True)
        s = jnp.var(v, axis=-1, keepdims=True)
        return (v - m) / jnp.sqrt(s + eps)

    def _to_tokens(v):
        B_, H_, W_, C_ = v.shape
        return v.reshape(B_, H_ * W_, C_)

    def _from_tokens(t, like):
        return t.reshape(like.shape)
    x = x + _L0_conv_ref(_ln_c(x), L0_conv_Wqkv, L0_conv_bqkv, L0_conv_Wm, L0_conv_bm, L0_conv_rel_table)
    t = _to_tokens(x)
    t = t + _L0_ffn_ref(_ln_t(t), L0_ffn_W1, L0_ffn_b1, L0_ffn_W2, L0_ffn_b2)
    x = _from_tokens(t, x)
    x = x + _L1_conv_ref(_ln_c(x), L1_conv_w_qkv, L1_conv_w_out, L1_conv_b_out)
    t = _to_tokens(x)
    t = t + _L1_ffn_ref(_ln_t(t), L1_ffn_gate_w, L1_ffn_gate_b, L1_ffn_w1, L1_ffn_b1, L1_ffn_w2, L1_ffn_b2)
    x = _from_tokens(t, x)
    x = x + _L2_conv_ref(_ln_c(x), L2_conv_w_pw1, L2_conv_star_scale, L2_conv_star_bias, L2_conv_w1, L2_conv_b1, L2_conv_w2, L2_conv_b2, L2_conv_w_pw2)
    t = _to_tokens(x)
    t = t + _L2_ffn_ref(_ln_t(t), L2_ffn_gate_w, L2_ffn_gate_b, L2_ffn_w1, L2_ffn_b1, L2_ffn_w2, L2_ffn_b2)
    x = _from_tokens(t, x)
    x = x + _L3_conv_ref(_ln_c(x), L3_conv_pwconv1_w, L3_conv_act1_scale, L3_conv_act1_bias, L3_conv_fc1_w, L3_conv_mlp_scale, L3_conv_mlp_bias, L3_conv_fc2_w, L3_conv_complex_weights, L3_conv_pwconv2_w)
    t = _to_tokens(x)
    t = t + _L3_ffn_ref(_ln_t(t), L3_ffn_gate_w, L3_ffn_gate_b, L3_ffn_w1, L3_ffn_b1, L3_ffn_w2, L3_ffn_b2)
    x = _from_tokens(t, x)
    return x

_drawn_inputs = setup_inputs


def setup_inputs(seed=0):
    import zlib

    import numpy as np

    out = dict(_drawn_inputs(seed))
    spreads = {'L0_conv_bqkv': (0.0, 0.1),
     'L0_conv_bm': (0.0, 0.1),
     'L1_ffn_gate_b': (0.0, 0.8),
     'L1_ffn_b1': (0.0, 0.8),
     'L1_ffn_b2': (0.0, 0.8),
     'L2_ffn_gate_b': (0.0, 0.8),
     'L2_ffn_b1': (0.0, 0.8),
     'L2_ffn_b2': (0.0, 0.8),
     'L3_ffn_gate_b': (0.0, 2.0),
     'L3_ffn_b1': (0.0, 2.0),
     'L3_ffn_b2': (0.0, 2.0)}
    factors = {'L0_conv_rel_table': 8.0,
     'L0_ffn_b1': 8.0,
     'L0_ffn_b2': 64.0,
     'L1_conv_b_out': 8.0,
     'L1_ffn_gate_w': 3.188,
     'L1_ffn_w1': 3.385,
     'L1_ffn_w2': 2.919,
     'L2_conv_w_pw1': 8.0,
     'L2_conv_w1': 8.0,
     'L2_conv_b1': 24.033,
     'L2_conv_w2': 8.0,
     'L2_conv_b2': 23.549,
     'L2_conv_w_pw2': 8.0,
     'L2_ffn_gate_w': 3.289,
     'L2_ffn_w1': 3.469,
     'L2_ffn_w2': 2.99,
     'L3_conv_pwconv1_w': 8.0,
     'L3_conv_fc1_w': 8.0,
     'L3_conv_fc2_w': 8.0,
     'L3_conv_complex_weights': 8.0,
     'L3_conv_pwconv2_w': 8.0,
     'L3_ffn_gate_w': 3.342,
     'L3_ffn_w1': 3.54,
     'L3_ffn_w2': 3.034}
    for name, (base, spread) in spreads.items():
        noise = np.random.default_rng([zlib.crc32(name.encode()), seed]).standard_normal(out[name].shape)
        drawn = base * np.exp(spread * noise) if base else spread * noise
        out[name] = jnp.asarray(drawn.astype(out[name].dtype))
    for name, factor in factors.items():
        out[name] = (out[name] * factor).astype(out[name].dtype)
    return out
```

```python
import numpy as np

import concourse.bass as bass
from concourse import mybir
from contextlib import ExitStack

F32 = mybir.dt.float32
F32R = mybir.dt.float32r
BF16 = mybir.dt.bfloat16
ALU = mybir.AluOpType
ACT = mybir.ActivationFunctionType
AX = mybir.AxisListType

P = 128
IMGS, HW, C = 16, 16, 96
TOK = IMGS * HW * HW
TILES = TOK // P
GT = 4
GROUPS = TILES // GT
GTOK = GT * P
HEADS, DH = 3, 32
QSCALE = DH ** -0.5
HID, EXP = 384, 4
CH = HID // P
CK = EXP * CH
MED = 192
WF = HW // 2 + 1
FR = HW * WF
NF = 4
BIG = 1e30
LAMBDA = 0.01
QB, QEPS = 128.0, 1e-5
QCLIP = float(np.float32(QB - QEPS))
FT = 6
FG = 5
EULER = float(np.e)
EPS_C, EPS_T = 1e-6, 1e-5


def ds(start, n):
    return bass.ds(start, n)


def program(nc, a, out, stop=99):
    ctx = ExitStack()
    with ctx:
        def sb(name, shape, dt=F32):
            return ctx.enter_context(nc.sbuf_tensor(name, shape, dt))

        def sem(name):
            return ctx.enter_context(nc.semaphore(name))

        PS = ctx.enter_context(nc.psum_tensor("PS", [P, 8, 512], F32))

        def bank(i, n=512, rows=P):
            return PS[0:rows, i, 0:n]

        TB = bank(7, 512, C)

        X = sb("X", [P, TILES * C])
        ident = sb("ident", [P, P])
        stats = sb("stats", [P, FT, 6])
        msum = sb("msum", [P, FT])
        mdif = sb("mdif", [P, FT])
        m2 = sb("m2", [P, FT])
        mean = sb("mean", [P, FT])
        ve = sb("ve", [P, FT])
        rs = sb("rs", [P, FT])
        half = sb("half", [P, 8])
        quarter = sb("quarter", [P, 8])
        euler = sb("euler", [P, GT * EXP])
        XN = sb("XN", [P, FT, C])
        XH = [sb(f"XH{i}", [C + 1, GTOK], F32R) for i in range(2)]
        XL = [sb(f"XL{i}", [C + 1, GTOK], F32R) for i in range(2)]
        raw = sb("raw", [C + 1, EXP * HID])
        onesf = sb("onesf", [P, P])

        WAh = [sb(f"WAh{i}", [C + 1, 3 * C], F32R) for i in range(2)]
        WAl = [sb(f"WAl{i}", [C + 1, 3 * C], F32R) for i in range(2)]
        WM = [sb(f"WM{i}", [C + 1, C]) for i in range(2)]
        rel = sb("rel", [49, HEADS])
        BI = sb("BI", [P, HEADS, 32])
        bm0 = sb("bm0", [P, 32])
        bm1 = sb("bm1", [P, 32])
        qT = sb("qT", [C, GTOK])
        kT = sb("kT", [C, GTOK])
        V = sb("V", [P, GT, HEADS, DH + 1])
        SC = sb("SC", [P, HEADS, GT, 64])
        mx = sb("mx", [P, HEADS * GT])
        PF = sb("PF", [P, HEADS, GT, P])
        PT = sb("PT", [P, HEADS, GTOK])
        rc = sb("rc", [P, GT, HEADS])
        O = sb("O", [P, GT, C])
        OT = sb("OT", [C + 1, GTOK])

        w1raw = sb("w1raw", [P, CH, C])
        w2raw = sb("w2raw", [C, HID])
        W1B = sb("W1B", [C, HID], F32R)
        w1t = sb("w1t", [C, HID])
        W2B = sb("W2B", [P, CH, C])
        w2t = sb("w2t", [P, CH, C])
        gsum = sb("gsum", [P, 8])
        gmean = sb("gmean", [P, 16])
        sg = sb("sg", [P, HID])
        b1c = sb("b1c", [P, CH])
        b2bc = sb("b2bc", [P, C])
        FH = sb("FH", [C, FT * P], F32R)
        FL = sb("FL", [C, FT * P], F32R)
        am = sb("am", [P, 8])
        am1 = sb("am1", [P, 1])
        gmx = sb("gmx", [1, 1])
        qs = sb("qs", [P, 2])
        Y2 = sb("Y2", [P, FT, C])

        M1h = [sb(f"M1h{i}", [C + 1, EXP * HID], F32R) for i in range(3)]
        M1l = [sb(f"M1l{i}", [C + 1, EXP * HID], F32R) for i in range(3)]
        M2 = [sb(f"M2_{i}", [P, CK, C]) for i in range(3)]
        GWr = [sb(f"GWr{i}", [C + 1, EXP]) for i in range(3)]
        GWh = [sb(f"GWh{i}", [C + 1, EXP], F32R) for i in range(3)]
        GWl = [sb(f"GWl{i}", [C + 1, EXP], F32R) for i in range(3)]
        B2s = [sb(f"B2s{i}", [65, EXP * C], BF16) for i in range(3)]
        onesb = sb("onesb", [65, P], BF16)
        H = [sb(f"H{i}", [P, CK, GTOK]) for i in range(2)]
        tie = sb("tie", [P, 2, EXP, EXP])
        smx = sb("smx", [P, GT])
        dl = sb("dl", [P, GT, EXP])
        ex = sb("ex", [P, GT, EXP])
        cg = sb("cg", [P, GT, EXP, EXP])
        ce = sb("ce", [P, GT, EXP, EXP])
        rk = sb("rk", [P, GT, EXP])
        me = sb("me", [P, GT, EXP])
        s1 = sb("s1", [P, GT])
        s0 = sb("s0", [P, GT])
        G = sb("G", [P, GT, EXP])

        FDFT = sb("FDFT", [P, 2, 2 * FR])
        GDFT = sb("GDFT", [C, 3, HW * HW])
        PWr = [sb(f"PWr{i}", [C, MED]) for i in range(2)]
        PWh = [sb(f"PWh{i}", [C, MED], F32R) for i in range(2)]
        PWl = [sb(f"PWl{i}", [C, MED], F32R) for i in range(2)]
        PO = [sb(f"PO{i}", [C, 2, C]) for i in range(2)]
        SBc = [sb(f"SBc{i}", [P, 2]) for i in range(2)]
        BW = [sb(f"BW{i}", [C, 2, 3, C]) for i in range(2)]
        BB = [sb(f"BB{i}", [C, 2, 2]) for i in range(2)]
        hflat = [H[i][:, :, :].rearrange("p a b -> p (a b)") for i in range(2)]
        R = hflat[0][:, 0:768].rearrange("p (t m) -> p t m", t=GT)
        SQ = hflat[0][:, 768:1536].rearrange("p (t m) -> p t m", t=GT)
        HH = hflat[0][:, 1536:2304].rearrange("p (t m) -> p t m", t=GT)
        XF = hflat[0][0:C, 2304:2304 + 1152].rearrange("p (c r i f) -> p c r i f", c=2, r=2, i=2)
        O1 = hflat[0][0:C, 3456:3456 + 1152].rearrange("p (c r n) -> p c r n", c=2, r=2)
        Z = hflat[0][0:C, 4608:4608 + 1152].rearrange("p (c r n) -> p c r n", c=2, r=2)
        CL = hflat[1][0:C, 0:1152].rearrange("p (c r n) -> p c r n", c=2, r=2)
        ZX = hflat[1][0:C, 1152:2304].rearrange("p (c r n) -> p c r n", c=2, r=2)
        OU = hflat[1][0:C, 2304:2304 + 1152].rearrange("p (c i n) -> p c i n", c=2, i=2)
        PSs = hflat[1][0:C, 3456:3456 + 576].rearrange("p (i n) -> p i n", i=2)
        Y1 = hflat[1][:, 0:CH * FT * P].rearrange("p (c n) -> p c n", c=CH)
        YH = hflat[0][:, 0:CH * FT * P].rearrange("p (c n) -> p c n", c=CH)
        n2 = EXP * C
        B2r = [hflat[1][0:65, i * n2:(i + 1) * n2] for i in range(3)]
        b2b, b2d = (hflat[1][0:65, (3 + i) * n2:(4 + i) * n2] for i in range(2))
        b2a, b2c, b2e = (hflat[1][0:65, (5 + i) * n2:(6 + i) * n2].bitcast(BF16)[:, 0:n2] for i in range(3))
        EH = hflat[0][0:49, 0:16 * P].rearrange("p (j n) -> p j n", j=16)
        cwx = sb("cwx", [112, 2 * NF])
        RB = sb("RB", [112, FR])
        CW = sb("CW", [NF, 3 * FR])
        fc1 = sb("fc1", [C, 24])
        fc2 = sb("fc2", [24, NF * MED])
        msb = sb("msb", [24, 2])
        pl = sb("pl", [C, 2])
        hr = sb("hr", [24, 2])
        hq = sb("hq", [24, 2])
        hh = sb("hh", [24, 2])
        lmx = sb("lmx", [C, 2, 2])
        lg = sb("lg", [C, NF, 2, 2])
        le = sb("le", [C, NF, 2, 2])
        lsum = sb("lsum", [C, 2, 2])
        lrc = sb("lrc", [C, 2, 2])
        RTm = sb("RTm", [C, 2, 2, NF])
        RT = [sb(f"RT{i}", [NF, 4, C]) for i in range(2)]
        MA = hflat[1][0:C, 0:1152].rearrange("p (q r n) -> p q r n", q=4, r=2)
        MB = hflat[1][0:C, 1152:2304].rearrange("p (q r n) -> p q r n", q=4, r=2)

        xin, cst, watt, wffn, wmoe, wfft = (sem(n) for n in ("xin", "cst", "watt", "wffn", "wmoe", "wfft"))
        ms_p, ms_v, split_v = sem("ms_p"), sem("ms_v"), sem("split_v")
        bias_pe, bias_v = sem("bias_pe"), sem("bias_v")
        wt_pe, wt_v, wm_s = sem("wt_pe"), sem("wt_v"), sem("wm_s")
        st_v, ag_p, rs_p, xn_v = (sem(n) for n in ("st_v", "ag_p", "rs_p", "xn_v"))
        tp_pe, hi_a, lo_v, xt_used = (sem(n) for n in ("tp_pe", "hi_a", "lo_v", "xt_used"))
        xu = [sem(f"x_updated{i}") for i in range(8)]
        q_pe, k_pe, q_a, k_a, v_v, s_pe, sc_r, mx_v, sub_v, exp_a = (
            sem(n) for n in ("q_pe", "k_pe", "q_a", "k_a", "v_v", "s_pe", "sc_r", "mx_v", "sub_v", "exp_a"))
        ptp_pe, pt_a, pt_v, pv_pe, rcp_v, nrm_v, ot_pe, ot_a, wo_pe = (
            sem(n) for n in ("ptp_pe", "pt_a", "pt_v", "pv_pe", "rcp_v", "nrm_v", "ot_pe", "ot_a", "wo_pe"))
        ft_pe, fh_a, fl_v, fu_pe, y1_a, ab_v, gt_pe, gm_v, gb_pe, qs_v = (
            sem(n) for n in ("ft_pe", "fh_a", "fl_v", "fu_pe", "y1_a", "ab_v", "gt_pe", "gm_v", "gb_pe", "qs_v"))
        fst_v, fag_p, frs_p, fxn_v = (sem(n) for n in ("fst_v", "fag_p", "frs_p", "fxn_v"))
        cl_v, ge_a, fd_pe, y2_v = (sem(n) for n in ("cl_v", "ge_a", "fd_pe", "y2_v"))
        up_pe, gelu_a, dn_pe, gate_v, gexp_p, comb_v = (
            sem(n) for n in ("up_pe", "gelu_a", "dn_pe", "gate_v", "gexp_p", "comb_v"))
        part_v = sem("part_v")
        h_pe, r_a, sq_a, h_v, dft_pe, xf_a, m1_pe, o1_a, m2_pe, z_a = (
            sem(n) for n in ("h_pe", "r_a", "sq_a", "h_v", "dft_pe", "xf_a", "m1_pe", "o1_a", "m2_pe", "z_a"))
        c_v, zx_p, o_v, pp_pe, ps_a, id_pe = (sem(n) for n in ("c_v", "zx_p", "o_v", "pp_pe", "ps_a", "id_pe"))
        cw_pe, cw_a, w_pe, prod_v, y_p, pool_v, f1_pe, rt_a, rt_v, f2_pe, rt_pe, rt_x, le_a = (
            sem(n) for n in ("cw_pe", "cw_a", "w_pe", "prod_v", "y_p", "pool_v", "f1_pe", "rt_a", "rt_v", "f2_pe",
                             "rt_pe", "rt_x", "le_a"))
        stored, split_m, split_b, ql_v, rt_m = (sem(n) for n in ("stored", "split_m", "split_b", "ql_v", "rt_m"))

        block = ctx.enter_context(nc.Block())

        NGV = 11
        AB = 8
        NWFFT = 3 + 8 + 2 * 20 + 5
        PB, IB = (0, 3), (2, 5)
        WB = (6, 0, 1, 2)

        def xt(g, t):
            return X[:, ds(g * (GT * C) + t * C, C)]

        def xg(g):
            return X[:, ds(g * (GT * C), GT * C)]


        def for_steps(eng, body, pairs=3):
            body(0, 0)
            body(1, 1)
            with eng.Fori(1, pairs) as i:
                body(2 * i, 0)
                body(2 * i + 1, 1)

        @block.sync
        def _(sp):
            with nc.allow_non_contiguous_dma(reason="small weights"):
                n = TILES // 2
                for i in range(2):
                    sp.dma_start(X[:, i * n * C:(i + 1) * n * C].rearrange("p (i c) -> p i c", c=C),
                                 a["x"][i * n * P:(i + 1) * n * P, :].rearrange("(i p) c -> p i c", p=P)).then_inc(xin, 16)
                sp.dma_start(EH, a["k_onehot"]).then_inc(cst, 16)
                sp.dma_start(bm0[:], a["k_bm0"]).then_inc(cst, 16)
                sp.dma_start(bm1[:], a["k_bm1"]).then_inc(cst, 16)
                sp.dma_start(tie[:], a["k_tie"]).then_inc(cst, 16)
                for i, nm in enumerate(("L1_ffn", "L2_ffn", "L3_ffn")):
                    sp.dma_start(M2[i][:], a[nm + "_w2"].rearrange("e (c p) d -> p (e c) d", p=P)).then_inc(wmoe, 16)
                    sp.dma_start(GWr[i][0:C, :], a[nm + "_gate_w"]).then_inc(wmoe, 16)
                    sp.dma_start(GWr[i][C:C + 1, :], a[nm + "_gate_b"].rearrange("(a n) -> a n", a=1)).then_inc(wmoe, 16)
                    sp.dma_start(B2r[i], a[nm + "_b2"].rearrange("e d -> (e d)").partition_broadcast(65)).then_inc(wmoe, 16)
                for i, nm in enumerate(("L1_ffn", "L2_ffn", "L3_ffn") if stop else ()):
                    sp.wait_ge(split_v, 4 if i == 0 else 4 * i + 2)
                    sp.dma_start(raw[0:C, :].rearrange("c (e h) -> c e h", e=EXP),
                                 a[nm + "_w1"].rearrange("e c h -> c e h")).then_inc(wm_s, 16)
                    sp.dma_start(raw[C:C + 1, :], a[nm + "_b1"].rearrange("(a e) h -> a (e h)", a=1)).then_inc(wm_s, 16)
                sp.dma_start(FDFT[:], a["k_dft"]).then_inc(wfft, 16)
                sp.dma_start(GDFT[:], a["k_idft"]).then_inc(wfft, 16)
                sp.dma_start(RB[:], a["k_bicubic"]).then_inc(wfft, 16)
            for g in range(GROUPS):
                sp.wait_ge(xu[min(stop, 7)], FG if stop == 1 else g + 1)
                sp.dma_start(out[g * GTOK:(g + 1) * GTOK, :].rearrange("(i p) c -> p i c", p=P),
                             X[:, g * GT * C:(g + 1) * GT * C].rearrange("p (i c) -> p i c", c=C)).then_inc(stored, 16)
            sp.wait_ge(stored, 16 * GROUPS)

        @block.gpsimd
        def _(pool):
            pool.memset(half[:], -0.5).then_inc(ms_p, 1)
            pool.memset(euler[:], EULER).then_inc(ms_p, 1)
            pool.memset(quarter[:], 0.25).then_inc(ms_p, 1)
            pool.wait_ge(ms_p, 3)

            def row_stats(m, eps, n, have, part, done):
                pool.wait_ge(have, m + 1)
                pool.tensor_tensor(msum[:, 0:n], stats[:, 0:n, 1], stats[:, 0:n, 4], ALU.add)
                pool.tensor_tensor(mdif[:, 0:n], stats[:, 0:n, 1], stats[:, 0:n, 4], ALU.subtract)
                pool.tensor_tensor(m2[:, 0:n], stats[:, 0:n, 2], stats[:, 0:n, 5], ALU.add).then_inc(part, 1)
                pool.wait_ge(part, 4 * m + 1)
                pool.tensor_tensor(mdif[:, 0:n], mdif[:, 0:n], mdif[:, 0:n], ALU.mult)
                pool.tensor_scalar(mean[:, 0:n], msum[:, 0:n], 0.5, None, ALU.mult)
                pool.tensor_scalar(m2[:, 0:n], m2[:, 0:n], 1.0 / C, eps, ALU.mult, ALU.add).then_inc(part, 1)
                pool.wait_ge(part, 4 * m + 2)
                pool.tensor_tensor(ve[:, 0:n], mdif[:, 0:n], quarter[:, 0:n], ALU.mult).then_inc(part, 1)
                pool.wait_ge(part, 4 * m + 3)
                pool.tensor_tensor(ve[:, 0:n], ve[:, 0:n], m2[:, 0:n], ALU.add).then_inc(part, 1)
                pool.wait_ge(part, 4 * m + 4)
                pool.tensor_tensor(rs[:, 0:n], ve[:, 0:n], half[:, 0:n], ALU.pow).then_inc(done, 1)

            def rstd(m, eps):
                row_stats(m, eps, GT, st_v, ag_p, rs_p)

            def gate_exp(b):
                pool.wait_ge(gate_v, NGV * b + 2)
                pool.tensor_tensor(ex[:, :, :].rearrange("p t e -> p (t e)"), euler[:],
                                   dl[:, :, :].rearrange("p t e -> p (t e)"), ALU.pow).then_inc(gexp_p, 1)

            def spectrum_plus(g):
                for j in range(4):
                    c, r = j // 2, j % 2
                    pool.wait_ge(z_a, 4 * g + j + 1)
                    pool.wait_ge(o_v, 4 * g)
                    pool.tensor_tensor(ZX[:, c, r, :], Z[:, c, r, :],
                                       XF[:, c, r, :, :].rearrange("p i f -> p (i f)"), ALU.add).then_inc(zx_p, 1)

            def product_sum(g):
                for j in range(4):
                    pool.wait_ge(prod_v, 3 * (4 * g + j) + 3)
                    pool.wait_ge(pp_pe, 16 + 2 * g)
                    pool.tensor_tensor(OU[:, j // 2, j % 2, :], MA[:, j, :, :].rearrange("p r n -> p (r n)"),
                                       MB[:, j, :, :].rearrange("p r n -> p (r n)"), ALU.add).then_inc(y_p, 1)

            def moe(k, e):
                def step(g, p):
                    gate_exp(8 * e + g)
                    rstd(8 * k + g + 2, EPS_T)
                rstd(8 * k + 1, EPS_T)
                for_steps(pool, step)
                gate_exp(8 * e + 6)
                if e < 2:
                    rstd(8 * k + 8, EPS_C)
                gate_exp(8 * e + 7)

            rstd(0, EPS_C)
            for_steps(pool, lambda g, p: rstd(g + 1, EPS_C))
            rstd(7, EPS_C)
            if stop < 1:
                return
            for q in range(FG):
                row_stats(q, EPS_T, FT, fst_v, fag_p, frs_p)
            if stop < 2:
                return
            rstd(8, EPS_C)
            for_steps(pool, lambda g, p: rstd(8 + g + 1, EPS_C))
            rstd(15, EPS_C)
            rstd(16, EPS_T)
            if stop < 3:
                return
            moe(2, 0)
            if stop < 4:
                return
            for_steps(pool, lambda g, p: (rstd(24 + g + 1, EPS_C), spectrum_plus(g)))
            for g in (6, 7):
                rstd(24 + g + 1, EPS_C if g == 6 else EPS_T)
                spectrum_plus(g)
            if stop < 5:
                return
            moe(4, 1)
            if stop < 6:
                return
            for_steps(pool, lambda g, p: (rstd(40 + g + 1, EPS_C), product_sum(g)))
            for g in (6, 7):
                rstd(40 + g + 1, EPS_C if g == 6 else EPS_T)
                product_sum(g)
            if stop < 7:
                return
            moe(6, 2)

        @block.scalar
        def _(act):
            with nc.allow_non_contiguous_dma(reason="small weights"):
                act.dma_start(ident[:], a["k_ident"]).then_inc(watt, 16)
                for i, (w, b) in enumerate((("L0_conv_Wqkv", "L0_conv_bqkv"), ("L1_conv_w_qkv", None))):
                    act.dma_start(raw[0:C, i * 3 * C:(i + 1) * 3 * C], a[w]).then_inc(watt, 16)
                act.wait_ge(ms_v, 1)
                act.dma_start(raw[C:C + 1, 0:3 * C], a["L0_conv_bqkv"].rearrange("(a n) -> a n", a=1)).then_inc(watt, 16)
                act.dma_start(WM[0][0:C, :], a["L0_conv_Wm"]).then_inc(watt, 16)
                act.dma_start(WM[0][C:C + 1, :], a["L0_conv_bm"].rearrange("(a n) -> a n", a=1)).then_inc(watt, 16)
                act.dma_start(WM[1][0:C, :], a["L1_conv_w_out"]).then_inc(watt, 16)
                act.dma_start(WM[1][C:C + 1, :], a["L1_conv_b_out"].rearrange("(a n) -> a n", a=1)).then_inc(watt, 16)
                act.dma_start(rel[:], a["L0_conv_rel_table"]).then_inc(watt, 16)
                act.dma_start(w1raw[:], a["L0_ffn_W1"].rearrange("(c p) i -> p c i", p=P)).then_inc(wffn, 16)
                act.dma_start(w2raw[:], a["L0_ffn_W2"]).then_inc(wffn, 16)
                act.dma_start(b1c[:], a["L0_ffn_b1"].rearrange("(c p) -> p c", p=P)).then_inc(wffn, 16)
                act.dma_start(b2bc[:], a["L0_ffn_b2"].partition_broadcast(P)).then_inc(wffn, 16)
                act.wait_ge(ms_v, 2)
                for i, (w, nm) in enumerate((("w_pw1", "L2_conv"), ("pwconv1_w", "L3_conv"))):
                    act.dma_start(PWr[i][:], a[f"{nm}_{w}"]).then_inc(wfft, 16)
                    w2 = a["L2_conv_w_pw2" if i == 0 else "L3_conv_pwconv2_w"]
                    act.dma_start(PO[i][:], w2.rearrange("(k p) c -> p k c", p=C)).then_inc(wfft, 16)
                    sc, bi = ("star_scale", "star_bias") if i == 0 else ("act1_scale", "act1_bias")
                    act.dma_start(SBc[i][:, 0:1], a[f"{nm}_{sc}"].partition_broadcast(P)).then_inc(wfft, 16)
                    act.dma_start(SBc[i][:, 1:2], a[f"{nm}_{bi}"].partition_broadcast(P)).then_inc(wfft, 16)
                for i in range(2):
                    w, b = a[f"L2_conv_w{i + 1}"], a[f"L2_conv_b{i + 1}"]
                    for c in range(2):
                        for r in range(2):
                            for k in range(4):
                                act.dma_start(BW[i][24 * k:24 * k + 24, c, r, 24 * k:24 * k + 24],
                                              w[r, 4 * c + k, :, :]).then_inc(wfft, 16)
                            act.dma_start(BB[i][:, c, r:r + 1],
                                          b[r, 4 * c:4 * c + 4, :].rearrange("k (o a) -> (k o) a", a=1)).then_inc(wfft, 16)
                act.dma_start(cwx[:], a["L3_conv_complex_weights"].rearrange("h w f r -> (h w) (f r)")).then_inc(wfft, 16)
                act.dma_start(fc1[:], a["L3_conv_fc1_w"]).then_inc(wfft, 16)
                act.dma_start(fc2[:], a["L3_conv_fc2_w"]).then_inc(wfft, 16)
                act.dma_start(msb[:, 0:1], a["L3_conv_mlp_scale"].partition_broadcast(24)).then_inc(wfft, 16)
                act.dma_start(msb[:, 1:2], a["L3_conv_mlp_bias"].partition_broadcast(24)).then_inc(wfft, 16)

            def prep_hi(m, p):
                act.wait_ge(tp_pe, m + 1)
                if not (isinstance(m, int) and m < 2):
                    act.wait_ge(xt_used, m - 1)
                act.activation(XH[p][0:C, :], TB, ACT.Copy).then_inc(hi_a, 1)

            def attention(ka, g):
                at = 8 * ka + g
                act.wait_ge(q_pe, at + 1)
                act.wait_ge(s_pe, at)
                act.activation(qT[:], bank(0, 512, C), ACT.Copy, scale=QSCALE).then_inc(q_a, 1)
                act.wait_ge(k_pe, at + 1)
                act.activation(kT[:], bank(1, 512, C), ACT.Copy).then_inc(k_a, 1)

            def attention_softmax(ka, g):
                at = 8 * ka + g
                bs = 32 if ka == 0 else 64
                if ka == 1:
                    act.wait_ge(s_pe, at + 1)
                    act.wait_ge(exp_a, at)
                    for q in range(P // bs):
                        rows = slice(q * bs, (q + 1) * bs)
                        S = PS[rows, 3:6, :].rearrange("p h (t j) -> p h t j", t=GT)[:, :, :, rows]
                        ins = act.activation(SC[rows, :, :, 0:bs], S, ACT.Copy)
                    ins.then_inc(sc_r, 1)
                act.wait_ge(sub_v, at + 1)
                act.wait_ge(ptp_pe, 3 * at)
                for q in range(P // bs):
                    rows = slice(q * bs, (q + 1) * bs)
                    ins = act.activation(PF[rows, :, :, rows], SC[rows, :, :, 0:bs], ACT.Exp)
                ins.then_inc(exp_a, 1)

            def attention_out(ka, g):
                at = 8 * ka + g
                act.wait_ge(pv_pe, at)
                for h in range(2):
                    act.wait_ge(ptp_pe, 3 * at + h + 1)
                    act.activation(PT[:, h, :], bank(3 + h), ACT.Copy).then_inc(pt_a, 1)
                act.wait_ge(ot_pe, at + 1)
                act.wait_ge(wo_pe, at)
                act.activation(OT[0:C, :], bank(0, 512, C), ACT.Copy).then_inc(ot_a, 1)

            def attention_step(ka, g, p, prep=True):
                m = 8 * ka + g
                attention(ka, g)
                attention_softmax(ka, g)
                if prep:
                    prep_hi(m + 1, 1 - p)
                attention_out(ka, g)

            prep_hi(0, 0)
            for_steps(act, lambda g, p: attention_step(0, g, p))
            attention_step(0, 6, 0)
            attention_step(0, 7, 1, prep=False)
            if stop < 1:
                return

            for q in range(FG):
                act.wait_ge(ft_pe, q + 1)
                act.wait_ge(fu_pe, 6 * q)
                act.activation(FH[:].rearrange("p (u n) -> p u n", u=2), PS[0:C, 6:8, 0:3 * P], ACT.Copy).then_inc(fh_a, 1)
                for j in range(6):
                    c, u = j // 2, j % 2
                    act.wait_ge(fu_pe, 6 * q + j + 1)
                    act.wait_ge(ge_a, 3 * q)
                    act.activation(Y1[:, c, u * 3 * P:(u + 1) * 3 * P], bank(j, 3 * P), ACT.Identity,
                                   bias=b1c[:, c:c + 1]).then_inc(y1_a, 1)
                for c in range(CH):
                    act.wait_ge(cl_v, 3 * q + c + 1)
                    act.wait_ge(fd_pe, 2 * q)
                    act.activation(YH[:, c, :], Y1[:, c, :], ACT.Gelu).then_inc(ge_a, 1)
            if stop < 2:
                return

            prep_hi(8, 0)
            for_steps(act, lambda g, p: attention_step(1, g, p))
            attention_step(1, 6, 0)
            attention_step(1, 7, 1)
            if stop < 3:
                return

            def gelus(b, p, lo, hi):
                for c in range(lo, hi):
                    act.wait_ge(up_pe, CK * b + c + 1)
                    if not (isinstance(b, int) and b < 2):
                        act.wait_ge(dn_pe, 4 * b - 4)
                    act.activation(H[p][:, c, :], bank(c % 4), ACT.Gelu).then_inc(gelu_a, 1)

            def moe(k, e):
                b = 8 * e
                gelus(b, 0, 0, 6)
                prep_hi(8 * k + 1, 1)
                gelus(b, 0, 6, 12)

                def step(g, p):
                    gelus(b + g + 1, 1 - p, 0, 9)
                    prep_hi(8 * k + g + 2, p)
                    gelus(b + g + 1, 1 - p, 9, 12)
                for_steps(act, step)
                gelus(b + 7, 1, 0, 9)
                if e < 2:
                    prep_hi(8 * k + 8, 0)
                gelus(b + 7, 1, 9, 12)

            def mix_head(kc, g):
                s = 8 * kc + g
                act.wait_ge(h_v, s)
                act.wait_ge(h_pe, s + 1)
                act.activation(R[:, 0:2, :], bank(0, 2 * MED).rearrange("p (t m) -> p t m", t=2), ACT.Relu).then_inc(r_a, 1)
                act.wait_ge(xt_used, (24 if kc == 0 else 40) + g + 1)
                act.activation(R[:, 2:4, :], bank(1, 2 * MED).rearrange("p (t m) -> p t m", t=2), ACT.Relu).then_inc(r_a, 1)
                act.wait_ge(r_a, 2 * s + 2)
                act.activation(SQ, R, ACT.Square).then_inc(sq_a, 1)
                for j in range(4):
                    c, i = j // 2, j % 2
                    act.wait_ge(dft_pe, 4 * s + j + 1)
                    if kc == 0:
                        act.wait_ge(zx_p, 4 * g)
                    else:
                        act.wait_ge(prod_v, 12 * g)
                    act.activation(XF[:, c, :, i, :], bank(2 + j, 2 * FR, C).rearrange("p (r f) -> p r f", r=2),
                                   ACT.Copy).then_inc(xf_a, 1)

            def mix_tail(kc, g):
                s = 8 * kc + g
                for i in range(2):
                    act.wait_ge(pp_pe, 2 * s + i + 1)
                    act.wait_ge(id_pe, s)
                    act.activation(PSs[:, i, :], bank(PB[kc] + i, 3 * C, C), ACT.Copy).then_inc(ps_a, 1)

            def mixer2(g, p):
                mix_head(0, g)
                prep_hi(24 + g + 1, 1 - p)
                for j in range(4):
                    c, r = j // 2, j % 2
                    act.wait_ge(m1_pe, 4 * g + j + 1)
                    act.wait_ge(m2_pe, 4 * g)
                    act.activation(O1[:, c, r, :], bank((6, 0, 1, 2)[j], 2 * FR, C), ACT.Relu,
                                   bias=BB[0][:, c, r:r + 1]).then_inc(o1_a, 1)
                for j in range(4):
                    c, r = j // 2, j % 2
                    act.wait_ge(m2_pe, 4 * g + j + 1)
                    act.wait_ge(o_v, 4 * g)
                    act.activation(Z[:, c, r, :], bank(3 + j, 2 * FR, C), ACT.Identity,
                                   bias=BB[1][:, c, r:r + 1]).then_inc(z_a, 1)
                mix_tail(0, g)

            moe(2, 0)
            if stop < 4:
                return
            for_steps(act, mixer2)
            mixer2(6, 0)
            mixer2(7, 1)
            if stop < 5:
                return
            moe(4, 1)
            if stop < 6:
                return

            def routing_relu(i):
                act.wait_ge(f1_pe, i + 1)
                act.activation(hr[:], TB[0:24, 0:2], ACT.Relu, scale=1.0 / (HW * HW)).then_inc(rt_a, 1)
                act.wait_ge(rt_a, 2 * i + 1)
                act.activation(hq[:], hr[:], ACT.Square).then_inc(rt_a, 1)

            def routing_exp(i):
                act.wait_ge(rt_v, 5 * i + 3)
                act.activation(le[:], lg[:], ACT.Exp).then_inc(le_a, 1)

            for j in range(3):
                act.wait_ge(cw_pe, j + 1)
                act.activation(CW[:, j * FR:(j + 1) * FR], bank(j, FR, NF), ACT.Copy,
                               scale=-1.0 if j == 1 else 1.0).then_inc(cw_a, 1)
            routing_relu(0)
            routing_exp(0)

            def mixer3(g, p, routing=True):
                mix_head(1, g)
                prep_hi(40 + g + 1, 1 - p)
                if routing:
                    routing_relu(g + 1)
                    routing_exp(g + 1)
                mix_tail(1, g)
            for_steps(act, mixer3)
            mixer3(6, 0)
            mixer3(7, 1, routing=False)
            if stop < 7:
                return
            moe(6, 2)

        @block.vector
        def _(dve):
            dve.memset(raw[C:C + 1, 0:2 * 3 * C], 0.0).then_inc(ms_v, 1)
            for i in range(2):
                ins = dve.memset(BW[i][:], 0.0)
            ins.then_inc(ms_v, 1)
            dve.memset(onesf[:], 1.0)
            dve.memset(onesb[:], 1.0)
            for i in range(2):
                dve.memset(XH[i][C:C + 1, :].bitcast(F32), 1.0)
                dve.memset(XL[i][C:C + 1, :].bitcast(F32), 0.0)
            for i in range(3):
                dve.memset(B2s[i][:], 0.0)
            dve.memset(OT[C:C + 1, :], 1.0)
            dve.memset(V[:], 1.0)
            dve.memset(PF[:], 0.0).then_inc(ms_v, 1)
            dve.wait_ge(ms_v, 3)

            def halves(hi, lo, src, count):
                dve.tensor_copy(hi, src).then_inc(split_v, 1)
                dve.wait_ge(split_v, count + 1)
                dve.tensor_tensor(lo, src, hi.bitcast(F32), ALU.subtract).then_inc(split_v, 1)

            def prep_stats(m, g, ready, value):
                dve.wait_ge(ready, value)
                dve.wait_ge(rs_p, m)
                for t in range(GT):
                    ins = dve.bn_stats(stats[:, t, :], xt(g, t))
                ins.then_inc(st_v, 1)

            def prep_norm(m, g):
                dve.wait_ge(rs_p, m + 1)
                if not (isinstance(m, int) and m == 0):
                    dve.wait_ge(tp_pe, m)
                for t in range(GT):
                    ins = dve.tensor_scalar(XN[:, t, :], xt(g, t), mean[:, t:t + 1], rs[:, t:t + 1],
                                            ALU.subtract, ALU.mult)
                ins.then_inc(xn_v, 1)

            def prep_lo(m, p):
                dve.wait_ge(hi_a, m + 1)
                dve.tensor_tensor(XL[p][0:C, :], TB, XH[p][0:C, :].bitcast(F32), ALU.subtract).then_inc(lo_v, 1)

            def attention_step(ka, g, p, prep=None):
                at = 8 * ka + g
                bs = 32 if ka == 0 else 64
                if prep:
                    prep_stats(*prep)
                dve.wait_ge(xt_used, at + 1)
                dve.wait_ge(pv_pe, at)
                dve.tensor_copy(V[:, :, :, 0:DH], bank(2, GT * C).rearrange("p (t h d) -> p t h d", t=GT, h=HEADS))\
                   .then_inc(v_v, 1)
                if prep:
                    prep_norm(prep[0], prep[1])
                if ka == 0:
                    dve.wait_ge(s_pe, at + 1)
                    dve.wait_ge(exp_a, at)
                    for q in range(P // bs):
                        rows = slice(q * bs, (q + 1) * bs)
                        S = PS[rows, 3:6, :].rearrange("p h (t j) -> p h t j", t=GT)[:, :, :, rows]
                        ins = dve.tensor_tensor(SC[rows, :, :, 0:bs], S,
                                                BI[rows, :, :].unsqueeze(2).to_broadcast([bs, HEADS, GT, bs]), ALU.add)
                    ins.then_inc(sc_r, 1)
                scv = SC[:, :, :, 0:bs].rearrange("p h t j -> p (h t) j")
                dve.wait_ge(sc_r, at + 1)
                dve.tensor_reduce(mx[:], scv, AX.X, ALU.max).then_inc(mx_v, 1)
                dve.wait_ge(mx_v, at + 1)
                dve.tensor_tensor(scv, scv, mx[:].unsqueeze(2).to_broadcast([P, HEADS * GT, bs]), ALU.subtract)\
                   .then_inc(sub_v, 1)
                if prep:
                    prep_lo(prep[0], 1 - p)
                dve.wait_ge(ptp_pe, 3 * at + 3)
                dve.wait_ge(pv_pe, at)
                dve.tensor_copy(PT[:, 2, :], bank(5)).then_inc(pt_v, 1)
                dve.wait_ge(pv_pe, at + 1)
                o = bank(6, GT * HEADS * (DH + 1)).rearrange("p (t h d) -> p t h d", t=GT, h=HEADS)
                dve.reciprocal(rc[:], o[:, :, :, DH]).then_inc(rcp_v, 1)
                dve.wait_ge(rcp_v, at + 1)
                dve.wait_ge(ot_pe, at)
                dve.tensor_tensor(O[:].rearrange("p t (h d) -> p t h d", h=HEADS), o[:, :, :, 0:DH],
                                  rc[:].unsqueeze(3).to_broadcast([P, GT, HEADS, DH]), ALU.mult).then_inc(nrm_v, 1)
                dve.wait_ge(wo_pe, at + 1)
                dve.tensor_tensor(xg(g), xg(g), bank(1, GT * C), ALU.add).then_inc(xu[0 if ka == 0 else 2], 1)

            dve.wait_ge(watt, 16 * 9)
            for i in range(2):
                halves(WAh[i][:], WAl[i][:], raw[:, i * 3 * C:(i + 1) * 3 * C], 2 * i)
            dve.wait_ge(cst, 16 * 4)
            dve.wait_ge(bias_pe, 1)
            bp = bank(0, 16 * HEADS).rearrange("p (j h) -> p h j", h=HEADS)
            for k in range(2):
                cols = slice(16 * k, 16 * k + 16)
                ins = dve.tensor_tensor(BI[:, :, cols], bp, bm0[:, cols].unsqueeze(1).to_broadcast([P, HEADS, 16]), ALU.mult)
            ins.then_inc(bias_v, 1)
            dve.wait_ge(bias_v, 1)
            dve.tensor_tensor(BI[:], BI[:], bm1[:].unsqueeze(1).to_broadcast([P, HEADS, 32]), ALU.add).then_inc(bias_v, 1)
            dve.wait_ge(bias_v, 2)

            prep_stats(0, 0, xin, 32)
            prep_norm(0, 0)
            prep_lo(0, 0)
            for_steps(dve, lambda g, p: attention_step(0, g, p, (g + 1, g + 1, xin, 32)))
            attention_step(0, 6, 0, (7, 7, xin, 32))
            attention_step(0, 7, 1)
            if stop < 1:
                return

            gs1, gs2 = HID // FG, C // FG
            dve.wait_ge(wt_pe, 1)
            dve.tensor_copy(w1t[:], bank(0, HID, C)).then_inc(wt_v, 1)
            dve.wait_ge(wt_pe, 2)
            dve.tensor_copy(w2t[:], bank(1, CH * C).rearrange("p (c o) -> p c o", c=CH)).then_inc(wt_v, 1)
            dve.memset(gsum[:], 0.0).then_inc(wt_v, 1)
            dve.wait_ge(wt_v, 3)
            dve.tensor_reduce(gsum[0:C, 0:FG], w1t[:, 0:FG * gs1].rearrange("p (g n) -> p g n", g=FG), AX.X, ALU.add)\
               .then_inc(wt_v, 1)
            dve.wait_ge(wt_pe, 3)
            dve.tensor_scalar(gmean[:, 0:FG], bank(2, FG), 1.0 / (gs1 * C), None, ALU.mult).then_inc(wt_v, 1)
            dve.wait_ge(wt_v, 5)
            dve.tensor_reduce(gsum[:, 0:FG], w2t[:, :, 0:FG * gs2].rearrange("p c (g n) -> p g c n", g=FG), AX.XY, ALU.add)\
               .then_inc(wt_v, 1)
            dve.wait_ge(wt_pe, 4)
            dve.tensor_scalar(gmean[:, 8:8 + FG], bank(3, FG), 1.0 / (gs2 * HID), None, ALU.mult).then_inc(wt_v, 1)
            dve.memset(W1B[:].bitcast(F32), 0.0)
            dve.memset(W2B[:], 0.0).then_inc(wt_v, 1)
            dve.wait_ge(wt_v, 8)
            for g in range(FG):
                cols = slice(g * gs1, (g + 1) * gs1)
                ins = dve.tensor_scalar(sg[0:C, cols], w1t[:, cols], gmean[0:C, g:g + 1], None, ALU.is_lt)
            ins.then_inc(wt_v, 1)
            dve.wait_ge(wt_v, 9)
            for g in range(FG):
                cols = slice(g * gs1, (g + 1) * gs1)
                ins = dve.scalar_tensor_tensor(W1B[:, cols], w1t[:, cols], gmean[0:C, g:g + 1], sg[0:C, cols],
                                               ALU.is_gt, ALU.subtract)
            ins.then_inc(wt_v, 1)
            dve.wait_ge(wt_v, 10)
            s2 = sg[:, 0:CH * C].rearrange("p (c o) -> p c o", c=CH)
            for g in range(FG):
                cols = slice(g * gs2, (g + 1) * gs2)
                ins = dve.tensor_scalar(s2[:, :, cols], w2t[:, :, cols], gmean[:, 8 + g:9 + g], None, ALU.is_lt)
            ins.then_inc(wt_v, 1)
            dve.wait_ge(wt_v, 11)
            for g in range(FG):
                cols = slice(g * gs2, (g + 1) * gs2)
                ins = dve.scalar_tensor_tensor(W2B[:, :, cols], w2t[:, :, cols], gmean[:, 8 + g:9 + g], s2[:, :, cols],
                                               ALU.is_gt, ALU.subtract)
            ins.then_inc(wt_v, 1)

            dve.wait_ge(wmoe, 16 * 12)
            for i in range(3):
                dve.wait_ge(wm_s, 32 * (i + 1))
                halves(M1h[i][:], M1l[i][:], raw[:], 4 + 4 * i)
                halves(GWh[i][:], GWl[i][:], GWr[i][:], 6 + 4 * i)
                dve.tensor_copy(b2a, B2r[i]).then_inc(split_m, 1)
                dve.wait_ge(split_b, 4 * i)
                dve.wait_ge(split_m, i + 1)
                dve.tensor_tensor(b2b, B2r[i], b2a, ALU.subtract).then_inc(split_b, 1)
                dve.wait_ge(split_b, 4 * i + 1)
                dve.tensor_copy(b2c, b2b).then_inc(split_b, 1)
                dve.wait_ge(split_b, 4 * i + 2)
                dve.tensor_tensor(b2d, b2b, b2c, ALU.subtract).then_inc(split_b, 1)
                dve.tensor_copy(B2s[i][0:1, :], b2a[0:1, :])
                dve.tensor_copy(B2s[i][32:33, :], b2c[32:33, :])
                dve.wait_ge(split_b, 4 * i + 3)
                dve.tensor_copy(B2s[i][64:65, :], b2d[64:65, :]).then_inc(split_b, 1)
            dve.wait_ge(wfft, 16 * NWFFT)
            for i in range(2):
                halves(PWh[i][:], PWl[i][:], PWr[i][:], 16 + 3 * i)
                dve.tensor_scalar(BW[i][:, :, 2, :], BW[i][:, :, 1, :], -1.0, None, ALU.mult).then_inc(split_v, 1)

            def absmax_scale(i, n):
                dve.wait_ge(ab_v, AB * (i // 2) + (6 if i % 2 == 0 else 8))
                dve.tensor_reduce(am1[:], am[:, 0:n], AX.X, ALU.max).then_inc(gm_v, 1)
                dve.wait_ge(gt_pe, i + 1)
                dve.tensor_reduce(gmx[:], PS[0:1, 6, 0:P], AX.X, ALU.max).then_inc(gm_v, 1)
                dve.wait_ge(gb_pe, i + 1)
                dve.tensor_scalar(qs[:, 0:1], bank(6, 1), QEPS, None, ALU.add).then_inc(qs_v, 1)
                dve.wait_ge(qs_v, 3 * i + 1)
                dve.reciprocal(qs[:, 1:2], qs[:, 0:1]).then_inc(qs_v, 1)
                dve.wait_ge(qs_v, 3 * i + 2)
                dve.tensor_scalar(qs[:, 0:1], qs[:, 1:2], QB, None, ALU.mult).then_inc(qs_v, 1)
                dve.wait_ge(qs_v, 3 * i + 3)

            dve.wait_ge(xu[0], GROUPS)
            for q in range(FG):
                X6 = X[:, q * FT * C:(q + 1) * FT * C].rearrange("p (t c) -> p t c", t=FT)
                for t in range(FT):
                    ins = dve.bn_stats(stats[:, t, :], X6[:, t, :])
                ins.then_inc(fst_v, 1)
                dve.wait_ge(frs_p, q + 1)
                dve.wait_ge(ft_pe, q)
                for t in range(FT):
                    ins = dve.tensor_scalar(XN[:, t, :], X6[:, t, :], mean[:, t:t + 1], rs[:, t:t + 1],
                                            ALU.subtract, ALU.mult)
                ins.then_inc(fxn_v, 1)
                dve.wait_ge(fh_a, q + 1)
                dve.tensor_tensor(FL[:].rearrange("p (u n) -> p u n", u=2), PS[0:C, 6:8, 0:3 * P],
                                  FH[:].bitcast(F32).rearrange("p (u n) -> p u n", u=2), ALU.subtract).then_inc(fl_v, 1)
                for j in range(6):
                    dve.wait_ge(y1_a, 6 * q + j + 1)
                    dve.tensor_reduce(am[:, j:j + 1], Y1[:, j // 2, (j % 2) * 3 * P:(j % 2 + 1) * 3 * P], AX.X, ALU.max,
                                      apply_absolute_value=True).then_inc(ab_v, 1)
                absmax_scale(2 * q, 6)
                for c in range(CH):
                    dve.tensor_scalar(Y1[:, c, :], Y1[:, c, :], qs[:, 0:1], QCLIP, ALU.mult, ALU.min).then_inc(ql_v, 1)
                for c in range(CH):
                    dve.wait_ge(ql_v, 3 * q + c + 1)
                    dve.tensor_scalar(Y1[:, c, :], Y1[:, c, :], -QCLIP, None, ALU.max).then_inc(cl_v, 1)
                for u in range(2):
                    dve.wait_ge(fd_pe, 2 * q + u + 1)
                    dve.tensor_tensor(Y2[:, 3 * u:3 * u + 3, :], bank(u, 3 * C).rearrange("p (t c) -> p t c", t=3),
                                      b2bc[:].unsqueeze(1).to_broadcast([P, 3, C]), ALU.add).then_inc(y2_v, 1)
                for u in range(2):
                    dve.wait_ge(y2_v, 3 * q + u + 1)
                    dve.tensor_reduce(am[:, u:u + 1], Y2[:, 3 * u:3 * u + 3, :], AX.XY, ALU.max,
                                      apply_absolute_value=True).then_inc(ab_v, 1)
                absmax_scale(2 * q + 1, 2)
                dve.tensor_scalar(Y2[:], Y2[:], qs[:, 0:1], QCLIP, ALU.mult, ALU.min).then_inc(y2_v, 1)
                dve.wait_ge(y2_v, 3 * q + 3)
                dve.scalar_tensor_tensor(X6, Y2[:], -QCLIP, X6, ALU.max, ALU.add).then_inc(xu[1], 1)
            if stop < 2:
                return

            prep_stats(8, 0, xu[1], FG)
            prep_norm(8, 0)
            prep_lo(8, 0)
            for_steps(dve, lambda g, p: attention_step(1, g, p, (8 + g + 1, g + 1, xu[1], FG)))
            attention_step(1, 6, 0, (15, 7, xu[1], FG))
            attention_step(1, 7, 1, (16, 0, xu[2], 1))
            if stop < 3:
                return

            def gating_head(k, b, m):
                sc = bank(6, GT * EXP).rearrange("p (t e) -> p t e", t=GT)
                dve.wait_ge(xt_used, m + 1)
                dve.tensor_reduce(smx[:], sc, AX.X, ALU.max).then_inc(gate_v, 1)
                dve.wait_ge(gate_v, NGV * b + 1)
                dve.tensor_tensor(dl[:], sc, smx[:].unsqueeze(2).to_broadcast([P, GT, EXP]), ALU.subtract).then_inc(gate_v, 1)

            def gating_tail(b):
                exr = ex[:].unsqueeze(3).to_broadcast([P, GT, EXP, EXP])
                exc = ex[:].unsqueeze(2).to_broadcast([P, GT, EXP, EXP])
                dve.wait_ge(gexp_p, b + 1)
                dve.tensor_tensor(cg[:], exc, exr, ALU.is_gt)
                dve.tensor_tensor(ce[:], exc, exr, ALU.is_ge)
                dve.tensor_reduce(s0[:], ex[:], AX.X, ALU.add).then_inc(gate_v, 1)
                dve.wait_ge(gate_v, NGV * b + 3)
                dve.tensor_tensor(cg[:], cg[:], tie[:, 0, :, :].unsqueeze(1).to_broadcast([P, GT, EXP, EXP]), ALU.mult)
                dve.tensor_tensor(ce[:], ce[:], tie[:, 1, :, :].unsqueeze(1).to_broadcast([P, GT, EXP, EXP]), ALU.mult)\
                   .then_inc(gate_v, 1)
                dve.wait_ge(gate_v, NGV * b + 4)
                dve.tensor_tensor(cg[:], cg[:], ce[:], ALU.add).then_inc(gate_v, 1)
                dve.wait_ge(gate_v, NGV * b + 5)
                dve.tensor_reduce(rk[:], cg[:], AX.X, ALU.add).then_inc(gate_v, 1)
                dve.wait_ge(gate_v, NGV * b + 6)
                dve.scalar_tensor_tensor(me[:], rk[:], 2.0, ex[:], ALU.is_lt, ALU.mult).then_inc(gate_v, 1)
                dve.wait_ge(gate_v, NGV * b + 7)
                dve.tensor_reduce(s1[:], me[:], AX.X, ALU.add).then_inc(gate_v, 1)
                dve.wait_ge(gate_v, NGV * b + 8)
                dve.scalar_tensor_tensor(s1[:], s0[:], 1e-9, s1[:], ALU.mult, ALU.add).then_inc(gate_v, 1)
                dve.wait_ge(gate_v, NGV * b + 9)
                dve.reciprocal(s0[:], s1[:]).then_inc(gate_v, 1)
                dve.wait_ge(gate_v, NGV * b + 10)
                dve.tensor_tensor(G[:], me[:], s0[:].unsqueeze(2).to_broadcast([P, GT, EXP]), ALU.mult).then_inc(gate_v, 1)
                dve.wait_ge(gate_v, NGV * b + 11)

            def combine(b, g, t, upd):
                dve.wait_ge(dn_pe, 4 * b + t + 1)
                for e in range(EXP):
                    if e > 0:
                        dve.wait_ge(part_v, 3 * (4 * b + t) + e)
                    ins = dve.scalar_tensor_tensor(xt(g, t), bank(4 + t % 2)[:, e * C:(e + 1) * C], G[:, t, e:e + 1],
                                                   xt(g, t), ALU.mult, ALU.add)
                    if e < EXP - 1:
                        ins.then_inc(part_v, 1)
                ins.then_inc(comb_v if t < GT - 1 else upd, 1)

            def moe(k, e, phase, prev):
                b0, m0 = 8 * e, 8 * k
                prep_stats(m0 + 1, 1, xu[prev], 2)
                prep_norm(m0 + 1, 1)
                prep_lo(m0 + 1, 1)

                def step(g, p, prep):
                    gating_head(k, b0 + g, m0 + g)
                    if prep:
                        prep_stats(*prep)
                    gating_tail(b0 + g)
                    if prep:
                        prep_norm(prep[0], prep[1])
                    for t in range(2):
                        combine(b0 + g, g, t, xu[phase])
                    if prep:
                        prep_lo(prep[0], p)
                    for t in range(2, 4):
                        combine(b0 + g, g, t, xu[phase])
                for_steps(dve, lambda g, p: step(g, p, (m0 + g + 2, g + 2, xu[prev], g + 3)))
                step(6, 0, (m0 + 8, 0, xu[phase], 1) if e < 2 else None)
                step(7, 1, None)

            moe(2, 0, 3, 2)
            if stop < 4:
                return

            def mix_h(kc, g):
                s = 8 * kc + g
                dve.wait_ge(sq_a, s + 1)
                dve.wait_ge(dft_pe, 4 * s)
                dve.tensor_scalar(HH, SQ, SBc[kc][:, 0:1], SBc[kc][:, 1:2], ALU.mult, ALU.add).then_inc(h_v, 1)

            def mix_x(kc, g, upd):
                dve.wait_ge(id_pe, 8 * kc + g + 1)
                dve.tensor_tensor(xg(g), xg(g), bank(IB[kc], GT * C), ALU.add).then_inc(upd, 1)

            def mixer2(g, p, prep):
                prep_stats(*prep)
                mix_h(0, g)
                prep_norm(prep[0], prep[1])
                prep_lo(prep[0], 1 - p)
                for j in range(4):
                    c, r = j // 2, j % 2
                    dve.wait_ge(z_a, 4 * g + j + 1)
                    dve.tensor_scalar(CL[:, c, r, :], Z[:, c, r, :], LAMBDA, -LAMBDA, ALU.min, ALU.max).then_inc(c_v, 1)
                    dve.wait_ge(c_v, 4 * g + j + 1)
                    dve.wait_ge(zx_p, 4 * g + j + 1)
                    dve.wait_ge(pp_pe, 2 * g)
                    dve.tensor_tensor(OU[:, c, :, r * FR:(r + 1) * FR], ZX[:, c, r, :].rearrange("p (i f) -> p i f", i=2),
                                      CL[:, c, r, :].rearrange("p (i f) -> p i f", i=2), ALU.subtract).then_inc(o_v, 1)
                mix_x(0, g, xu[4])
            for_steps(dve, lambda g, p: mixer2(g, p, (24 + g + 1, g + 1, xu[3], g + 2)))
            mixer2(6, 0, (31, 7, xu[3], 8))
            mixer2(7, 1, (32, 0, xu[4], 1))
            if stop < 5:
                return
            moe(4, 1, 5, 4)
            if stop < 6:
                return

            def pooled(i):
                dve.tensor_reduce(pl[:], TB.rearrange("p (i n) -> p i n", i=2), AX.X, ALU.add).then_inc(pool_v, 1)

            def routing(i):
                dve.wait_ge(rt_a, 2 * i + 2)
                dve.tensor_scalar(hh[:], hq[:], msb[:, 0:1], msb[:, 1:2], ALU.mult, ALU.add).then_inc(rt_v, 1)
                dve.wait_ge(f2_pe, i + 1)
                L = TB[:, 16:16 + 4 * NF].rearrange("p (f c i) -> p f c i", f=NF, c=2)
                dve.tensor_reduce(lmx[:], L.rearrange("p f c i -> p c i f"), AX.X, ALU.max).then_inc(rt_v, 1)
                dve.wait_ge(rt_v, 5 * i + 2)
                dve.tensor_tensor(lg[:], L, lmx[:].unsqueeze(1).to_broadcast([C, NF, 2, 2]), ALU.subtract).then_inc(rt_v, 1)
                dve.wait_ge(le_a, i + 1)
                dve.tensor_reduce(lsum[:], le[:].rearrange("p f c i -> p c i f"), AX.X, ALU.add).then_inc(rt_v, 1)
                dve.wait_ge(rt_v, 5 * i + 4)
                dve.reciprocal(lrc[:], lsum[:]).then_inc(rt_v, 1)
                dve.wait_ge(rt_v, 5 * i + 5)
                if not (isinstance(i, int) and i == 0):
                    dve.wait_ge(rt_pe, i)
                dve.tensor_tensor(RTm[:].rearrange("p c i f -> p f c i"), le[:],
                                  lrc[:].unsqueeze(1).to_broadcast([C, NF, 2, 2]), ALU.mult).then_inc(rt_m, 1)

            def routing_out(i, p):
                dve.wait_ge(rt_pe, i + 1)
                dve.wait_ge(w_pe, 4 * (i - 1) if not isinstance(i, int) or i > 0 else 0)
                dve.tensor_copy(RT[p][:].rearrange("p q c -> p (q c)"), TB[0:NF, 128:128 + 4 * C]).then_inc(rt_x, 1)

            dve.wait_ge(lo_v, 41)
            pooled(0)
            routing(0)
            routing_out(0, 0)

            def mixer3(g, p, prep, route=True):
                prep_stats(*prep)
                mix_h(1, g)
                prep_norm(prep[0], prep[1])
                prep_lo(prep[0], 1 - p)
                if route:
                    pooled(g + 1)
                    routing(g + 1)
                for j in range(4):
                    c, i = j // 2, j % 2
                    W = bank(WB[j], 3 * FR, C).rearrange("p (r f) -> p r f", r=3)
                    dve.wait_ge(w_pe, 4 * g + j + 1)
                    dve.wait_ge(xf_a, 32 + 4 * g + j + 1)
                    dve.wait_ge(y_p, 4 * g)
                    dve.tensor_tensor(MA[:, j, :, :], XF[:, c, :, i, :], W[:, 0:1, :].to_broadcast([C, 2, FR]), ALU.mult)\
                       .then_inc(prod_v, 1)
                    dve.tensor_tensor(MB[:, j, 0, :], XF[:, c, 1, i, :], W[:, 1, :], ALU.mult).then_inc(prod_v, 1)
                    dve.tensor_tensor(MB[:, j, 1, :], XF[:, c, 0, i, :], W[:, 2, :], ALU.mult).then_inc(prod_v, 1)
                if route:
                    routing_out(g + 1, 1 - p)
                mix_x(1, g, xu[6])
            for_steps(dve, lambda g, p: mixer3(g, p, (40 + g + 1, g + 1, xu[5], g + 2)))
            mixer3(6, 0, (47, 7, xu[5], 8))
            mixer3(7, 1, (48, 0, xu[6], 1), route=False)
            if stop < 7:
                return
            moe(6, 2, 7, 6)

        @block.tensor
        def _(pe):
            def three(o, wh, wl, xh, xl, flip=False):
                prods = ((wh, xh), (wh, xl), (wl, xh)) if not flip else ((wh, xh), (wl, xh), (wh, xl))
                for n, (w, x) in enumerate(prods):
                    ins = pe.matmul(o, w, x, start=n == 0, stop=n == 2)
                return ins

            def prep_turn(m, windows=False, extra=None):
                pe.wait_ge(xn_v, m + 1)
                if not (isinstance(m, int) and m == 0):
                    pe.wait_ge(lo_v, m)
                if extra:
                    pe.wait_ge(*extra)
                for t in range(GT):
                    o = TB[:, t * P:(t + 1) * P]
                    if windows:
                        o = o.rearrange("p (h r c) -> p r h c", h=2, r=8)
                    ins = pe.transpose(o, XN[:, t, :], ident[:])
                ins.then_inc(tp_pe, 1)

            def attention_step(ka, g, p, prep=False):
                at = 8 * ka + g
                xh, xl = XH[p], XL[p]
                wh, wl = WAh[ka], WAl[ka]
                pe.wait_ge(lo_v, at + 1)
                pe.wait_ge(ot_a, at)
                three(bank(0, 512, C), wh[:, 0:C], wl[:, 0:C], xh[:], xl[:]).then_inc(q_pe, 1)
                pe.wait_ge(xu[0 if ka == 0 else 2], g)
                three(bank(1, 512, C), wh[:, C:2 * C], wl[:, C:2 * C], xh[:], xl[:]).then_inc(k_pe, 1)
                for t in range(GT):
                    ts = slice(t * P, (t + 1) * P)
                    ins = three(PS[:, 2, t * C:(t + 1) * C], xh[:, ts], xl[:, ts], wh[:, 2 * C:], wl[:, 2 * C:])
                ins.then_inc(xt_used, 1)
                pe.wait_ge(q_a, at + 1)
                pe.wait_ge(k_a, at + 1)
                pe.wait_ge(pt_a, 2 * at)
                pe.wait_ge(pt_v, at)
                for t in range(GT):
                    for h in range(HEADS):
                        rows, ts = slice(h * DH, (h + 1) * DH), slice(t * P, (t + 1) * P)
                        ins = pe.matmul(PS[:, 3 + h, ts], qT[rows, ts], kT[rows, ts], start=True, stop=True)
                ins.then_inc(s_pe, 1)
                if prep:
                    prep_turn(at + 1, *prep)
                pe.wait_ge(exp_a, at + 1)
                for h in range(HEADS):
                    for t in range(GT):
                        ins = pe.transpose(PS[:, 3 + h, t * P:(t + 1) * P], PF[:, h, t, :], ident[:])
                    ins.then_inc(ptp_pe, 1)
                pe.wait_ge(v_v, at + 1)
                pe.wait_ge(nrm_v, at)
                pe.wait_ge(pt_a, 2 * at + 2)
                pe.wait_ge(pt_v, at + 1)
                for t in range(GT):
                    for h in range(HEADS):
                        n = (t * HEADS + h) * (DH + 1)
                        ins = pe.matmul(PS[:, 6, n:n + DH + 1], PT[:, h, t * P:(t + 1) * P], V[:, t, h, :],
                                        start=True, stop=True)
                ins.then_inc(pv_pe, 1)
                pe.wait_ge(nrm_v, at + 1)
                for t in range(GT):
                    o = PS[0:C, 0, t * P:(t + 1) * P]
                    i = ident[:]
                    if ka == 1:
                        o = o.rearrange("p (r h c) -> p h r c", h=2, r=8)
                    ins = pe.transpose(o, O[:, t, :], i)
                ins.then_inc(ot_pe, 1)
                pe.wait_ge(ot_a, at + 1)
                for t in range(GT):
                    ins = pe.matmul(PS[:, 1, t * C:(t + 1) * C], OT[:, t * P:(t + 1) * P], WM[ka][:], start=True, stop=True)
                ins.then_inc(wo_pe, 1)

            pe.wait_ge(watt, 16 * 9)
            pe.wait_ge(cst, 16 * 4)
            for j in range(16):
                ins = pe.matmul(PS[:, 0, j * HEADS:(j + 1) * HEADS], EH[:, j, :], rel[:], start=True, stop=True)
            ins.then_inc(bias_pe, 1)
            prep_turn(0)
            pe.wait_ge(split_v, 4)
            pe.wait_ge(bias_v, 2)
            for_steps(pe, lambda g, p: attention_step(0, g, p, (False,)))
            attention_step(0, 6, 0, (False,))
            attention_step(0, 7, 1)
            if stop < 1:
                return

            pe.wait_ge(wffn, 16 * 4)
            pe.wait_ge(xu[0], GROUPS)
            for c in range(CH):
                ins = pe.transpose(PS[0:C, 0, c * P:(c + 1) * P], w1raw[:, c, :], ident[:])
            ins.then_inc(wt_pe, 1)
            for c in range(CH):
                ins = pe.transpose(PS[:, 1, c * C:(c + 1) * C], w2raw[:, c * P:(c + 1) * P], ident[0:C, 0:C])
            ins.then_inc(wt_pe, 1)
            pe.wait_ge(wt_v, 4)
            pe.matmul(PS[:, 2, 0:FG], onesf[0:C, :], gsum[0:C, 0:FG], start=True, stop=True).then_inc(wt_pe, 1)
            pe.wait_ge(wt_v, 6)
            pe.matmul(PS[:, 3, 0:FG], onesf[:], gsum[:, 0:FG], start=True, stop=True).then_inc(wt_pe, 1)
            pe.wait_ge(wt_v, 12)
            pe.wait_ge(split_v, 22)

            def absmax(i):
                pe.wait_ge(gm_v, 2 * i + 1)
                pe.transpose(PS[0:1, 6, 0:P], am1[:], ident[:]).then_inc(gt_pe, 1)
                pe.wait_ge(gm_v, 2 * i + 2)
                pe.matmul(PS[:, 6, 0:1], onesf[0:1, :], gmx[:], start=True, stop=True).then_inc(gb_pe, 1)

            for q in range(FG):
                pe.wait_ge(fxn_v, q + 1)
                for t in range(FT):
                    ins = pe.transpose(PS[0:C, 6 + t // 3, (t % 3) * P:(t % 3 + 1) * P], XN[:, t, :], ident[:])
                ins.then_inc(ft_pe, 1)
                pe.wait_ge(fl_v, q + 1)
                for j in range(6):
                    c, u = j // 2, j % 2
                    if j < 2:
                        pe.wait_ge(y2_v, 3 * q)
                    w, us = W1B[:, c * P:(c + 1) * P], slice(u * 3 * P, (u + 1) * 3 * P)
                    pe.matmul(bank(j, 3 * P), w, FH[:, us], start=True, stop=False)
                    pe.matmul(bank(j, 3 * P), w, FL[:, us], start=False, stop=True).then_inc(fu_pe, 1)
                absmax(2 * q)
                pe.wait_ge(ge_a, 3 * q + 3)
                for u in range(2):
                    for t in range(3 * u, 3 * u + 3):
                        for c in range(CH):
                            ins = pe.matmul(PS[:, u, (t % 3) * C:(t % 3 + 1) * C], YH[:, c, t * P:(t + 1) * P], W2B[:, c, :],
                                            start=c == 0, stop=c == CH - 1)
                    ins.then_inc(fd_pe, 1)
                absmax(2 * q + 1)
            if stop < 2:
                return
            pe.wait_ge(xu[1], FG)
            prep_turn(8, True)
            for_steps(pe, lambda g, p: attention_step(1, g, p, (True,)))
            attention_step(1, 6, 0, (True,))
            attention_step(1, 7, 1, (False,))
            if stop < 3:
                return

            def up(e, b, p, lo, hi):
                for c in range(lo, hi):
                    if not (isinstance(b, int) and CK * b + c < 4):
                        pe.wait_ge(gelu_a, CK * b + c - 3)
                    cs = slice(c * P, (c + 1) * P)
                    three(bank(c % 4), M1h[e][:, cs], M1l[e][:, cs], XH[p][:], XL[p][:]).then_inc(up_pe, 1)

            def gate(e, b, p):
                pe.wait_ge(gate_v, NGV * b - NGV + 2 if not (isinstance(b, int) and b == 0) else 0)
                for t in range(GT):
                    ts = slice(t * P, (t + 1) * P)
                    ins = three(PS[:, 6, t * EXP:(t + 1) * EXP], XH[p][:, ts], XL[p][:, ts], GWh[e][:], GWl[e][:])
                ins.then_inc(xt_used, 1)

            def down(e, b, p, t, upd):
                Y = bank(4 + t % 2, EXP * C)
                if t == 0:
                    pe.wait_ge(gelu_a, CK * b + CK)
                if t == 1:
                    pe.wait_ge(upd, b - 8 * e)
                else:
                    pe.wait_ge(comb_v, 3 * b + t // 2 + t % 2)
                pe.matmul(Y, onesb[:], B2s[e][:], start=True, stop=False)
                for x in range(EXP):
                    for c in range(CH):
                        j = x * CH + c
                        ins = pe.matmul(Y[:, x * C:(x + 1) * C], H[p][:, j, t * P:(t + 1) * P], M2[e][:, j, :],
                                        start=False, stop=j == CK - 1)
                ins.then_inc(dn_pe, 1)

            def moe(k, e, prev):
                b0, m0 = 8 * e, 8 * k
                pe.wait_ge(xu[prev], GROUPS)
                pe.wait_ge(lo_v, m0 + 1)
                up(e, b0, 0, 0, 6)
                prep_turn(m0 + 1)
                up(e, b0, 0, 6, 12)
                gate(e, b0, 0)

                def step(g, p, more, prep):
                    for t in range(GT):
                        if more:
                            if t == 0:
                                pe.wait_ge(lo_v, m0 + g + 2)
                            up(e, b0 + g + 1, 1 - p, 3 * t, 3 * t + 3)
                        down(e, b0 + g, p, t, xu[prev + 1])
                        if t == 1 and prep is not None:
                            prep_turn(prep)
                    if more:
                        gate(e, b0 + g + 1, 1 - p)
                for_steps(pe, lambda g, p: step(g, p, True, m0 + g + 2))
                step(6, 0, True, m0 + 8 if e < 2 else None)
                step(7, 1, False, None)

            moe(2, 0, 2)
            if stop < 4:
                return

            def mix_head(kc, k, g, p):
                s, m = 8 * kc + g, 8 * k + g
                pe.wait_ge(lo_v, m + 1)
                pe.wait_ge(ps_a, 2 * s)
                for t in range(GT):
                    ts = slice(t * P, (t + 1) * P)
                    ins = three(PS[:, t // 2, (t % 2) * MED:(t % 2 + 1) * MED], XH[p][0:C, ts], XL[p][0:C, ts],
                                PWh[kc][:], PWl[kc][:])
                    if t == 1:
                        ins.then_inc(h_pe, 1)
                ins.then_inc(xt_used, 1)
                pe.wait_ge(h_v, s + 1)
                for j in range(4):
                    c, i = j // 2, j % 2
                    if j == 0:
                        pe.wait_ge(xu[4 if kc == 0 else 6], g)
                    for kk in range(2):
                        ins = pe.matmul(bank(2 + j, 2 * FR, C), HH[:, 2 * i + kk, c * C:(c + 1) * C], FDFT[:, kk, :],
                                        start=kk == 0, stop=kk == 1)
                    ins.then_inc(dft_pe, 1)

            def mix_tail(kc, g):
                s = 8 * kc + g
                for i in range(2):
                    for n in range(3):
                        for c in range(2):
                            ins = pe.matmul(PS[0:C, PB[kc] + i, n * C:(n + 1) * C], OU[:, c, i, n * C:(n + 1) * C],
                                            PO[kc][:, c, :], start=c == 0, stop=c == 1)
                    ins.then_inc(pp_pe, 1)
                for i in range(2):
                    pe.wait_ge(ps_a, 2 * s + i + 1)
                    for kk in range(2):
                        t = 2 * i + kk
                        for n in range(3):
                            ins = pe.matmul(PS[:, IB[kc], t * C:(t + 1) * C], GDFT[:, n, kk * P:(kk + 1) * P],
                                            PSs[:, i, n * C:(n + 1) * C], start=n == 0, stop=n == 2)
                ins.then_inc(id_pe, 1)

            def block_mlp(w, src, banks, done):
                for j in range(4):
                    c, r = j // 2, j % 2
                    o = bank(banks[j], 2 * FR, C)
                    pe.matmul(o, BW[w][:, c, 0, :], src(c, r), start=True, stop=False)
                    pe.matmul(o, BW[w][:, c, 2 if r == 0 else 1, :], src(c, 1 - r), start=False, stop=True).then_inc(done, 1)

            def mixer2(g, p):
                mix_head(0, 3, g, p)
                prep_turn(24 + g + 1)
                pe.wait_ge(xf_a, 4 * g + 4)
                pe.wait_ge(z_a, 4 * g)
                block_mlp(0, lambda c, r: XF[:, c, r, :, :].rearrange("p i f -> p (i f)"), (6, 0, 1, 2), m1_pe)
                pe.wait_ge(o1_a, 4 * g + 4)
                block_mlp(1, lambda c, r: O1[:, c, r, :], (3, 4, 5, 6), m2_pe)
                pe.wait_ge(o_v, 4 * g + 4)
                mix_tail(0, g)
            pe.wait_ge(xu[3], GROUPS)
            for_steps(pe, mixer2)
            mixer2(6, 0)
            mixer2(7, 1)
            if stop < 5:
                return
            moe(4, 1, 4)
            if stop < 6:
                return

            pe.wait_ge(xu[5], GROUPS)
            cwv = cwx[:].rearrange("p (f r) -> p f r", r=2)
            for j in range(3):
                pe.matmul(bank(j, FR, NF), cwv[:, :, min(j, 1)], RB[:], start=True, stop=True).then_inc(cw_pe, 1)

            def fc1_(i):
                pe.wait_ge(pool_v, i + 1)
                pe.matmul(TB[0:24, 0:2], fc1[:], pl[:], start=True, stop=True).then_inc(f1_pe, 1)

            def fc2_(i):
                pe.wait_ge(rt_v, 5 * i + 1)
                for f in range(NF):
                    for c in range(2):
                        n = 16 + (f * 2 + c) * 2
                        w = f * MED + c * C
                        ins = pe.matmul(TB[:, n:n + 2], fc2[:, w:w + C], hh[:], start=True, stop=True)
                ins.then_inc(f2_pe, 1)

            def route_turn(i):
                pe.wait_ge(rt_m, i + 1)
                for q in range(4):
                    ins = pe.transpose(TB[0:NF, 128 + q * C:128 + (q + 1) * C], RTm[:, q // 2, q % 2, :], ident[0:C, 0:C])
                ins.then_inc(rt_pe, 1)

            fc1_(0)
            fc2_(0)
            route_turn(0)
            pe.wait_ge(cw_a, 3)

            def mixer3(g, p, route=True):
                mix_head(1, 5, g, p)
                prep_turn(40 + g + 1, False, (rt_x, g + 1))
                if route:
                    fc1_(g + 1)
                for j in range(4):
                    pe.wait_ge(rt_x, g + 1)
                    pe.wait_ge(xf_a, 32 + 4 * g + 4)
                    pe.matmul(bank(WB[j], 3 * FR, C), RT[p][:, j, :], CW[:], start=True, stop=True).then_inc(w_pe, 1)
                if route:
                    fc2_(g + 1)
                    route_turn(g + 1)
                pe.wait_ge(y_p, 4 * g + 4)
                mix_tail(1, g)
            for_steps(pe, mixer3)
            mixer3(6, 0)
            mixer3(7, 1, route=False)
            if stop < 7:
                return
            moe(6, 2, 6)


def shape_constants():
    k = {"k_ident": np.eye(P)}
    i = np.arange(P)
    col = np.arange(32)
    same = ((i[:, None] % 32) // 16 == col[None, :] // 16).astype(np.float64)
    k["k_bm0"], k["k_bm1"] = same, (same - 1) * BIG
    e = np.arange(EXP)
    tie = np.stack([e[None, :] > e[:, None], e[None, :] < e[:, None]])
    k["k_tie"] = np.broadcast_to(tie[None], (P, 2, EXP, EXP))
    c = np.stack(np.meshgrid(np.arange(4), np.arange(4), indexing="ij")).reshape(2, -1)
    d = (c[:, :, None] - c[:, None, :] + 3).transpose(1, 2, 0)
    idx = d[..., 0] * 7 + d[..., 1]
    k["k_onehot"] = (idx[i % 16][None].transpose(0, 2, 1) == np.arange(49)[:, None, None])
    h, w = np.divmod(np.arange(HW * HW), HW)
    ky, kx = np.divmod(np.arange(FR), WF)
    th = 2 * np.pi * ((h[:, None] * ky[None] + w[:, None] * kx[None]) % HW) / HW
    fwd = np.concatenate([np.cos(th), -np.sin(th)], 1) / HW
    k["k_dft"] = fwd.reshape(2, P, 2 * FR).transpose(1, 0, 2)
    twice = np.where((kx == 0) | (kx == HW // 2), 1.0, 2.0)[:, None]
    inv = np.concatenate([np.cos(th).T * twice, -np.sin(th).T * twice]) / HW
    k["k_idft"] = inv.reshape(3, C, HW * HW).transpose(1, 0, 2)

    def cubic(old, new):
        A, m = -0.75, np.zeros((new, old))
        pos = np.arange(new, dtype=np.float32) * np.float32((old - 1) / (new - 1))
        i0 = np.floor(pos).astype(int)
        fr = (pos - i0.astype(np.float32)).astype(np.float64)
        for o in (-1, 0, 1, 2):
            t = np.abs(fr - o)
            w1 = ((A + 2) * t - (A + 3)) * t * t + 1
            w2 = A * (((t - 5) * t + 8) * t - 4)
            wt = np.where(t <= 1, w1, np.where(t < 2, w2, 0))
            for n in range(new):
                m[n, np.clip(i0[n] + o, 0, old - 1)] += wt[n]
        return m
    k["k_bicubic"] = np.kron(cubic(14, HW), cubic(8, WF)).T
    return {n: np.ascontiguousarray(v, dtype=np.float32) for n, v in k.items()}


def kernel(**inputs):
    import concourse.bacc as bacc
    from concourse.bass_utils import run_bass_kernel_spmd

    nc = bacc.Bacc("TRN2", target_bir_lowering=False, num_devices=1)
    arrays = {n: np.ascontiguousarray(v) for n, v in inputs.items()}
    arrays["x"] = arrays["x"].reshape(TOK, C)
    arrays.update(shape_constants())
    aps = {n: nc.dram_tensor(n, v.shape, mybir.dt.from_np(v.dtype), kind="ExternalInput").ap() for n, v in arrays.items()}
    out = nc.dram_tensor("out", (TOK, C), F32, kind="ExternalOutput").ap()
    program(nc, aps, out)
    r = run_bass_kernel_spmd(nc, [arrays], core_ids=[0])
    return r.results[0]["out"].reshape(IMGS, HW, HW, C)
```

```python
import numpy as np

import concourse.bass as bass
from concourse import mybir
from contextlib import ExitStack

F32 = mybir.dt.float32
F32R = mybir.dt.float32r
BF16 = mybir.dt.bfloat16
ALU = mybir.AluOpType
ACT = mybir.ActivationFunctionType
AX = mybir.AxisListType

P = 128
IMGS, HW, C = 16, 16, 96
TOK = IMGS * HW * HW
TILES = TOK // P
GT = 4
GROUPS = TILES // GT
GTOK = GT * P
HEADS, DH = 3, 32
QSCALE = DH ** -0.5
HID, EXP = 384, 4
CH = HID // P
CK = EXP * CH
MED = 192
WF = HW // 2 + 1
FR = HW * WF
NF = 4
BIG = 1e30
LAMBDA = 0.01
QB, QEPS = 128.0, 1e-5
QCLIP = float(np.float32(QB - QEPS))
FT = 6
FG = 5
EULER = float(np.e)
EPS_C, EPS_T = 1e-6, 1e-5


def ds(start, n):
    return bass.ds(start, n)


def program(nc, a, out, stop=99):
    ctx = ExitStack()
    with ctx:
        def sb(name, shape, dt=F32):
            return ctx.enter_context(nc.sbuf_tensor(name, shape, dt))

        def sem(name):
            return ctx.enter_context(nc.semaphore(name))

        PS = ctx.enter_context(nc.psum_tensor("PS", [P, 8, 512], F32))

        def bank(i, n=512, rows=P):
            return PS[0:rows, i, 0:n]

        TB = bank(7, 512, C)

        X = sb("X", [P, TILES * C])
        ident = sb("ident", [P, P])
        stats = sb("stats", [P, FT, 6])
        msum = sb("msum", [P, FT])
        mdif = sb("mdif", [P, FT])
        m2 = sb("m2", [P, FT])
        mean = sb("mean", [P, FT])
        ve = sb("ve", [P, FT])
        rs = sb("rs", [P, FT])
        half = sb("half", [P, 8])
        quarter = sb("quarter", [P, 8])
        euler = sb("euler", [P, GT * EXP])
        XN = sb("XN", [P, FT, C])
        XH = [sb(f"XH{i}", [C + 1, GTOK], F32R) for i in range(2)]
        XL = [sb(f"XL{i}", [C + 1, GTOK], F32R) for i in range(2)]
        raw = sb("raw", [C + 1, EXP * HID])
        onesf = sb("onesf", [P, P])

        WAh = [sb(f"WAh{i}", [C + 1, 3 * C], F32R) for i in range(2)]
        WAl = [sb(f"WAl{i}", [C + 1, 3 * C], F32R) for i in range(2)]
        WM = [sb(f"WM{i}", [C + 1, C]) for i in range(2)]
        rel = sb("rel", [49, HEADS])
        BI = sb("BI", [P, HEADS, 32])
        bm0 = sb("bm0", [P, 32])
        bm1 = sb("bm1", [P, 32])
        qT = sb("qT", [C, GTOK])
        kT = sb("kT", [C, GTOK])
        V = sb("V", [P, GT, HEADS, DH + 1])
        SC = sb("SC", [P, HEADS, GT, 64])
        mx = sb("mx", [P, HEADS * GT])
        PF = sb("PF", [P, HEADS, GT, P])
        PT = sb("PT", [P, HEADS, GTOK])
        rc = sb("rc", [P, GT, HEADS])
        O = sb("O", [P, GT, C])
        OT = sb("OT", [C + 1, GTOK])

        w1raw = sb("w1raw", [P, CH, C])
        w2raw = sb("w2raw", [C, HID])
        W1B = sb("W1B", [C, HID], F32R)
        w1t = sb("w1t", [C, HID])
        W2B = sb("W2B", [P, CH, C])
        w2t = sb("w2t", [P, CH, C])
        gsum = sb("gsum", [P, 8])
        gsum2 = sb("gsum2", [P, 8])
        sg2 = sb("sg2", [P, CH * C])
        gmean = sb("gmean", [P, 16])
        sg = sb("sg", [P, HID])
        b1c = sb("b1c", [P, CH])
        b2bc = sb("b2bc", [P, C])
        FH = sb("FH", [C, FT * P], F32R)
        FL = sb("FL", [C, FT * P], F32R)
        am = sb("am", [P, 2, 6])
        am1 = sb("am1", [P, 2])
        gmx = sb("gmx", [1, 2])
        qe = sb("qe", [P, 2])
        qr = sb("qr", [P, 2])
        qs = sb("qs", [P, 2])
        ql = sb("ql", [P, 2, 2])
        Y2 = sb("Y2", [P, FT, C])

        M1h = [sb(f"M1h{i}", [C + 1, EXP * HID], F32R) for i in range(3)]
        M1l = [sb(f"M1l{i}", [C + 1, EXP * HID], F32R) for i in range(3)]
        M2 = [sb(f"M2_{i}", [P, CK, C]) for i in range(3)]
        GWr = [sb(f"GWr{i}", [C + 1, EXP]) for i in range(3)]
        GWh = [sb(f"GWh{i}", [C + 1, EXP], F32R) for i in range(3)]
        GWl = [sb(f"GWl{i}", [C + 1, EXP], F32R) for i in range(3)]
        B2s = [sb(f"B2s{i}", [65, EXP * C], BF16) for i in range(3)]
        onesb = sb("onesb", [65, P], BF16)
        H = [sb(f"H{i}", [P, CK, GTOK]) for i in range(2)]
        tie = sb("tie", [P, 2, EXP, EXP])
        smx = sb("smx", [P, GT])
        dl = sb("dl", [P, GT, EXP])
        ex = sb("ex", [P, GT, EXP])
        cg = sb("cg", [P, GT, EXP, EXP])
        ce = sb("ce", [P, GT, EXP, EXP])
        rk = sb("rk", [P, GT, EXP])
        me = sb("me", [P, GT, EXP])
        s1 = sb("s1", [P, GT])
        s0 = sb("s0", [P, GT])
        G = sb("G", [P, GT, EXP])

        FDFT = sb("FDFT", [P, 2, 2 * FR])
        GDFT = sb("GDFT", [C, 3, HW * HW])
        PWr = [sb(f"PWr{i}", [C, MED]) for i in range(2)]
        PWh = [sb(f"PWh{i}", [C, MED], F32R) for i in range(2)]
        PWl = [sb(f"PWl{i}", [C, MED], F32R) for i in range(2)]
        PO = [sb(f"PO{i}", [C, 2, C]) for i in range(2)]
        SBc = [sb(f"SBc{i}", [P, 2]) for i in range(2)]
        BW = [sb(f"BW{i}", [C, 2, 3, C]) for i in range(2)]
        BB = [sb(f"BB{i}", [C, 2, 2]) for i in range(2)]
        hflat = [H[i][:, :, :].rearrange("p a b -> p (a b)") for i in range(2)]
        R = hflat[0][:, 0:768].rearrange("p (t m) -> p t m", t=GT)
        SQ = hflat[0][:, 768:1536].rearrange("p (t m) -> p t m", t=GT)
        HH = hflat[0][:, 1536:2304].rearrange("p (t m) -> p t m", t=GT)
        XF = [hflat[0][0:C, o:o + 1152].rearrange("p (c r i f) -> p c r i f", c=2, r=2, i=2) for o in (2304, 3456)]
        O1 = hflat[0][0:C, 4608:4608 + 1152].rearrange("p (c r n) -> p c r n", c=2, r=2)
        Z = hflat[1][0:C, 4608:4608 + 1152].rearrange("p (c r n) -> p c r n", c=2, r=2)
        CL = hflat[1][0:C, 0:1152].rearrange("p (c r n) -> p c r n", c=2, r=2)
        ZX = hflat[1][0:C, 1152:2304].rearrange("p (c r n) -> p c r n", c=2, r=2)
        OU = hflat[1][0:C, 2304:2304 + 1152].rearrange("p (c i n) -> p c i n", c=2, i=2)
        PSs = hflat[1][0:C, 3456:3456 + 576].rearrange("p (i n) -> p i n", i=2)
        Y1 = [hflat[1][:, o:o + CH * FT * P].rearrange("p (c n) -> p c n", c=CH) for o in (0, CH * FT * P)]
        YH = hflat[0][:, 0:CH * FT * P].rearrange("p (c n) -> p c n", c=CH)
        n2 = EXP * C
        B2r = [hflat[1][0:65, i * n2:(i + 1) * n2] for i in range(3)]
        b2b, b2d = (hflat[1][0:65, (3 + i) * n2:(4 + i) * n2] for i in range(2))
        b2a, b2c, b2e = (hflat[1][0:65, (5 + i) * n2:(6 + i) * n2].bitcast(BF16)[:, 0:n2] for i in range(3))
        EH = hflat[0][0:49, 0:16 * P].rearrange("p (j n) -> p j n", j=16)
        cwx = sb("cwx", [112, 2 * NF])
        RB = sb("RB", [112, FR])
        CW = sb("CW", [NF, 3 * FR])
        fc1 = sb("fc1", [C, 24])
        fc2 = sb("fc2", [24, NF * MED])
        msb = sb("msb", [24, 2])
        pl = sb("pl", [C, 2, 2])
        hr = sb("hr", [24, 2])
        hq = sb("hq", [24, 2])
        hh = sb("hh", [24, 2])
        lmx = sb("lmx", [C, 2, 2])
        lg = sb("lg", [C, NF, 2, 2])
        le = sb("le", [C, NF, 2, 2])
        lsum = sb("lsum", [C, 2, 2])
        lrc = sb("lrc", [C, 2, 2])
        RTm = sb("RTm", [C, 2, 2, NF])
        RT = [sb(f"RT{i}", [NF, 4, C]) for i in range(2)]
        MA = hflat[1][0:C, 0:1152].rearrange("p (q r n) -> p q r n", q=4, r=2)
        MB = hflat[1][0:C, 1152:2304].rearrange("p (q r n) -> p q r n", q=4, r=2)

        xin, cst, watt, wffn, wmoe, wfft = (sem(n) for n in ("xin", "cst", "watt", "wffn", "wmoe", "wfft"))
        ms_p, ms_v, split_v = sem("ms_p"), sem("ms_v"), sem("split_v")
        bias_pe, bias_v = sem("bias_pe"), sem("bias_v")
        wt_pe, wt_v, wm_s = sem("wt_pe"), sem("wt_v"), sem("wm_s")
        st_v, ag_p, rs_p, xn_v = (sem(n) for n in ("st_v", "ag_p", "rs_p", "xn_v"))
        tp_pe, hi_a, lo_v, xt_used = (sem(n) for n in ("tp_pe", "hi_a", "lo_v", "xt_used"))
        xu = [sem(f"x_updated{i}") for i in range(8)]
        q_pe, k_pe, q_a, k_a, v_v, s_pe, sc_r, mx_v, sub_v, exp_a = (
            sem(n) for n in ("q_pe", "k_pe", "q_a", "k_a", "v_v", "s_pe", "sc_r", "mx_v", "sub_v", "exp_a"))
        ptp_pe, pt_a, pt_v, pv_pe, rcp_v, nrm_v, ot_pe, ot_a, wo_pe = (
            sem(n) for n in ("ptp_pe", "pt_a", "pt_v", "pv_pe", "rcp_v", "nrm_v", "ot_pe", "ot_a", "wo_pe"))
        ft_pe, fh_a, fl_v, fu_pe, y1_a, ab_v, gm1_v, gm2_v, g1_pe, g2_pe = (
            sem(n) for n in ("ft_pe", "fh_a", "fl_v", "fu_pe", "y1_a", "ab_v", "gm1_v", "gm2_v", "g1_pe", "g2_pe"))
        qs1_v, qs2_v = sem("qs1_v"), sem("qs2_v")
        fst_v, fag_p, frs_p, fxn_v = (sem(n) for n in ("fst_v", "fag_p", "frs_p", "fxn_v"))
        cl_v, ge_a, fd_pe, y2_v = (sem(n) for n in ("cl_v", "ge_a", "fd_pe", "y2_v"))
        up_pe, gelu_a, dn_pe, gate_v, gexp_p, comb_v = (
            sem(n) for n in ("up_pe", "gelu_a", "dn_pe", "gate_v", "gexp_p", "comb_v"))
        part_v = sem("part_v")
        h_pe, r_a, sq_a, h_v, dft_pe, xf_a, m1_pe, o1_a, m2_pe, z_a = (
            sem(n) for n in ("h_pe", "r_a", "sq_a", "h_v", "dft_pe", "xf_a", "m1_pe", "o1_a", "m2_pe", "z_a"))
        c_v, zx_p, o_v, pp_pe, ps_a, id_pe = (sem(n) for n in ("c_v", "zx_p", "o_v", "pp_pe", "ps_a", "id_pe"))
        cw_pe, cw_a, w_pe, prod_v, y_p, pool_v, f1_pe, rt_a, rt_v, f2_pe, rt_pe, rt_x, le_a = (
            sem(n) for n in ("cw_pe", "cw_a", "w_pe", "prod_v", "y_p", "pool_v", "f1_pe", "rt_a", "rt_v", "f2_pe",
                             "rt_pe", "rt_x", "le_a"))
        stored, split_m, split_b, ql_v, rt_m = (sem(n) for n in ("stored", "split_m", "split_b", "ql_v", "rt_m"))

        block = ctx.enter_context(nc.Block())

        NGV = 11
        AB = 8
        NWFFT = 4 + 8 + 2 * 20 + 5
        DB, PB, IB = ((3, 4, 5, 6), (6, 4, 5, 0)), (0, 1), (2, 3)

        def xt(g, t):
            return X[:, ds(g * (GT * C) + t * C, C)]

        def xg(g):
            return X[:, ds(g * (GT * C), GT * C)]


        def walk(eng, body, first, lo, hi, last):
            for g in range(first, lo):
                body(g, g % 2)
            with eng.Fori(0, (hi + 1 - lo) // 2) as pair:
                body(2 * pair + lo, lo % 2)
                body(2 * pair + (lo + 1), 1 - lo % 2)
            for g in range(hi + 1, last + 1):
                body(g, g % 2)

        def has(g, n, least=0, most=GROUPS - 1):
            return not isinstance(g, int) or least <= g + n <= most

        def after(eng, s, value):
            if not (isinstance(value, int) and value <= 0):
                eng.wait_ge(s, value)

        def attention_walk(eng, body):
            walk(eng, body, -2, 1, 4, GROUPS - 1)

        def moe_walk(eng, body):
            walk(eng, body, -1, 1, 4, GROUPS - 1)

        def mixer_walk(eng, body):
            walk(eng, body, -1, 1, 4, GROUPS - 1)

        PREPS = {0: 7, 2: 9, 3: 9, 4: 9, 5: 9, 6: 9, 7: 7}
        EPS = {0: EPS_C, 2: EPS_C, 3: EPS_T, 4: EPS_C, 5: EPS_T, 6: EPS_C, 7: EPS_T}

        def eps_of(phase, n):
            return EPS[phase + 1] if isinstance(n, int) and n >= GROUPS else EPS[phase]

        @block.sync
        def _(sp):
            with nc.allow_non_contiguous_dma(reason="small weights"):
                n = TILES // 4
                for i in range(4):
                    sp.dma_start(X[:, i * n * C:(i + 1) * n * C].rearrange("p (i c) -> p i c", c=C),
                                 a["x"][i * n * P:(i + 1) * n * P, :].rearrange("(i p) c -> p i c", p=P)).then_inc(xin, 16)
                sp.dma_start(w1raw[:], a["L0_ffn_W1"].rearrange("(c p) i -> p c i", p=P)).then_inc(wffn, 16)
                sp.dma_start(w2raw[:], a["L0_ffn_W2"]).then_inc(wffn, 16)
                sp.dma_start(b1c[:], a["L0_ffn_b1"].rearrange("(c p) -> p c", p=P)).then_inc(wffn, 16)
                sp.dma_start(b2bc[:], a["L0_ffn_b2"].partition_broadcast(P)).then_inc(wffn, 16)
                for i, nm in enumerate(("L1_ffn", "L2_ffn", "L3_ffn")):
                    if i and stop < 3:
                        break
                    sp.wait_ge(split_v, 4 if i == 0 else 4 * i + 2)
                    sp.dma_start(raw[0:C, :].rearrange("c (e h) -> c e h", e=EXP),
                                 a[nm + "_w1"].rearrange("e c h -> c e h")).then_inc(wm_s, 16)
                    sp.dma_start(raw[C:C + 1, :], a[nm + "_b1"].rearrange("(a e) h -> a (e h)", a=1)).then_inc(wm_s, 16)
                    if i > 0:
                        continue
                    for x, nx in enumerate(("L1_ffn", "L2_ffn", "L3_ffn")):
                        sp.dma_start(GWr[x][0:C, :], a[nx + "_gate_w"]).then_inc(wmoe, 16)
                        sp.dma_start(GWr[x][C:C + 1, :], a[nx + "_gate_b"].rearrange("(a n) -> a n", a=1)).then_inc(wmoe, 16)
                        sp.dma_start(B2r[x], a[nx + "_b2"].rearrange("e d -> (e d)").partition_broadcast(65))\
                            .then_inc(wmoe, 16)
                        sp.dma_start(M2[x][:], a[nx + "_w2"].rearrange("e (c p) d -> p (e c) d", p=P)).then_inc(wmoe, 16)
                    sp.dma_start(tie[:], a["k_tie"]).then_inc(wfft, 16)
                    sp.dma_start(FDFT[:], a["k_dft"]).then_inc(wfft, 16)
                    sp.dma_start(GDFT[:], a["k_idft"]).then_inc(wfft, 16)
                    sp.dma_start(RB[:], a["k_bicubic"]).then_inc(wfft, 16)
                    sp.wait_ge(ms_v, 2)
                    for l, (w, nc_) in enumerate((("w_pw1", "L2_conv"), ("pwconv1_w", "L3_conv"))):
                        sp.dma_start(PWr[l][:], a[f"{nc_}_{w}"]).then_inc(wfft, 16)
                        w2 = a["L2_conv_w_pw2" if l == 0 else "L3_conv_pwconv2_w"]
                        sp.dma_start(PO[l][:], w2.rearrange("(k p) c -> p k c", p=C)).then_inc(wfft, 16)
                        sc, bi = ("star_scale", "star_bias") if l == 0 else ("act1_scale", "act1_bias")
                        sp.dma_start(SBc[l][:, 0:1], a[f"{nc_}_{sc}"].partition_broadcast(P)).then_inc(wfft, 16)
                        sp.dma_start(SBc[l][:, 1:2], a[f"{nc_}_{bi}"].partition_broadcast(P)).then_inc(wfft, 16)
                    for l in range(2):
                        w, b = a[f"L2_conv_w{l + 1}"], a[f"L2_conv_b{l + 1}"]
                        for c in range(2):
                            for r in range(2):
                                for k in range(4):
                                    sp.dma_start(BW[l][24 * k:24 * k + 24, c, r, 24 * k:24 * k + 24],
                                                 w[r, 4 * c + k, :, :]).then_inc(wfft, 16)
                                sp.dma_start(BB[l][:, c, r:r + 1],
                                             b[r, 4 * c:4 * c + 4, :].rearrange("k (o a) -> (k o) a", a=1)).then_inc(wfft, 16)
                    sp.dma_start(cwx[:], a["L3_conv_complex_weights"].rearrange("h w f r -> (h w) (f r)")).then_inc(wfft, 16)
                    sp.dma_start(fc1[:], a["L3_conv_fc1_w"]).then_inc(wfft, 16)
                    sp.dma_start(fc2[:], a["L3_conv_fc2_w"]).then_inc(wfft, 16)
                    sp.dma_start(msb[:, 0:1], a["L3_conv_mlp_scale"].partition_broadcast(24)).then_inc(wfft, 16)
                    sp.dma_start(msb[:, 1:2], a["L3_conv_mlp_bias"].partition_broadcast(24)).then_inc(wfft, 16)
            for g in range(GROUPS):
                sp.wait_ge(xu[min(stop, 7)], FG if stop == 1 else g + 1)
                sp.dma_start(out[g * GTOK:(g + 1) * GTOK, :].rearrange("(i p) c -> p i c", p=P),
                             X[:, g * GT * C:(g + 1) * GT * C].rearrange("p (i c) -> p i c", c=C)).then_inc(stored, 16)
            sp.wait_ge(stored, 16 * GROUPS)

        @block.gpsimd
        def _(pool):
            pool.memset(half[:], -0.5).then_inc(ms_p, 1)
            pool.memset(euler[:], EULER).then_inc(ms_p, 1)
            pool.memset(quarter[:], 0.25).then_inc(ms_p, 1)
            pool.wait_ge(ms_p, 3)

            def row_stats(m, eps, n, have, part, done):
                pool.wait_ge(have, m + 1)
                pool.tensor_tensor(msum[:, 0:n], stats[:, 0:n, 1], stats[:, 0:n, 4], ALU.add)
                pool.tensor_tensor(mdif[:, 0:n], stats[:, 0:n, 1], stats[:, 0:n, 4], ALU.subtract)
                pool.tensor_tensor(m2[:, 0:n], stats[:, 0:n, 2], stats[:, 0:n, 5], ALU.add).then_inc(part, 1)
                pool.wait_ge(part, 4 * m + 1)
                pool.tensor_tensor(mdif[:, 0:n], mdif[:, 0:n], mdif[:, 0:n], ALU.mult)
                pool.tensor_scalar(mean[:, 0:n], msum[:, 0:n], 0.5, None, ALU.mult)
                pool.tensor_scalar(m2[:, 0:n], m2[:, 0:n], 1.0 / C, eps, ALU.mult, ALU.add).then_inc(part, 1)
                pool.wait_ge(part, 4 * m + 2)
                pool.tensor_tensor(ve[:, 0:n], mdif[:, 0:n], quarter[:, 0:n], ALU.mult).then_inc(part, 1)
                pool.wait_ge(part, 4 * m + 3)
                pool.tensor_tensor(ve[:, 0:n], ve[:, 0:n], m2[:, 0:n], ALU.add).then_inc(part, 1)
                pool.wait_ge(part, 4 * m + 4)
                pool.tensor_tensor(rs[:, 0:n], ve[:, 0:n], half[:, 0:n], ALU.pow).then_inc(done, 1)

            def prep(phase, k, n):
                row_stats(8 * k + n, eps_of(phase, n), GT, st_v, ag_p, rs_p)

            def attention(phase, k):
                def body(g, p):
                    if has(g, 3, 2, PREPS[phase]):
                        prep(phase, k, g + 3)
                attention_walk(pool, body)

            def moe(phase, k, e):
                def body(g, p):
                    if has(g, 0):
                        pool.wait_ge(gate_v, NGV * (8 * e + g) + 2)
                        pool.tensor_tensor(ex[:, :, :].rearrange("p t e -> p (t e)"), euler[:],
                                           dl[:, :, :].rearrange("p t e -> p (t e)"), ALU.pow).then_inc(gexp_p, 1)
                    if has(g, 2, 2, PREPS[phase]):
                        prep(phase, k, g + 2)
                moe_walk(pool, body)

            def mixer2(g, p):
                if has(g, 2, 2, PREPS[4]):
                    prep(4, 3, g + 2)
                if has(g, 0):
                    for j in range(4):
                        c, r = j // 2, j % 2
                        pool.wait_ge(z_a, 4 * g + j + 1)
                        after(pool, o_v, 4 * g)
                        pool.tensor_tensor(ZX[:, c, r, :], Z[:, c, r, :],
                                           XF[p][:, c, r, :, :].rearrange("p i f -> p (i f)"), ALU.add).then_inc(zx_p, 1)

            def mixer3(g, p):
                if has(g, 2, 2, PREPS[6]):
                    prep(6, 5, g + 2)
                if has(g, 0):
                    for j in range(4):
                        pool.wait_ge(prod_v, 3 * (4 * g + j) + 3)
                        pool.wait_ge(pp_pe, 16 + 2 * g)
                        pool.tensor_tensor(OU[:, j // 2, j % 2, :], MA[:, j, :, :].rearrange("p r n -> p (r n)"),
                                           MB[:, j, :, :].rearrange("p r n -> p (r n)"), ALU.add).then_inc(y_p, 1)

            prep(0, 0, 0)
            prep(0, 0, 1)
            attention(0, 0)
            if stop < 1:
                return
            for q in range(FG):
                row_stats(q, EPS_T, FT, fst_v, fag_p, frs_p)
            if stop < 2:
                return
            prep(2, 1, 0)
            prep(2, 1, 1)
            attention(2, 1)
            if stop < 3:
                return
            moe(3, 2, 0)
            if stop < 4:
                return
            mixer_walk(pool, mixer2)
            if stop < 5:
                return
            moe(5, 4, 1)
            if stop < 6:
                return
            mixer_walk(pool, mixer3)
            if stop < 7:
                return
            moe(7, 6, 2)

        @block.scalar
        def _(act):
            with nc.allow_non_contiguous_dma(reason="small weights"):
                act.dma_start(ident[:], a["k_ident"]).then_inc(watt, 16)
                act.dma_start(raw[0:C, 0:3 * C], a["L0_conv_Wqkv"]).then_inc(watt, 16)
                act.wait_ge(ms_v, 1)
                act.dma_start(raw[C:C + 1, 0:3 * C], a["L0_conv_bqkv"].rearrange("(a n) -> a n", a=1)).then_inc(watt, 16)
                act.dma_start(EH, a["k_onehot"]).then_inc(watt, 16)
                act.dma_start(rel[:], a["L0_conv_rel_table"]).then_inc(watt, 16)
                act.dma_start(bm0[:], a["k_bm0"]).then_inc(watt, 16)
                act.dma_start(bm1[:], a["k_bm1"]).then_inc(watt, 16)
                act.dma_start(raw[0:C, 3 * C:6 * C], a["L1_conv_w_qkv"]).then_inc(watt, 16)
                act.dma_start(WM[0][0:C, :], a["L0_conv_Wm"]).then_inc(watt, 16)
                act.dma_start(WM[0][C:C + 1, :], a["L0_conv_bm"].rearrange("(a n) -> a n", a=1)).then_inc(watt, 16)
                act.dma_start(WM[1][0:C, :], a["L1_conv_w_out"]).then_inc(watt, 16)
                act.dma_start(WM[1][C:C + 1, :], a["L1_conv_b_out"].rearrange("(a n) -> a n", a=1)).then_inc(watt, 16)

            def prep_hi(m, p):
                act.wait_ge(tp_pe, m + 1)
                after(act, xt_used, m - 1)
                act.activation(XH[p][0:C, :], TB, ACT.Copy).then_inc(hi_a, 1)

            def attention(phase, ka):
                bs = 32 if ka == 0 else 64

                def body(g, p):
                    n, m = 8 * ka + g, 8 * ka + g
                    if has(g, 0):
                        after(act, pv_pe, n)
                        for h in range(2):
                            act.wait_ge(ptp_pe, 3 * n + h + 1)
                            act.activation(PT[:, h, :], bank(h), ACT.Copy).then_inc(pt_a, 1)
                    if has(g, 1) and ka == 1:
                        act.wait_ge(s_pe, n + 2)
                        after(act, exp_a, n + 1)
                        for q in range(P // bs):
                            rows = slice(q * bs, (q + 1) * bs)
                            S = PS[rows, 3:6, :].rearrange("p h (t j) -> p h t j", t=GT)[:, :, :, rows]
                            ins = act.activation(SC[rows, :, :, 0:bs], S, ACT.Copy)
                        ins.then_inc(sc_r, 1)
                    if has(g, 2):
                        act.wait_ge(q_pe, n + 3)
                        after(act, s_pe, n + 2)
                        act.activation(qT[:], bank(0, 512, C), ACT.Copy, scale=QSCALE).then_inc(q_a, 1)
                        act.wait_ge(k_pe, n + 3)
                        act.activation(kT[:], bank(1, 512, C), ACT.Copy).then_inc(k_a, 1)
                    if has(g, 0):
                        act.wait_ge(ot_pe, n + 1)
                        after(act, wo_pe, n)
                        act.activation(OT[0:C, :], bank(6, 512, C), ACT.Copy).then_inc(ot_a, 1)
                    if has(g, 1):
                        act.wait_ge(sub_v, n + 2)
                        after(act, ptp_pe, 3 * n + 3)
                        for q in range(P // bs):
                            rows = slice(q * bs, (q + 1) * bs)
                            ins = act.activation(PF[rows, :, :, rows], SC[rows, :, :, 0:bs], ACT.Exp)
                        ins.then_inc(exp_a, 1)
                    if has(g, 3, 2, PREPS[phase]):
                        prep_hi(m + 3, 1 - p)
                attention_walk(act, body)

            prep_hi(0, 0)
            prep_hi(1, 1)
            attention(0, 0)
            if stop < 1:
                return

            for q in range(-2, FG):
                if 0 <= q + 1 < FG:
                    for j in range(6):
                        c, u = j // 2, j % 2
                        act.wait_ge(fu_pe, 6 * (q + 1) + j + 1)
                        after(act, ge_a, 3 * q)
                        act.activation(Y1[(q + 1) % 2][:, c, u * 3 * P:(u + 1) * 3 * P], bank(j % 3, 3 * P), ACT.Identity,
                                       bias=b1c[:, c:c + 1]).then_inc(y1_a, 1)
                if q + 2 < FG:
                    act.wait_ge(ft_pe, q + 3)
                    act.activation(FH[:].rearrange("p (u n) -> p u n", u=2), PS[0:C, 5:7, 0:3 * P], ACT.Copy).then_inc(fh_a, 1)
                if 0 <= q + 1 < FG:
                    for c in range(CH):
                        act.wait_ge(cl_v, 3 * (q + 1) + c + 1)
                        after(act, fd_pe, 2 * (q + 1))
                        act.activation(YH[:, c, :], Y1[(q + 1) % 2][:, c, :], ACT.Gelu, scale=qs[:, 0:1]).then_inc(ge_a, 1)
            if stop < 2:
                return

            prep_hi(8, 0)
            prep_hi(9, 1)
            attention(2, 1)
            if stop < 3:
                return

            def moe(phase, k, e):
                def gelus(b, p, lo, hi):
                    for c in range(lo, hi):
                        act.wait_ge(up_pe, CK * b + c + 1)
                        after(act, dn_pe, 4 * b - 4)
                        act.activation(H[p][:, c, :], bank(c % 4), ACT.Gelu).then_inc(gelu_a, 1)

                def body(g, p):
                    if has(g, 1):
                        gelus(8 * e + g + 1, 1 - p, 0, 9)
                    if has(g, 2, 2, PREPS[phase]):
                        prep_hi(8 * k + g + 2, p)
                    if has(g, 1):
                        gelus(8 * e + g + 1, 1 - p, 9, 12)
                moe_walk(act, body)

            def mix_relu(kc, k, g):
                s = 8 * kc + g + 1
                after(act, h_v, s)
                act.wait_ge(h_pe, s + 1)
                act.activation(R[:, 0:2, :], bank(4, 2 * MED).rearrange("p (t m) -> p t m", t=2), ACT.Relu).then_inc(r_a, 1)
                act.wait_ge(xt_used, 8 * k + g + 2)
                act.activation(R[:, 2:4, :], bank(5, 2 * MED).rearrange("p (t m) -> p t m", t=2), ACT.Relu).then_inc(r_a, 1)
                act.wait_ge(r_a, 2 * s + 2)
                act.activation(SQ, R, ACT.Square).then_inc(sq_a, 1)

            def mix_spectrum(kc, g, p):
                s = 8 * kc + g + 1
                for j in range(4):
                    c, i = j // 2, j % 2
                    act.wait_ge(dft_pe, 4 * s + j + 1)
                    if kc == 0:
                        after(act, zx_p, 4 * g)
                    else:
                        after(act, prod_v, 12 * g)
                    act.activation(XF[1 - p][:, c, :, i, :], bank(DB[kc][j], 2 * FR, C).rearrange("p (r f) -> p r f", r=2),
                                   ACT.Copy).then_inc(xf_a, 1)

            def mix_out(kc, g):
                s = 8 * kc + g
                for i in range(2):
                    act.wait_ge(pp_pe, 2 * s + i + 1)
                    after(act, id_pe, s)
                    act.activation(PSs[:, i, :], bank(PB[kc] + i, 3 * C, C), ACT.Copy).then_inc(ps_a, 1)

            def mixer2(g, p):
                if has(g, 0):
                    for j in range(4):
                        c, r = j // 2, j % 2
                        act.wait_ge(m1_pe, 4 * g + j + 1)
                        after(act, m2_pe, 4 * g)
                        act.activation(O1[:, c, r, :], bank(j, 2 * FR, C), ACT.Relu,
                                       bias=BB[0][:, c, r:r + 1]).then_inc(o1_a, 1)
                if has(g, 1):
                    mix_relu(0, 3, g)
                if has(g, 0):
                    for j in range(4):
                        c, r = j // 2, j % 2
                        act.wait_ge(m2_pe, 4 * g + j + 1)
                        after(act, o_v, 4 * g)
                        act.activation(Z[:, c, r, :], bank((6, 0, 1, 2)[j], 2 * FR, C), ACT.Identity,
                                       bias=BB[1][:, c, r:r + 1]).then_inc(z_a, 1)
                if has(g, 1):
                    mix_spectrum(0, g, p)
                if has(g, 2, 2, PREPS[4]):
                    prep_hi(24 + g + 2, p)
                if has(g, 0):
                    mix_out(0, g)

            moe(3, 2, 0)
            if stop < 4:
                return
            mixer_walk(act, mixer2)
            if stop < 5:
                return
            moe(5, 4, 1)
            if stop < 6:
                return

            def routing_relu(i):
                act.wait_ge(f1_pe, i + 1)
                act.activation(hr[:], TB[0:24, 0:2], ACT.Relu, scale=1.0 / (HW * HW)).then_inc(rt_a, 1)
                act.wait_ge(rt_a, 2 * i + 1)
                act.activation(hq[:], hr[:], ACT.Square).then_inc(rt_a, 1)

            def routing_exp(i):
                act.wait_ge(rt_v, 5 * i + 3)
                act.activation(le[:], lg[:], ACT.Exp).then_inc(le_a, 1)

            for j in range(3):
                act.wait_ge(cw_pe, j + 1)
                act.activation(CW[:, j * FR:(j + 1) * FR], bank(j, FR, NF), ACT.Copy,
                               scale=-1.0 if j == 1 else 1.0).then_inc(cw_a, 1)
            for i in range(2):
                routing_relu(i)
                routing_exp(i)

            def mixer3(g, p):
                if has(g, 1):
                    mix_relu(1, 5, g)
                if has(g, 2, 2, PREPS[6]):
                    prep_hi(40 + g + 2, p)
                if has(g, 1):
                    mix_spectrum(1, g, p)
                if has(g, 2, 2):
                    routing_relu(g + 2)
                if has(g, 0):
                    mix_out(1, g)
                if has(g, 2, 2):
                    routing_exp(g + 2)
            mixer_walk(act, mixer3)
            if stop < 7:
                return
            moe(7, 6, 2)

        @block.vector
        def _(dve):
            dve.memset(raw[C:C + 1, 0:2 * 3 * C], 0.0).then_inc(ms_v, 1)
            for i in range(2):
                ins = dve.memset(BW[i][:], 0.0)
            ins.then_inc(ms_v, 1)
            dve.memset(onesf[:], 1.0)
            for i in range(2):
                dve.memset(XH[i][C:C + 1, :].bitcast(F32), 1.0)
                dve.memset(XL[i][C:C + 1, :].bitcast(F32), 0.0)
            dve.memset(OT[C:C + 1, :], 1.0)
            dve.memset(V[:], 1.0).then_inc(ms_v, 1)
            dve.wait_ge(ms_v, 3)

            def halves(hi, lo, src, count):
                dve.tensor_copy(hi, src).then_inc(split_v, 1)
                dve.wait_ge(split_v, count + 1)
                dve.tensor_tensor(lo, src, hi.bitcast(F32), ALU.subtract).then_inc(split_v, 1)

            def prep_stats(m, n, prev, this):
                if isinstance(n, int) and n >= GROUPS:
                    dve.wait_ge(this, n - GROUPS + 1)
                    n = n - GROUPS
                elif isinstance(prev, tuple):
                    dve.wait_ge(*prev)
                else:
                    dve.wait_ge(prev, n + 1)
                after(dve, rs_p, m)
                for t in range(GT):
                    ins = dve.bn_stats(stats[:, t, :], xt(n, t))
                ins.then_inc(st_v, 1)

            def prep_norm(m, n):
                n = n - GROUPS if isinstance(n, int) and n >= GROUPS else n
                dve.wait_ge(rs_p, m + 1)
                after(dve, tp_pe, m)
                for t in range(GT):
                    ins = dve.tensor_scalar(XN[:, t, :], xt(n, t), mean[:, t:t + 1], rs[:, t:t + 1],
                                            ALU.subtract, ALU.mult)
                ins.then_inc(xn_v, 1)

            def prep_lo(m, p, pool=None):
                dve.wait_ge(hi_a, m + 1)
                dve.tensor_tensor(XL[p][0:C, :], TB, XH[p][0:C, :].bitcast(F32), ALU.subtract).then_inc(lo_v, 1)
                if pool is not None:
                    after(dve, f1_pe, pool - 1)
                    dve.tensor_reduce(pl[:, p, :], TB.rearrange("p (i n) -> p i n", i=2), AX.X, ALU.add).then_inc(pool_v, 1)

            def attention(phase, ka, prev):
                bs = 32 if ka == 0 else 64
                scv = SC[:, :, :, 0:bs].rearrange("p h t j -> p (h t) j")
                o = bank(6, GT * HEADS * (DH + 1)).rearrange("p (t h d) -> p t h d", t=GT, h=HEADS)
                upd = xu[phase]

                def body(g, p):
                    n, m = 8 * ka + g, 8 * ka + g
                    prep = has(g, 3, 2, PREPS[phase])
                    if has(g, 0):
                        dve.wait_ge(ptp_pe, 3 * n + 3)
                        after(dve, pv_pe, n)
                        dve.tensor_copy(PT[:, 2, :], bank(2)).then_inc(pt_v, 1)
                    if prep:
                        prep_stats(m + 3, g + 3, prev, upd)
                    if has(g, 1) and ka == 0:
                        dve.wait_ge(s_pe, n + 2)
                        after(dve, exp_a, n + 1)
                        for q in range(P // bs):
                            rows = slice(q * bs, (q + 1) * bs)
                            S = PS[rows, 3:6, :].rearrange("p h (t j) -> p h t j", t=GT)[:, :, :, rows]
                            ins = dve.tensor_tensor(SC[rows, :, :, 0:bs], S,
                                                    BI[rows, :, :].unsqueeze(2).to_broadcast([bs, HEADS, GT, bs]), ALU.add)
                        ins.then_inc(sc_r, 1)
                    if has(g, 0):
                        dve.wait_ge(pv_pe, n + 1)
                        dve.reciprocal(rc[:], o[:, :, :, DH]).then_inc(rcp_v, 1)
                        dve.wait_ge(rcp_v, n + 1)
                        after(dve, ot_pe, n)
                        dve.tensor_tensor(O[:].rearrange("p t (h d) -> p t h d", h=HEADS), o[:, :, :, 0:DH],
                                          rc[:].unsqueeze(3).to_broadcast([P, GT, HEADS, DH]), ALU.mult).then_inc(nrm_v, 1)
                    if has(g, 1):
                        dve.wait_ge(sc_r, n + 2)
                        dve.tensor_reduce(mx[:], scv, AX.X, ALU.max).then_inc(mx_v, 1)
                        dve.wait_ge(mx_v, n + 2)
                        dve.tensor_tensor(scv, scv, mx[:].unsqueeze(2).to_broadcast([P, HEADS * GT, bs]), ALU.subtract)\
                           .then_inc(sub_v, 1)
                    if prep:
                        prep_norm(m + 3, g + 3)
                    if has(g, 1):
                        dve.wait_ge(xt_used, m + 2)
                        dve.tensor_copy(V[:, :, :, 0:DH], bank(2, GT * C).rearrange("p (t h d) -> p t h d", t=GT, h=HEADS))\
                           .then_inc(v_v, 1)
                    if prep:
                        prep_lo(m + 3, 1 - p)
                    if has(g, 0):
                        dve.wait_ge(wo_pe, n + 1)
                        dve.tensor_tensor(xg(g), xg(g), bank(6, GT * C), ALU.add).then_inc(upd, 1)
                attention_walk(dve, body)

            for i in range(2):
                dve.wait_ge(xin, 64)
                prep_stats(i, i, (xin, 64), None)
                prep_norm(i, i)
                if i == 0:
                    dve.memset(PF[:], 0.0)
                    dve.memset(onesb[:], 1.0)
                    for e in range(3):
                        ins = dve.memset(B2s[e][:], 0.0)
                    ins.then_inc(ms_v, 1)
                    dve.wait_ge(watt, 16 * 12)
                    for w in range(2):
                        halves(WAh[w][:], WAl[w][:], raw[:, w * 3 * C:(w + 1) * 3 * C], 2 * w)
                prep_lo(i, i)
            dve.wait_ge(bias_pe, 1)
            bp = bank(0, 16 * HEADS).rearrange("p (j h) -> p h j", h=HEADS)
            for k in range(2):
                cols = slice(16 * k, 16 * k + 16)
                ins = dve.tensor_tensor(BI[:, :, cols], bp, bm0[:, cols].unsqueeze(1).to_broadcast([P, HEADS, 16]), ALU.mult)
            ins.then_inc(bias_v, 1)
            dve.wait_ge(bias_v, 1)
            dve.tensor_tensor(BI[:], BI[:], bm1[:].unsqueeze(1).to_broadcast([P, HEADS, 32]), ALU.add).then_inc(bias_v, 1)
            dve.wait_ge(bias_v, 2)

            gs1, gs2 = HID // FG, C // FG
            dve.wait_ge(wt_pe, 1)
            dve.tensor_copy(w1t[:], bank(1, HID, C)).then_inc(wt_v, 1)
            dve.wait_ge(wt_pe, 2)
            dve.tensor_copy(w2t[:], bank(2, CH * C).rearrange("p (c o) -> p c o", c=CH)).then_inc(wt_v, 1)
            dve.wait_ge(wt_v, 2)
            dve.tensor_reduce(gsum[0:C, 0:FG], w1t[:, 0:FG * gs1].rearrange("p (g n) -> p g n", g=FG), AX.X, ALU.add)
            dve.tensor_reduce(gsum2[:, 0:FG], w2t[:, :, 0:FG * gs2].rearrange("p c (g n) -> p g c n", g=FG), AX.XY, ALU.add)\
               .then_inc(wt_v, 1)
            dve.memset(W1B[:].bitcast(F32), 0.0)
            dve.memset(W2B[:], 0.0).then_inc(wt_v, 1)
            dve.wait_ge(wt_pe, 3)
            dve.tensor_scalar(gmean[:, 0:FG], bank(3, FG), 1.0 / (gs1 * C), None, ALU.mult)
            dve.tensor_scalar(gmean[:, 8:8 + FG], bank(4, FG), 1.0 / (gs2 * HID), None, ALU.mult).then_inc(wt_v, 1)
            dve.wait_ge(wt_v, 5)
            s2 = sg2[:].rearrange("p (c o) -> p c o", c=CH)
            for g in range(FG):
                c1, c2 = slice(g * gs1, (g + 1) * gs1), slice(g * gs2, (g + 1) * gs2)
                dve.tensor_scalar(sg[0:C, c1], w1t[:, c1], gmean[0:C, g:g + 1], None, ALU.is_lt)
                ins = dve.tensor_scalar(s2[:, :, c2], w2t[:, :, c2], gmean[:, 8 + g:9 + g], None, ALU.is_lt)
            ins.then_inc(wt_v, 1)
            dve.wait_ge(wt_v, 6)
            for g in range(FG):
                c1, c2 = slice(g * gs1, (g + 1) * gs1), slice(g * gs2, (g + 1) * gs2)
                dve.scalar_tensor_tensor(W1B[:, c1], w1t[:, c1], gmean[0:C, g:g + 1], sg[0:C, c1], ALU.is_gt, ALU.subtract)
                ins = dve.scalar_tensor_tensor(W2B[:, :, c2], w2t[:, :, c2], gmean[:, 8 + g:9 + g], s2[:, :, c2],
                                               ALU.is_gt, ALU.subtract)
            ins.then_inc(wt_v, 1)

            def expert_weights(i):
                if i == 0:
                    dve.wait_ge(wmoe, 16 * 12)
                dve.wait_ge(wm_s, 32 * (i + 1))
                halves(M1h[i][:], M1l[i][:], raw[:], 4 + 4 * i)
                halves(GWh[i][:], GWl[i][:], GWr[i][:], 6 + 4 * i)

            def expert_bias(i):
                after(dve, split_b, 4 * i)
                dve.tensor_copy(b2a, B2r[i]).then_inc(split_m, 1)
                dve.wait_ge(split_m, i + 1)
                dve.tensor_tensor(b2b, B2r[i], b2a, ALU.subtract).then_inc(split_b, 1)
                dve.wait_ge(split_b, 4 * i + 1)
                dve.tensor_copy(b2c, b2b).then_inc(split_b, 1)
                dve.wait_ge(split_b, 4 * i + 2)
                dve.tensor_tensor(b2d, b2b, b2c, ALU.subtract).then_inc(split_b, 1)
                dve.tensor_copy(B2s[i][0:1, :], b2a[0:1, :])
                dve.tensor_copy(B2s[i][32:33, :], b2c[32:33, :])
                dve.wait_ge(split_b, 4 * i + 3)
                dve.tensor_copy(B2s[i][64:65, :], b2d[64:65, :]).then_inc(split_b, 1)

            attention(0, 0, (xin, 64))
            if stop < 1:
                return
            expert_weights(0)
            for i in range(3):
                expert_bias(i)

            dve.wait_ge(xu[0], GROUPS)

            def x6(q):
                return X[:, q * FT * C:(q + 1) * FT * C].rearrange("p (t c) -> p t c", t=FT)

            for q in range(-3, FG):
                if 0 <= q + 1 < FG:
                    for j in range(6):
                        dve.wait_ge(y1_a, 6 * (q + 1) + j + 1)
                        ins = dve.tensor_reduce(am[:, 0, j:j + 1], Y1[(q + 1) % 2][:, j // 2, (j % 2) * 3 * P:(j % 2 + 1) * 3 * P],
                                                AX.X, ALU.max, apply_absolute_value=True)
                    ins.then_inc(ab_v, 1)
                    dve.wait_ge(ab_v, q + 2)
                    dve.tensor_reduce(am1[:, 0:1], am[:, 0, :], AX.X, ALU.max).then_inc(gm1_v, 1)
                if q + 3 < FG:
                    for t in range(FT):
                        ins = dve.bn_stats(stats[:, t, :], x6(q + 3)[:, t, :])
                    ins.then_inc(fst_v, 1)
                if q >= 0:
                    after(dve, xu[1], q)
                    for u in range(2):
                        dve.wait_ge(fd_pe, 2 * q + u + 1)
                        dve.tensor_tensor(Y2[:, 3 * u:3 * u + 3, :], bank(3 + u, 3 * C).rearrange("p (t c) -> p t c", t=3),
                                          b2bc[:].unsqueeze(1).to_broadcast([P, 3, C]), ALU.add).then_inc(y2_v, 1)
                if 0 <= q + 1 < FG:
                    dve.wait_ge(g1_pe, 2 * (q + 1) + 1)
                    dve.tensor_reduce(gmx[:, 0:1], PS[0:1, 7, 0:P], AX.X, ALU.max).then_inc(gm1_v, 1)
                if q >= 0:
                    dve.wait_ge(y2_v, 3 * q + 2)
                    dve.tensor_reduce(am1[:, 1:2], Y2[:], AX.XY, ALU.max, apply_absolute_value=True).then_inc(gm2_v, 1)
                if q + 3 < FG:
                    dve.wait_ge(frs_p, q + 4)
                    after(dve, ft_pe, q + 3)
                    for t in range(FT):
                        ins = dve.tensor_scalar(XN[:, t, :], x6(q + 3)[:, t, :], mean[:, t:t + 1], rs[:, t:t + 1],
                                                ALU.subtract, ALU.mult)
                    ins.then_inc(fxn_v, 1)
                if 0 <= q + 1 < FG:
                    dve.wait_ge(g1_pe, 2 * (q + 1) + 2)
                    dve.tensor_scalar(qe[:, 0:1], PS[:, 7, P:P + 1], QEPS, None, ALU.add).then_inc(qs1_v, 1)
                if q >= 0:
                    dve.wait_ge(g2_pe, 2 * q + 1)
                    dve.tensor_reduce(gmx[:, 1:2], PS[0:1, 7, 256:256 + P], AX.X, ALU.max).then_inc(gm2_v, 1)
                if 0 <= q + 1 < FG:
                    dve.wait_ge(qs1_v, 3 * (q + 1) + 1)
                    dve.reciprocal(qr[:, 0:1], qe[:, 0:1])
                    dve.tensor_scalar(ql[:, 0, 0:1], qe[:, 0:1], QCLIP / QB, None, ALU.mult)
                    dve.tensor_scalar(ql[:, 0, 1:2], qe[:, 0:1], -QCLIP / QB, None, ALU.mult).then_inc(qs1_v, 1)
                    dve.wait_ge(qs1_v, 3 * (q + 1) + 2)
                    after(dve, ge_a, 3 * (q + 1))
                    dve.tensor_scalar(qs[:, 0:1], qr[:, 0:1], QB, None, ALU.mult).then_inc(qs1_v, 1)
                    for c in range(CH):
                        y = Y1[(q + 1) % 2][:, c, :]
                        dve.tensor_scalar(y, y, ql[:, 0, 0:1], ql[:, 0, 1:2], ALU.min, ALU.max).then_inc(cl_v, 1)
                if 0 <= q + 2 < FG or q == -2:
                    dve.wait_ge(fh_a, q + 3)
                    dve.tensor_tensor(FL[:].rearrange("p (u n) -> p u n", u=2), PS[0:C, 5:7, 0:3 * P],
                                      FH[:].bitcast(F32).rearrange("p (u n) -> p u n", u=2), ALU.subtract).then_inc(fl_v, 1)
                if q >= 0:
                    dve.wait_ge(g2_pe, 2 * q + 2)
                    dve.tensor_scalar(qe[:, 1:2], PS[:, 7, 384:385], QEPS, None, ALU.add).then_inc(qs2_v, 1)
                    dve.wait_ge(qs2_v, 3 * q + 1)
                    dve.reciprocal(qr[:, 1:2], qe[:, 1:2])
                    dve.tensor_scalar(ql[:, 1, 0:1], qe[:, 1:2], QCLIP / QB, None, ALU.mult)
                    dve.tensor_scalar(ql[:, 1, 1:2], qe[:, 1:2], -QCLIP / QB, None, ALU.mult).then_inc(qs2_v, 1)
                    dve.wait_ge(qs2_v, 3 * q + 2)
                    dve.tensor_scalar(qs[:, 1:2], qr[:, 1:2], QB, None, ALU.mult).then_inc(qs2_v, 1)
                    dve.tensor_scalar(Y2[:], Y2[:], ql[:, 1, 0:1], ql[:, 1, 1:2], ALU.min, ALU.max).then_inc(y2_v, 1)
                    dve.wait_ge(qs2_v, 3 * q + 3)
                    dve.wait_ge(y2_v, 3 * q + 3)
                    dve.scalar_tensor_tensor(x6(q), Y2[:], qs[:, 1:2], x6(q), ALU.mult, ALU.add).then_inc(xu[1], 1)
            if stop < 2:
                return

            for i in range(2):
                prep_stats(8 + i, i, (xu[1], FG), None)
                prep_norm(8 + i, i)
                prep_lo(8 + i, i)
            attention(2, 1, (xu[1], FG))
            if stop < 3:
                return

            def gating_head(b, m):
                sc = bank(6, GT * EXP).rearrange("p (t e) -> p t e", t=GT)
                dve.wait_ge(xt_used, m + 1)
                dve.tensor_reduce(smx[:], sc, AX.X, ALU.max).then_inc(gate_v, 1)
                dve.wait_ge(gate_v, NGV * b + 1)
                dve.tensor_tensor(dl[:], sc, smx[:].unsqueeze(2).to_broadcast([P, GT, EXP]), ALU.subtract).then_inc(gate_v, 1)

            def gating_tail(b):
                exr = ex[:].unsqueeze(3).to_broadcast([P, GT, EXP, EXP])
                exc = ex[:].unsqueeze(2).to_broadcast([P, GT, EXP, EXP])
                dve.wait_ge(gexp_p, b + 1)
                dve.tensor_tensor(cg[:], exc, exr, ALU.is_gt)
                dve.tensor_tensor(ce[:], exc, exr, ALU.is_ge)
                dve.tensor_reduce(s0[:], ex[:], AX.X, ALU.add).then_inc(gate_v, 1)
                dve.wait_ge(gate_v, NGV * b + 3)
                dve.tensor_tensor(cg[:], cg[:], tie[:, 0, :, :].unsqueeze(1).to_broadcast([P, GT, EXP, EXP]), ALU.mult)
                dve.tensor_tensor(ce[:], ce[:], tie[:, 1, :, :].unsqueeze(1).to_broadcast([P, GT, EXP, EXP]), ALU.mult)\
                   .then_inc(gate_v, 1)
                dve.wait_ge(gate_v, NGV * b + 4)
                dve.tensor_tensor(cg[:], cg[:], ce[:], ALU.add).then_inc(gate_v, 1)
                dve.wait_ge(gate_v, NGV * b + 5)
                dve.tensor_reduce(rk[:], cg[:], AX.X, ALU.add).then_inc(gate_v, 1)
                dve.wait_ge(gate_v, NGV * b + 6)
                dve.scalar_tensor_tensor(me[:], rk[:], 2.0, ex[:], ALU.is_lt, ALU.mult).then_inc(gate_v, 1)
                dve.wait_ge(gate_v, NGV * b + 7)
                dve.tensor_reduce(s1[:], me[:], AX.X, ALU.add).then_inc(gate_v, 1)
                dve.wait_ge(gate_v, NGV * b + 8)
                dve.scalar_tensor_tensor(s1[:], s0[:], 1e-9, s1[:], ALU.mult, ALU.add).then_inc(gate_v, 1)
                dve.wait_ge(gate_v, NGV * b + 9)
                dve.reciprocal(s0[:], s1[:]).then_inc(gate_v, 1)
                dve.wait_ge(gate_v, NGV * b + 10)
                dve.tensor_tensor(G[:], me[:], s0[:].unsqueeze(2).to_broadcast([P, GT, EXP]), ALU.mult).then_inc(gate_v, 1)
                dve.wait_ge(gate_v, NGV * b + 11)

            def combine(b, g, t, upd):
                dve.wait_ge(dn_pe, 4 * b + t + 1)
                for e in range(EXP):
                    if e > 0:
                        dve.wait_ge(part_v, 3 * (4 * b + t) + e)
                    ins = dve.scalar_tensor_tensor(xt(g, t), bank(4 + t % 2)[:, e * C:(e + 1) * C], G[:, t, e:e + 1],
                                                   xt(g, t), ALU.mult, ALU.add)
                    if e < EXP - 1:
                        ins.then_inc(part_v, 1)
                ins.then_inc(comb_v if t < GT - 1 else upd, 1)

            def moe(phase, k, e, pool_next=False):
                def body(g, p):
                    b, m = 8 * e + g, 8 * k + g
                    prep = has(g, 2, 2, PREPS[phase])
                    if has(g, 0):
                        gating_head(b, m)
                    if prep:
                        prep_stats(m + 2, g + 2, xu[phase - 1], xu[phase])
                    if has(g, 0):
                        gating_tail(b)
                    if prep:
                        prep_norm(m + 2, g + 2)
                    if has(g, 0):
                        for t in range(2):
                            combine(b, g, t, xu[phase])
                    if prep:
                        prep_lo(m + 2, p, g + 2 - GROUPS if pool_next and isinstance(g, int) and g + 2 >= GROUPS else None)
                    if has(g, 0):
                        for t in range(2, 4):
                            combine(b, g, t, xu[phase])
                    if phase == 3 and isinstance(g, int) and g in (-1, 0):
                        expert_weights(g + 2)
                    if phase == 3 and isinstance(g, int) and g == 0:
                        mixer_weights()
                moe_walk(dve, body)

            def mixer_weights():
                dve.wait_ge(wfft, 16 * NWFFT)
                for i in range(2):
                    halves(PWh[i][:], PWl[i][:], PWr[i][:], 16 + 3 * i)
                    dve.tensor_scalar(BW[i][:, :, 2, :], BW[i][:, :, 1, :], -1.0, None, ALU.mult).then_inc(split_v, 1)

            moe(3, 2, 0)
            if stop < 4:
                return

            def mix_h(kc, g):
                s = 8 * kc + g + 1
                dve.wait_ge(sq_a, s + 1)
                after(dve, dft_pe, 4 * s)
                dve.tensor_scalar(HH, SQ, SBc[kc][:, 0:1], SBc[kc][:, 1:2], ALU.mult, ALU.add).then_inc(h_v, 1)

            def mix_x(kc, g, upd):
                dve.wait_ge(id_pe, 8 * kc + g + 1)
                dve.tensor_tensor(xg(g), xg(g), bank(IB[kc], GT * C), ALU.add).then_inc(upd, 1)

            def mixer2(g, p):
                m = 24 + g
                prep = has(g, 2, 2, PREPS[4])
                if prep:
                    prep_stats(m + 2, g + 2, xu[3], xu[4])
                if has(g, 1):
                    mix_h(0, g)
                if prep:
                    prep_norm(m + 2, g + 2)
                if has(g, 0):
                    after(dve, pp_pe, 2 * g)
                    for j in range(4):
                        c, r = j // 2, j % 2
                        dve.wait_ge(z_a, 4 * g + j + 1)
                        dve.tensor_scalar(CL[:, c, r, :], Z[:, c, r, :], LAMBDA, -LAMBDA, ALU.min, ALU.max).then_inc(c_v, 1)
                        dve.wait_ge(c_v, 4 * g + j + 1)
                        dve.wait_ge(zx_p, 4 * g + j + 1)
                        dve.tensor_tensor(OU[:, c, :, r * FR:(r + 1) * FR], ZX[:, c, r, :].rearrange("p (i f) -> p i f", i=2),
                                          CL[:, c, r, :].rearrange("p (i f) -> p i f", i=2), ALU.subtract).then_inc(o_v, 1)
                if prep:
                    prep_lo(m + 2, p)
                if has(g, 0):
                    mix_x(0, g, xu[4])
            mixer_walk(dve, mixer2)
            if stop < 5:
                return
            moe(5, 4, 1, pool_next=True)
            if stop < 6:
                return

            def routing(i):
                dve.wait_ge(rt_a, 2 * i + 2)
                dve.tensor_scalar(hh[:], hq[:], msb[:, 0:1], msb[:, 1:2], ALU.mult, ALU.add).then_inc(rt_v, 1)
                dve.wait_ge(f2_pe, i + 1)
                L = TB[:, 16:16 + 4 * NF].rearrange("p (f c i) -> p f c i", f=NF, c=2)
                dve.tensor_reduce(lmx[:], L.rearrange("p f c i -> p c i f"), AX.X, ALU.max).then_inc(rt_v, 1)
                dve.wait_ge(rt_v, 5 * i + 2)
                dve.tensor_tensor(lg[:], L, lmx[:].unsqueeze(1).to_broadcast([C, NF, 2, 2]), ALU.subtract).then_inc(rt_v, 1)
                dve.wait_ge(le_a, i + 1)
                dve.tensor_reduce(lsum[:], le[:].rearrange("p f c i -> p c i f"), AX.X, ALU.add).then_inc(rt_v, 1)
                dve.wait_ge(rt_v, 5 * i + 4)
                dve.reciprocal(lrc[:], lsum[:]).then_inc(rt_v, 1)
                dve.wait_ge(rt_v, 5 * i + 5)
                after(dve, rt_pe, i)
                dve.tensor_tensor(RTm[:].rearrange("p c i f -> p f c i"), le[:],
                                  lrc[:].unsqueeze(1).to_broadcast([C, NF, 2, 2]), ALU.mult).then_inc(rt_m, 1)

            def routing_out(i, p):
                dve.wait_ge(rt_pe, i + 1)
                after(dve, w_pe, 4 * (i - 1))
                dve.tensor_copy(RT[p][:].rearrange("p q c -> p (q c)"), TB[0:NF, 128:128 + 4 * C]).then_inc(rt_x, 1)

            for i in range(2):
                routing(i)
                routing_out(i, i)

            def mixer3(g, p):
                m = 40 + g
                prep = has(g, 2, 2, PREPS[6])
                if prep:
                    prep_stats(m + 2, g + 2, xu[5], xu[6])
                if has(g, 1):
                    mix_h(1, g)
                if prep:
                    prep_norm(m + 2, g + 2)
                if has(g, 0):
                    for j in range(4):
                        c, i = j // 2, j % 2
                        W = bank(j, 3 * FR, C).rearrange("p (r f) -> p r f", r=3)
                        dve.wait_ge(w_pe, 4 * g + j + 1)
                        dve.wait_ge(xf_a, 32 + 4 * g + j + 1)
                        after(dve, y_p, 4 * g)
                        dve.tensor_tensor(MA[:, j, :, :], XF[p][:, c, :, i, :], W[:, 0:1, :].to_broadcast([C, 2, FR]), ALU.mult)\
                           .then_inc(prod_v, 1)
                        dve.tensor_tensor(MB[:, j, 0, :], XF[p][:, c, 1, i, :], W[:, 1, :], ALU.mult).then_inc(prod_v, 1)
                        dve.tensor_tensor(MB[:, j, 1, :], XF[p][:, c, 0, i, :], W[:, 2, :], ALU.mult).then_inc(prod_v, 1)
                if prep:
                    prep_lo(m + 2, p, g + 2 if has(g, 2, 2) else None)
                if has(g, 2, 2):
                    routing(g + 2)
                if has(g, 0):
                    mix_x(1, g, xu[6])
                if has(g, 2, 2):
                    routing_out(g + 2, p)
            mixer_walk(dve, mixer3)
            if stop < 7:
                return
            moe(7, 6, 2)

        @block.tensor
        def _(pe):
            def three(o, wh, wl, xh, xl):
                pe.matmul(o, wh, xh, start=True, stop=False)
                pe.matmul(o, wh, xl, start=False, stop=False)
                return pe.matmul(o, wl, xh, start=False, stop=True)

            def prep_turn(m, windows=False, extra=None):
                pe.wait_ge(xn_v, m + 1)
                after(pe, lo_v, m)
                if extra:
                    after(pe, *extra)
                for t in range(GT):
                    o = TB[:, t * P:(t + 1) * P]
                    if windows:
                        o = o.rearrange("p (h r c) -> p r h c", h=2, r=8)
                    ins = pe.transpose(o, XN[:, t, :], ident[:])
                ins.then_inc(tp_pe, 1)

            def attention(phase, ka):
                wh, wl = WAh[ka], WAl[ka]

                def body(g, p):
                    n, m = 8 * ka + g, 8 * ka + g
                    more = has(g, 1)
                    if has(g, 0):
                        pe.wait_ge(exp_a, n + 1)
                        pe.wait_ge(v_v, n + 1)
                        pe.wait_ge(q_a, n + 2 if more else n + 1)
                        pe.wait_ge(k_a, n + 2 if more else n + 1)
                        for h in range(HEADS):
                            for t in range(GT):
                                ins = pe.transpose(PS[:, h, t * P:(t + 1) * P], PF[:, h, t, :], ident[:])
                            ins.then_inc(ptp_pe, 1)
                    if more:
                        pe.wait_ge(q_a, n + 2)
                        pe.wait_ge(k_a, n + 2)
                        for t in range(GT):
                            for h in range(HEADS):
                                rows, ts = slice(h * DH, (h + 1) * DH), slice(t * P, (t + 1) * P)
                                ins = pe.matmul(PS[:, 3 + h, ts], qT[rows, ts], kT[rows, ts], start=True, stop=True)
                        ins.then_inc(s_pe, 1)
                    if has(g, 0):
                        pe.wait_ge(pt_a, 2 * n + 2)
                        pe.wait_ge(pt_v, n + 1)
                        after(pe, xu[phase], g)
                        for t in range(GT):
                            for h in range(HEADS):
                                c = (t * HEADS + h) * (DH + 1)
                                ins = pe.matmul(PS[:, 6, c:c + DH + 1], PT[:, h, t * P:(t + 1) * P], V[:, t, h, :],
                                                start=True, stop=True)
                        ins.then_inc(pv_pe, 1)
                    if has(g, 2):
                        xh, xl = XH[p], XL[p]
                        pe.wait_ge(lo_v, m + 3)
                        three(bank(0, 512, C), wh[:, 0:C], wl[:, 0:C], xh[:], xl[:]).then_inc(q_pe, 1)
                        three(bank(1, 512, C), wh[:, C:2 * C], wl[:, C:2 * C], xh[:], xl[:]).then_inc(k_pe, 1)
                    if has(g, 0):
                        pe.wait_ge(nrm_v, n + 1)
                        for t in range(GT):
                            o = PS[0:C, 6, t * P:(t + 1) * P]
                            if ka == 1:
                                o = o.rearrange("p (r h c) -> p h r c", h=2, r=8)
                            ins = pe.transpose(o, O[:, t, :], ident[:])
                        ins.then_inc(ot_pe, 1)
                    if more:
                        xh, xl = XH[1 - p], XL[1 - p]
                        for t in range(GT):
                            ts = slice(t * P, (t + 1) * P)
                            ins = three(PS[:, 2, t * C:(t + 1) * C], xh[:, ts], xl[:, ts], wh[:, 2 * C:], wl[:, 2 * C:])
                        ins.then_inc(xt_used, 1)
                    if has(g, 3, 2, PREPS[phase]):
                        prep_turn(m + 3, ka == 1 and has(g, 3))
                    if has(g, 0):
                        pe.wait_ge(ot_a, n + 1)
                        for t in range(GT):
                            ins = pe.matmul(PS[:, 6, t * C:(t + 1) * C], OT[:, t * P:(t + 1) * P], WM[ka][:],
                                            start=True, stop=True)
                        ins.then_inc(wo_pe, 1)
                attention_walk(pe, body)

            pe.wait_ge(watt, 16 * 12)
            prep_turn(0)
            for j in range(16):
                ins = pe.matmul(PS[:, 0, j * HEADS:(j + 1) * HEADS], EH[:, j, :], rel[:], start=True, stop=True)
            ins.then_inc(bias_pe, 1)
            prep_turn(1)
            pe.wait_ge(wffn, 16 * 4)
            for c in range(CH):
                ins = pe.transpose(PS[0:C, 1, c * P:(c + 1) * P], w1raw[:, c, :], ident[:])
            ins.then_inc(wt_pe, 1)
            for c in range(CH):
                ins = pe.transpose(PS[:, 2, c * C:(c + 1) * C], w2raw[:, c * P:(c + 1) * P], ident[0:C, 0:C])
            ins.then_inc(wt_pe, 1)
            pe.wait_ge(wt_v, 3)
            pe.wait_ge(ms_v, 3)
            pe.matmul(PS[:, 3, 0:FG], onesf[0:C, :], gsum[0:C, 0:FG], start=True, stop=True)
            pe.matmul(PS[:, 4, 0:FG], onesf[:], gsum2[:, 0:FG], start=True, stop=True).then_inc(wt_pe, 1)
            pe.wait_ge(split_v, 4)
            pe.wait_ge(bias_v, 2)
            pe.wait_ge(wt_v, 5)
            pe.wait_ge(ms_v, 4)
            attention(0, 0)
            if stop < 1:
                return

            pe.wait_ge(wt_v, 7)
            pe.wait_ge(xu[0], GROUPS)
            for q in range(-2, FG):
                if 0 <= q + 1 < FG:
                    pe.wait_ge(fl_v, q + 2)
                    for j in range(6):
                        c, u = j // 2, j % 2
                        after(pe, y1_a, 6 * (q + 1) + j - 2)
                        w, us = W1B[:, c * P:(c + 1) * P], slice(u * 3 * P, (u + 1) * 3 * P)
                        pe.matmul(bank(j % 3, 3 * P), w, FH[:, us], start=True, stop=False)
                        pe.matmul(bank(j % 3, 3 * P), w, FL[:, us], start=False, stop=True).then_inc(fu_pe, 1)
                if q + 2 < FG:
                    pe.wait_ge(fxn_v, q + 3)
                    after(pe, fl_v, q + 2)
                    for t in range(FT):
                        ins = pe.transpose(PS[0:C, 5 + t // 3, (t % 3) * P:(t % 3 + 1) * P], XN[:, t, :], ident[:])
                    ins.then_inc(ft_pe, 1)
                if q >= 0:
                    pe.wait_ge(ge_a, 3 * q + 3)
                    after(pe, y2_v, 3 * q)
                    for u in range(2):
                        for t in range(3 * u, 3 * u + 3):
                            for c in range(CH):
                                ins = pe.matmul(PS[:, 3 + u, (t % 3) * C:(t % 3 + 1) * C], YH[:, c, t * P:(t + 1) * P],
                                                W2B[:, c, :], start=c == 0, stop=c == CH - 1)
                        ins.then_inc(fd_pe, 1)
                if 0 <= q + 1 < FG:
                    pe.wait_ge(gm1_v, 2 * (q + 1) + 1)
                    after(pe, qs2_v, 3 * (q - 1) + 1)
                    pe.transpose(PS[0:1, 7, 0:P], am1[:, 0:1], ident[:]).then_inc(g1_pe, 1)
                    pe.wait_ge(gm1_v, 2 * (q + 1) + 2)
                    pe.matmul(PS[:, 7, P:P + 1], onesf[0:1, :], gmx[:, 0:1], start=True, stop=True).then_inc(g1_pe, 1)
                if q >= 0:
                    pe.wait_ge(gm2_v, 2 * q + 1)
                    after(pe, qs1_v, 3 * min(q + 1, FG - 1) + 1)
                    pe.transpose(PS[0:1, 7, 256:256 + P], am1[:, 1:2], ident[:]).then_inc(g2_pe, 1)
                    pe.wait_ge(gm2_v, 2 * q + 2)
                    pe.matmul(PS[:, 7, 384:385], onesf[0:1, :], gmx[:, 1:2], start=True, stop=True).then_inc(g2_pe, 1)
            if stop < 2:
                return
            pe.wait_ge(xu[1], FG)
            prep_turn(8, True)
            prep_turn(9, True)
            attention(2, 1)
            if stop < 3:
                return

            def moe(phase, k, e):
                def up(b, p, lo, hi):
                    for c in range(lo, hi):
                        after(pe, gelu_a, CK * b + c - 3)
                        cs = slice(c * P, (c + 1) * P)
                        three(bank(c % 4), M1h[e][:, cs], M1l[e][:, cs], XH[p][:], XL[p][:]).then_inc(up_pe, 1)

                def gate(b, p):
                    after(pe, gate_v, NGV * b - NGV + 2)
                    for t in range(GT):
                        ts = slice(t * P, (t + 1) * P)
                        ins = three(PS[:, 6, t * EXP:(t + 1) * EXP], XH[p][:, ts], XL[p][:, ts], GWh[e][:], GWl[e][:])
                    ins.then_inc(xt_used, 1)

                def down(b, g, p, t):
                    Y = bank(4 + t % 2, EXP * C)
                    if t == 0:
                        pe.wait_ge(gelu_a, CK * b + CK)
                    if t == 1:
                        after(pe, xu[phase], g)
                    else:
                        after(pe, comb_v, 3 * b + t // 2 + t % 2)
                    pe.matmul(Y, onesb[:], B2s[e][:], start=True, stop=False)
                    for x in range(EXP):
                        for c in range(CH):
                            j = x * CH + c
                            ins = pe.matmul(Y[:, x * C:(x + 1) * C], H[p][:, j, t * P:(t + 1) * P], M2[e][:, j, :],
                                            start=False, stop=j == CK - 1)
                    ins.then_inc(dn_pe, 1)

                def body(g, p):
                    b, m = 8 * e + g, 8 * k + g
                    if has(g, 1):
                        pe.wait_ge(lo_v, m + 2)
                    for t in range(GT):
                        if has(g, 1):
                            up(b + 1, 1 - p, 3 * t, 3 * t + 3)
                        if has(g, 0):
                            down(b, g, p, t)
                        if t == 1 and has(g, 2, 2, PREPS[phase]):
                            prep_turn(m + 2)
                    if has(g, 1):
                        gate(b + 1, 1 - p)
                pe.wait_ge(xu[phase - 1], GROUPS)
                moe_walk(pe, body)

            pe.wait_ge(split_v, 8)
            pe.wait_ge(split_b, 12)
            moe(3, 2, 0)
            if stop < 4:
                return

            def mix_h(kc, k, g, p):
                m = 8 * k + g
                pe.wait_ge(lo_v, m + 2)
                for t in range(GT):
                    ts = slice(t * P, (t + 1) * P)
                    ins = three(PS[:, 4 + t // 2, (t % 2) * MED:(t % 2 + 1) * MED], XH[1 - p][0:C, ts], XL[1 - p][0:C, ts],
                                PWh[kc][:], PWl[kc][:])
                    if t == 1:
                        ins.then_inc(h_pe, 1)
                ins.then_inc(xt_used, 1)

            def mix_dft(kc, g):
                s = 8 * kc + g + 1
                pe.wait_ge(h_v, s + 1)
                for j in range(4):
                    c, i = j // 2, j % 2
                    if kc == 0 and j == 3:
                        after(pe, z_a, 4 * g + 1)
                    if kc == 1 and j == 3:
                        after(pe, prod_v, 12 * g + 3)
                    for kk in range(2):
                        ins = pe.matmul(bank(DB[kc][j], 2 * FR, C), HH[:, 2 * i + kk, c * C:(c + 1) * C], FDFT[:, kk, :],
                                        start=kk == 0, stop=kk == 1)
                    ins.then_inc(dft_pe, 1)

            def mix_channels(kc, g):
                for i in range(2):
                    for n in range(3):
                        for c in range(2):
                            ins = pe.matmul(PS[0:C, PB[kc] + i, n * C:(n + 1) * C], OU[:, c, i, n * C:(n + 1) * C],
                                            PO[kc][:, c, :], start=c == 0, stop=c == 1)
                    ins.then_inc(pp_pe, 1)

            def mix_tokens(kc, g):
                s = 8 * kc + g
                for i in range(2):
                    pe.wait_ge(ps_a, 2 * s + i + 1)
                    for kk in range(2):
                        t = 2 * i + kk
                        for n in range(3):
                            ins = pe.matmul(PS[:, IB[kc], t * C:(t + 1) * C], GDFT[:, n, kk * P:(kk + 1) * P],
                                            PSs[:, i, n * C:(n + 1) * C], start=n == 0, stop=n == 2)
                ins.then_inc(id_pe, 1)

            def block_mlp(w, src, banks, done):
                for j in range(4):
                    c, r = j // 2, j % 2
                    o = bank(banks[j], 2 * FR, C)
                    pe.matmul(o, BW[w][:, c, 0, :], src(c, r), start=True, stop=False)
                    pe.matmul(o, BW[w][:, c, 2 if r == 0 else 1, :], src(c, 1 - r), start=False, stop=True).then_inc(done, 1)

            def mixer2(g, p):
                if has(g, 0):
                    pe.wait_ge(xf_a, 4 * g + 4)
                    after(pe, xu[4], g)
                    block_mlp(0, lambda c, r: XF[p][:, c, r, :, :].rearrange("p i f -> p (i f)"), (0, 1, 2, 3), m1_pe)
                if has(g, 1):
                    mix_h(0, 3, g, p)
                if has(g, 0):
                    pe.wait_ge(o1_a, 4 * g + 4)
                    block_mlp(1, lambda c, r: O1[:, c, r, :], (6, 0, 1, 2), m2_pe)
                if has(g, 1):
                    mix_dft(0, g)
                if has(g, 2, 2, PREPS[4]):
                    prep_turn(24 + g + 2)
                if has(g, 0):
                    pe.wait_ge(o_v, 4 * g + 4)
                    mix_channels(0, g)
                    mix_tokens(0, g)
            pe.wait_ge(xu[3], GROUPS)
            pe.wait_ge(split_v, 22)
            mixer_walk(pe, mixer2)
            if stop < 5:
                return
            moe(5, 4, 1)
            if stop < 6:
                return

            pe.wait_ge(xu[5], GROUPS)
            cwv = cwx[:].rearrange("p (f r) -> p f r", r=2)
            for j in range(3):
                pe.matmul(bank(j, FR, NF), cwv[:, :, min(j, 1)], RB[:], start=True, stop=True).then_inc(cw_pe, 1)

            def route_in(i, p):
                pe.wait_ge(pool_v, i + 1)
                pe.matmul(TB[0:24, 0:2], fc1[:], pl[:, p, :], start=True, stop=True).then_inc(f1_pe, 1)

            def route_logits(i):
                pe.wait_ge(rt_v, 5 * i + 1)
                for f in range(NF):
                    for c in range(2):
                        n = 16 + (f * 2 + c) * 2
                        w = f * MED + c * C
                        ins = pe.matmul(TB[:, n:n + 2], fc2[:, w:w + C], hh[:], start=True, stop=True)
                ins.then_inc(f2_pe, 1)

            def route_turn(i):
                pe.wait_ge(rt_m, i + 1)
                for q in range(4):
                    ins = pe.transpose(TB[0:NF, 128 + q * C:128 + (q + 1) * C], RTm[:, q // 2, q % 2, :], ident[0:C, 0:C])
                ins.then_inc(rt_pe, 1)

            for i in range(2):
                after(pe, rt_x, i)
                route_in(i, i)
                route_logits(i)
                route_turn(i)
            pe.wait_ge(cw_a, 3)

            def mixer3(g, p):
                if has(g, 0):
                    pe.wait_ge(rt_x, g + 1)
                    after(pe, ps_a, 16 + 2 * g)
                    after(pe, xu[6], g)
                    pe.wait_ge(xf_a, 32 + 4 * g + 4)
                    for j in range(4):
                        pe.matmul(bank(j, 3 * FR, C), RT[p][:, j, :], CW[:], start=True, stop=True).then_inc(w_pe, 1)
                if has(g, 1):
                    mix_h(1, 5, g, p)
                if has(g, 2, 2, PREPS[6]):
                    prep_turn(40 + g + 2, False, (rt_x, g + 2 if has(g, 2, 2, 8) else GROUPS))
                if has(g, 1):
                    mix_dft(1, g)
                if has(g, 2, 2):
                    route_in(g + 2, p)
                if has(g, 0):
                    pe.wait_ge(y_p, 4 * g + 4)
                    mix_channels(1, g)
                if has(g, 2, 2):
                    route_logits(g + 2)
                if has(g, 0):
                    mix_tokens(1, g)
                if has(g, 2, 2):
                    route_turn(g + 2)
            mixer_walk(pe, mixer3)
            if stop < 7:
                return
            moe(7, 6, 2)


def shape_constants():
    k = {"k_ident": np.eye(P)}
    i = np.arange(P)
    col = np.arange(32)
    same = ((i[:, None] % 32) // 16 == col[None, :] // 16).astype(np.float64)
    k["k_bm0"], k["k_bm1"] = same, (same - 1) * BIG
    e = np.arange(EXP)
    tie = np.stack([e[None, :] > e[:, None], e[None, :] < e[:, None]])
    k["k_tie"] = np.broadcast_to(tie[None], (P, 2, EXP, EXP))
    c = np.stack(np.meshgrid(np.arange(4), np.arange(4), indexing="ij")).reshape(2, -1)
    d = (c[:, :, None] - c[:, None, :] + 3).transpose(1, 2, 0)
    idx = d[..., 0] * 7 + d[..., 1]
    k["k_onehot"] = (idx[i % 16][None].transpose(0, 2, 1) == np.arange(49)[:, None, None])
    h, w = np.divmod(np.arange(HW * HW), HW)
    ky, kx = np.divmod(np.arange(FR), WF)
    th = 2 * np.pi * ((h[:, None] * ky[None] + w[:, None] * kx[None]) % HW) / HW
    fwd = np.concatenate([np.cos(th), -np.sin(th)], 1) / HW
    k["k_dft"] = fwd.reshape(2, P, 2 * FR).transpose(1, 0, 2)
    twice = np.where((kx == 0) | (kx == HW // 2), 1.0, 2.0)[:, None]
    inv = np.concatenate([np.cos(th).T * twice, -np.sin(th).T * twice]) / HW
    k["k_idft"] = inv.reshape(3, C, HW * HW).transpose(1, 0, 2)

    def cubic(old, new):
        A, m = -0.75, np.zeros((new, old))
        pos = np.arange(new, dtype=np.float32) * np.float32((old - 1) / (new - 1))
        i0 = np.floor(pos).astype(int)
        fr = (pos - i0.astype(np.float32)).astype(np.float64)
        for o in (-1, 0, 1, 2):
            t = np.abs(fr - o)
            w1 = ((A + 2) * t - (A + 3)) * t * t + 1
            w2 = A * (((t - 5) * t + 8) * t - 4)
            wt = np.where(t <= 1, w1, np.where(t < 2, w2, 0))
            for n in range(new):
                m[n, np.clip(i0[n] + o, 0, old - 1)] += wt[n]
        return m
    k["k_bicubic"] = np.kron(cubic(14, HW), cubic(8, WF)).T
    return {n: np.ascontiguousarray(v, dtype=np.float32) for n, v in k.items()}


def kernel(**inputs):
    import concourse.bacc as bacc
    from concourse.bass_utils import run_bass_kernel_spmd

    nc = bacc.Bacc("TRN2", target_bir_lowering=False, num_devices=1)
    arrays = {n: np.ascontiguousarray(v) for n, v in inputs.items()}
    arrays["x"] = arrays["x"].reshape(TOK, C)
    arrays.update(shape_constants())
    aps = {n: nc.dram_tensor(n, v.shape, mybir.dt.from_np(v.dtype), kind="ExternalInput").ap() for n, v in arrays.items()}
    out = nc.dram_tensor("out", (TOK, C), F32, kind="ExternalOutput").ap()
    program(nc, aps, out)
    r = run_bass_kernel_spmd(nc, [arrays], core_ids=[0])
    return r.results[0]["out"].reshape(IMGS, HW, HW, C)
```

```python
import numpy as np

import concourse.bass as bass
from concourse import mybir
from contextlib import ExitStack

F32 = mybir.dt.float32
F32R = mybir.dt.float32r
ALU = mybir.AluOpType
ACT = mybir.ActivationFunctionType
AX = mybir.AxisListType

P = 128
IMGS, HW, C = 16, 16, 96
TOK = IMGS * HW * HW
TILES = TOK // P
GT = 4
GROUPS = TILES // GT
GTOK = GT * P
HEADS, DH = 3, 32
QSCALE = DH ** -0.5
HID, EXP = 384, 4
CH = HID // P
CK = EXP * CH
MED = 192
WF = HW // 2 + 1
FR = HW * WF
NF = 4
BIG = 1e30
LAMBDA = 0.01
QB, QEPS = 128.0, 1e-5
QCLIP = float(np.float32(QB - QEPS))
FT = 6
FG = 5
EULER = float(np.e)
EPS_C, EPS_T = 1e-6, 1e-5


def ds(start, n):
    return bass.ds(start, n)


def program(nc, a, out):
    ctx = ExitStack()
    with ctx:
        def sb(name, shape, dt=F32):
            return ctx.enter_context(nc.sbuf_tensor(name, shape, dt))

        def sem(name):
            return ctx.enter_context(nc.semaphore(name))

        PS = ctx.enter_context(nc.psum_tensor("PS", [P, 8, 512], F32))

        def bank(i, n=512, rows=P):
            return PS[0:rows, i, 0:n]

        TB = bank(7, 512, C)

        X = sb("X", [P, TILES * C])
        ident = sb("ident", [P, P])
        stats = sb("stats", [P, FT, 6])
        msum = sb("msum", [P, FT])
        mdif = sb("mdif", [P, FT])
        m2 = sb("m2", [P, FT])
        mean = sb("mean", [P, FT])
        ve = sb("ve", [P, FT])
        rs = sb("rs", [P, FT])
        half = sb("half", [P, 8])
        quarter = sb("quarter", [P, 8])
        euler = sb("euler", [P, GT * EXP])
        XN = sb("XN", [P, GT, C])
        XH = [sb(f"XH{i}", [P, GTOK], F32R) for i in range(2)]
        XL = [sb(f"XL{i}", [P, GTOK], F32R) for i in range(2)]
        raw = sb("raw", [P, EXP * HID])
        onesf = sb("onesf", [P, P])

        WAh = [sb(f"WAh{i}", [P, 3 * C], F32R) for i in range(2)]
        WAl = [sb(f"WAl{i}", [P, 3 * C], F32R) for i in range(2)]
        WM = [sb(f"WM{i}", [C + 1, C]) for i in range(2)]
        rel = sb("rel", [49, HEADS])
        BI = sb("BI", [P, HEADS, 32])
        bm0 = sb("bm0", [P, 32])
        bm1 = sb("bm1", [P, 32])
        qT = sb("qT", [P, GTOK])
        V = sb("V", [P, GT, C])
        SC = sb("SC", [P, HEADS, GT, 64])
        mx = sb("mx", [P, HEADS * GT])
        PF = sb("PF", [P, HEADS, GT, P])
        PT = sb("PT", [P, HEADS, GTOK])
        sm = sb("sm", [P, HEADS * GT])
        rc = sb("rc", [P, HEADS * GT])
        OT = sb("OT", [C + 1, GTOK])

        w1raw = sb("w1raw", [P, CH, C])
        w2raw = sb("w2raw", [C, HID])
        W1B = sb("W1B", [P, HID], F32R)
        w1t = sb("w1t", [C, HID])
        W2B = sb("W2B", [P, CH, C])
        w2t = sb("w2t", [P, CH, C])
        gsum = sb("gsum", [P, 8])
        gsum2 = sb("gsum2", [P, 8])
        sg2 = sb("sg2", [P, CH * C])
        gmean = sb("gmean", [P, 16])
        sg = sb("sg", [P, HID])
        b1c = sb("b1c", [P, CH])
        b2bc = sb("b2bc", [P, C])
        FH = sb("FH", [P, FT * P], F32R)
        FL = sb("FL", [P, FT * P], F32R)
        am = sb("am", [P, 2, 6])
        am1 = sb("am1", [P, 2])
        gmx = sb("gmx", [1, 2])
        qe = sb("qe", [P, 2])
        qr = sb("qr", [P, 2])
        qs = sb("qs", [P, 2])
        ql = sb("ql", [P, 2, 2])
        Y2 = sb("Y2", [P, FT, C])

        M1h = [sb(f"M1h{i}", [P, EXP * HID], F32R) for i in range(3)]
        M1l = [sb(f"M1l{i}", [P, EXP * HID], F32R) for i in range(3)]
        M2 = [sb(f"M2_{i}", [P, CK, C]) for i in range(3)]
        GWr = [sb(f"GWr{i}", [P, EXP]) for i in range(3)]
        GW = [sb(f"GW{i}", [P, 2 * EXP], F32R) for i in range(3)]
        gs = sb("gs", [P, GT, 2 * EXP])
        B2 = [sb(f"B2_{i}", [P, EXP, C]) for i in range(3)]
        GB = PF[:].rearrange("p h t j -> p (h t j)")[:, 0:GT * EXP * C].rearrange("p (t e c) -> p t e c", t=GT, e=EXP)
        H = [sb(f"H{i}", [P, CK, GTOK]) for i in range(2)]
        tie = sb("tie", [P, 2, EXP, EXP])
        smx = sb("smx", [P, GT])
        dl = sb("dl", [P, GT, EXP])
        ex = sb("ex", [P, GT, EXP])
        cg = sb("cg", [P, GT, EXP, EXP])
        ce = sb("ce", [P, GT, EXP, EXP])
        rk = sb("rk", [P, GT, EXP])
        me = sb("me", [P, GT, EXP])
        s1 = sb("s1", [P, GT])
        s0 = sb("s0", [P, GT])
        G = sb("G", [P, GT, EXP])

        FDFT = sb("FDFT", [P, 2, 2 * FR])
        GDFT = sb("GDFT", [P, 3, HW * HW])
        PWr = [sb(f"PWr{i}", [C, w]) for i, w in enumerate((2 * P, MED))]
        PWh = [sb(f"PWh{i}", [C, w], F32R) for i, w in enumerate((2 * P, MED))]
        PWl = [sb(f"PWl{i}", [C, w], F32R) for i, w in enumerate((2 * P, MED))]
        PO = [sb(f"PO{i}", [P, 2, C]) for i in range(2)]
        SBc = [sb(f"SBc{i}", [P, 2]) for i in range(2)]
        BL, BK, BR = 8, 24, 32
        BW = [sb(f"BW{i}", [P, BL // 2, P]) for i in range(2)]
        BB = [sb(f"BB{i}", [P, BL // 2]) for i in range(2)]
        hflat = [H[i][:, :, :].rearrange("p a b -> p (a b)") for i in range(2)]
        WID = (2 * P, MED)
        R, HH = ([hflat[0][:, o:o + GT * w].rearrange("p (t m) -> p t m", t=GT) for w in WID] for o in (0, 1024))
        XP = [hflat[0][:, o:o + 1152].rearrange("p (q i f) -> p q i f", q=4, i=2) for o in (2048, 3200)]
        O1 = hflat[0][:, 4352:4352 + 1152].rearrange("p (q n) -> p q n", q=4)
        Z = hflat[1][:, 4608:4608 + 1152].rearrange("p (q n) -> p q n", q=4)
        CL = hflat[1][:, 0:1152].rearrange("p (q n) -> p q n", q=4)
        ZX = hflat[1][:, 1152:2304].rearrange("p (q n) -> p q n", q=4)
        XF = [hflat[0][0:C, o:o + 1152].rearrange("p (c r i f) -> p c r i f", c=2, r=2, i=2) for o in (2048, 3200)]
        OU = hflat[1][:, 2304:2304 + 1152].rearrange("p (c i n) -> p c i n", c=2, i=2)
        PSs = hflat[1][:, 3456:3456 + 576].rearrange("p (i n) -> p i n", i=2)
        PA = [hflat[1][:, o:o + HEADS * GTOK].rearrange("p (h t) -> p h t", h=HEADS) for o in (3072, 4608)]
        kT = hflat[0][:, 4608:4608 + HEADS * GTOK].rearrange("p (h t) -> p h t", h=HEADS)
        Y1 = [hflat[1][:, o:o + CH * FT * P].rearrange("p (c n) -> p c n", c=CH) for o in (0, CH * FT * P)]
        FX = hflat[0][:, CH * FT * P:CH * FT * P + FT * C].rearrange("p (t c) -> p t c", t=FT)
        FT_BANKS = (slice(0, 2), slice(5, 7))
        YH = hflat[0][:, 0:CH * FT * P].rearrange("p (c n) -> p c n", c=CH)
        EH = hflat[0][0:49, 0:16 * P].rearrange("p (j n) -> p j n", j=16)
        cwx = sb("cwx", [112, 2 * NF])
        RB = sb("RB", [112, FR])
        CW = sb("CW", [NF, 3 * FR])
        CWS = sb("CWS", [P, 3 * FR], F32R)
        fc1 = sb("fc1", [C, 24])
        fc2 = sb("fc2", [24, NF * MED])
        msb = sb("msb", [24, 2])
        pl = sb("pl", [C, 2, 2])
        hr = sb("hr", [24, 2])
        hq = sb("hq", [24, 2])
        hh = sb("hh", [24, 2])
        lmx = sb("lmx", [C, 2, 2])
        lg = sb("lg", [C, NF, 2, 2])
        le = sb("le", [C, NF, 2, 2])
        lsum = sb("lsum", [C, 2, 2])
        lrc = sb("lrc", [C, 2, 2])
        RTm = sb("RTm", [C, 2, 2, NF])
        RT = [sb(f"RT{i}", [P, 4, C], F32R) for i in range(2)]
        MA = hflat[1][0:C, 0:1152].rearrange("p (q r n) -> p q r n", q=4, r=2)
        MB = hflat[1][0:C, 1152:2304].rearrange("p (q r n) -> p q r n", q=4, r=2)

        xin, x_first, watt, wffn, wmoe, wfft = (sem(n) for n in ("xin", "x_first", "watt", "wffn", "wmoe", "wfft"))
        ms_p, ms_v, ones_v, split_v = (sem(n) for n in ("ms_p", "ms_v", "ones_v", "split_v"))
        bias_pe, bias_v = sem("bias_pe"), sem("bias_v")
        wt_pe, wt_v, wm_s = sem("wt_pe"), sem("wt_v"), sem("wm_s")
        st_v, ag_p, xn_p = (sem(n) for n in ("st_v", "ag_p", "xn_p"))
        tp_pe, hi_a, lo_v, xt_used = (sem(n) for n in ("tp_pe", "hi_a", "lo_v", "xt_used"))
        xu = [sem(f"x_updated{i}") for i in range(8)]
        q_pe, k_pe, q_a, k_a, v_a, s_pe, sc_r, sc_a, mx_v, sub_v, exp_a = (
            sem(n) for n in ("q_pe", "k_pe", "q_a", "k_a", "v_a", "s_pe", "sc_r", "sc_a", "mx_v", "sub_v", "exp_a"))
        ptp_pe, pt_a, pt_v, tr_v, pv_pe, sum_v, rcp_v, nrm_v, ot_a, wo_pe = (
            sem(n) for n in ("ptp_pe", "pt_a", "pt_v", "tr_v", "pv_pe", "sum_v", "rcp_v", "nrm_v", "ot_a", "wo_pe"))
        ft_pe, fh_a, fl_v, fu_pe, y1_a, ab_v, gm1_v, gm2_v, g1_pe, g2_pe = (
            sem(n) for n in ("ft_pe", "fh_a", "fl_v", "fu_pe", "y1_a", "ab_v", "gm1_v", "gm2_v", "g1_pe", "g2_pe"))
        qs1_v, qs2_v = sem("qs1_v"), sem("qs2_v")
        fst_v, fag_p, fxn_p = (sem(n) for n in ("fst_v", "fag_p", "fxn_p"))
        cl_v, ge_a, fd_pe, y2_v = (sem(n) for n in ("cl_v", "ge_a", "fd_pe", "y2_v"))
        up_pe, gelu_a, dn_pe, gate_v, gexp_p, comb_v = (
            sem(n) for n in ("up_pe", "gelu_a", "dn_pe", "gate_v", "gexp_p", "comb_v"))
        part_v = sem("part_v")
        h_pe, r_a, sq_a, h_v, dft_pe, xf_a, m1_pe, o1_a, m2_pe, z_a = (
            sem(n) for n in ("h_pe", "r_a", "sq_a", "h_v", "dft_pe", "xf_a", "m1_pe", "o1_a", "m2_pe", "z_a"))
        c_v, zx_p, o_v, pp_pe, ps_a, id_pe = (sem(n) for n in ("c_v", "zx_p", "o_v", "pp_pe", "ps_a", "id_pe"))
        cw_pe, cw_a, w_pe, prod_v, y_p, pool_v, f1_pe, rt_a, rt_v, f2_pe, rt_pe, rt_x, le_a = (
            sem(n) for n in ("cw_pe", "cw_a", "w_pe", "prod_v", "y_p", "pool_v", "f1_pe", "rt_a", "rt_v", "f2_pe",
                             "rt_pe", "rt_x", "le_a"))
        cw_v, rt_h, sq_v = sem("cw_v"), sem("rt_h"), sem("sq_v")
        stored, rt_m, gb_p, pad_v = (sem(n) for n in ("stored", "rt_m", "gb_p", "pad_v"))

        block = ctx.enter_context(nc.Block())

        EW, MW = (4, 14, 18), 8
        NGV = 13
        NWFFT = 4 + 2 + 4 + 5 + 2 * (8 + 4) + 5
        BY_IMAGE = (0, 2, 1, 3)
        DB, PB, IB = ((3, 5, 4, 6), (6, 5, 4, 0)), ((0, 1), (2, 1)), (2, 3)

        def xt(g, t):
            return X[:, ds(g * (GT * C) + t * C, C)]

        def xg(g):
            return X[:, ds(g * (GT * C), GT * C)]

        def walk(eng, body, first, lo, hi, last):
            for g in range(first, lo):
                body(g, g % 2)
            with eng.Fori(0, (hi + 1 - lo) // 2) as pair:
                body(2 * pair + lo, lo % 2)
                body(2 * pair + (lo + 1), 1 - lo % 2)
            for g in range(hi + 1, last + 1):
                body(g, g % 2)

        def has(g, n, least=0, most=GROUPS - 1):
            return not isinstance(g, int) or least <= g + n <= most

        def after(eng, s, value):
            if not (isinstance(value, int) and value <= 0):
                eng.wait_ge(s, value)

        def attention_walk(eng, body):
            walk(eng, body, -2, 1, 4, GROUPS - 1)

        def moe_walk(eng, body):
            walk(eng, body, -1, 1, 4, GROUPS - 1)

        def mixer_walk(eng, body):
            walk(eng, body, -1, 1, 4, GROUPS - 1)

        PREPS = {0: 7, 2: 9, 3: 9, 4: 9, 5: 9, 6: 9, 7: 7}
        EPS = {0: EPS_C, 2: EPS_C, 3: EPS_T, 4: EPS_C, 5: EPS_T, 6: EPS_C, 7: EPS_T}

        def eps_of(phase, n):
            return EPS[phase + 1] if isinstance(n, int) and n >= GROUPS else EPS[phase]

        @block.sync
        def _(sp):
            with nc.allow_non_contiguous_dma(reason="small weights"):
                n = TILES // 4
                for i in range(4):
                    sp.dma_start(X[:, i * n * C:(i + 1) * n * C].rearrange("p (i c) -> p i c", c=C),
                                 a["x"][i * n * P:(i + 1) * n * P, :].rearrange("(i p) c -> p i c", p=P))\
                      .then_inc(xin if i else x_first, 16)
                sp.dma_start(w1raw[:], a["L0_ffn_W1"].rearrange("(c p) i -> p c i", p=P)).then_inc(wffn, 16)
                sp.dma_start(w2raw[:], a["L0_ffn_W2"]).then_inc(wffn, 16)
                sp.dma_start(b1c[:], a["L0_ffn_b1"].rearrange("(c p) -> p c", p=P)).then_inc(wffn, 16)
                sp.dma_start(b2bc[:], a["L0_ffn_b2"].partition_broadcast(P)).then_inc(wffn, 16)
                for i, nm in enumerate(("L1_ffn", "L2_ffn", "L3_ffn")):
                    sp.wait_ge(split_v, (4, EW[0] + 2, EW[1] + 2)[i])
                    sp.dma_start(raw[0:C, :].rearrange("c (e h) -> c e h", e=EXP),
                                 a[nm + "_w1"].rearrange("e c h -> c e h")).then_inc(wm_s, 16)
                    sp.dma_start(raw[C:C + 1, :], a[nm + "_b1"].rearrange("(a e) h -> a (e h)", a=1)).then_inc(wm_s, 16)
                    if i > 0:
                        continue
                    for x, nx in enumerate(("L1_ffn", "L2_ffn", "L3_ffn")):
                        sp.dma_start(GWr[x][0:C, :], a[nx + "_gate_w"]).then_inc(wmoe, 16)
                        sp.dma_start(GWr[x][C:C + 1, :], a[nx + "_gate_b"].rearrange("(a n) -> a n", a=1)).then_inc(wmoe, 16)
                        sp.dma_start(B2[x][:].rearrange("p e d -> p (e d)"),
                                     a[nx + "_b2"].rearrange("e d -> (e d)").partition_broadcast(P))\
                            .then_inc(wmoe, 16)
                        sp.dma_start(M2[x][:], a[nx + "_w2"].rearrange("e (c p) d -> p (e c) d", p=P)).then_inc(wmoe, 16)
                    sp.dma_start(tie[:], a["k_tie"]).then_inc(wfft, 16)
                    sp.dma_start(FDFT[:], a["k_dft"]).then_inc(wfft, 16)
                    sp.dma_start(GDFT[0:C], a["k_idft"]).then_inc(wfft, 16)
                    sp.dma_start(RB[:], a["k_bicubic"]).then_inc(wfft, 16)
                    sp.wait_ge(ms_p, 5)
                    for l, (w, nc_) in enumerate((("w_pw1", "L2_conv"), ("pwconv1_w", "L3_conv"))):
                        w2 = a["L2_conv_w_pw2" if l == 0 else "L3_conv_pwconv2_w"]
                        if l == 0:
                            sp.dma_start(PWr[l][:].rearrange("i (b k) -> i b k", b=BL)[:, :, 0:BK],
                                         a[f"{nc_}_{w}"].rearrange("i (b k) -> i b k", b=BL)).then_inc(wfft, 16)
                            for b in range(4):
                                sp.dma_start(PO[l][b * BR:b * BR + BK, :, :],
                                             w2.rearrange("(c b k) o -> b k c o", c=2, b=4)[b]).then_inc(wfft, 16)
                        else:
                            sp.dma_start(PWr[l][:], a[f"{nc_}_{w}"]).then_inc(wfft, 16)
                            sp.dma_start(PO[l][0:C], w2.rearrange("(k p) c -> p k c", p=C)).then_inc(wfft, 16)
                        sc, bi = ("star_scale", "star_bias") if l == 0 else ("act1_scale", "act1_bias")
                        sp.dma_start(SBc[l][:, 0:1], a[f"{nc_}_{sc}"].partition_broadcast(P)).then_inc(wfft, 16)
                        sp.dma_start(SBc[l][:, 1:2], a[f"{nc_}_{bi}"].partition_broadcast(P)).then_inc(wfft, 16)
                    for l in range(2):
                        w, b = a[f"L2_conv_w{l + 1}"], a[f"L2_conv_b{l + 1}"]
                        for k in range(2):
                            for r in range(2):
                                for o in range(2):
                                    rows, cols = (slice(64 * x + BR * k, 64 * x + BR * k + BK) for x in (r, o))
                                    sp.dma_start(BW[l][rows, :, cols],
                                                 w[int(r != o)].rearrange("(q k) i o -> k i q o", k=2)[k]).then_inc(wfft, 16)
                                sp.dma_start(BB[l][64 * r + BR * k:64 * r + BR * k + BK, :],
                                             b[r].rearrange("(q k) i -> k i q", k=2)[k]).then_inc(wfft, 16)
                    sp.dma_start(cwx[:], a["L3_conv_complex_weights"].rearrange("h w f r -> (h w) (f r)")).then_inc(wfft, 16)
                    sp.dma_start(fc1[:], a["L3_conv_fc1_w"]).then_inc(wfft, 16)
                    sp.dma_start(fc2[:], a["L3_conv_fc2_w"]).then_inc(wfft, 16)
                    sp.dma_start(msb[:, 0:1], a["L3_conv_mlp_scale"].partition_broadcast(24)).then_inc(wfft, 16)
                    sp.dma_start(msb[:, 1:2], a["L3_conv_mlp_bias"].partition_broadcast(24)).then_inc(wfft, 16)
            for g in range(GROUPS):
                sp.wait_ge(xu[7], g + 1)
                sp.dma_start(out[g * GTOK:(g + 1) * GTOK, :].rearrange("(i p) c -> p i c", p=P),
                             X[:, g * GT * C:(g + 1) * GT * C].rearrange("p (i c) -> p i c", c=C)).then_inc(stored, 16)
            sp.wait_ge(stored, 16 * GROUPS)

        @block.gpsimd
        def _(pool):
            pool.memset(half[:], -0.5).then_inc(ms_p, 1)
            pool.memset(euler[:], EULER).then_inc(ms_p, 1)
            pool.memset(quarter[:], 0.25).then_inc(ms_p, 1)
            pool.wait_ge(ms_p, 3)

            def normalise(m, eps, n, have, part, x, xn, turned, done):
                def rows(v):
                    return v[:, 0:n].unsqueeze(2).to_broadcast([P, n, C])
                x = x.rearrange("p (t c) -> p t c", t=n)
                pool.wait_ge(have, m + 1)
                pool.tensor_tensor(msum[:, 0:n], stats[:, 0:n, 1], stats[:, 0:n, 4], ALU.add)
                pool.tensor_tensor(mdif[:, 0:n], stats[:, 0:n, 1], stats[:, 0:n, 4], ALU.subtract)
                pool.tensor_tensor(m2[:, 0:n], stats[:, 0:n, 2], stats[:, 0:n, 5], ALU.add).then_inc(part, 1)
                pool.wait_ge(part, 6 * m + 1)
                pool.tensor_tensor(mdif[:, 0:n], mdif[:, 0:n], mdif[:, 0:n], ALU.mult)
                pool.tensor_scalar(mean[:, 0:n], msum[:, 0:n], 0.5, None, ALU.mult)
                pool.tensor_scalar(m2[:, 0:n], m2[:, 0:n], 1.0 / C, eps, ALU.mult, ALU.add).then_inc(part, 1)
                pool.wait_ge(part, 6 * m + 2)
                pool.tensor_tensor(ve[:, 0:n], mdif[:, 0:n], quarter[:, 0:n], ALU.mult).then_inc(part, 1)
                after(pool, turned, m)
                pool.tensor_tensor(xn, x, rows(mean), ALU.subtract).then_inc(part, 1)
                pool.wait_ge(part, 6 * m + 3)
                pool.tensor_tensor(ve[:, 0:n], ve[:, 0:n], m2[:, 0:n], ALU.add).then_inc(part, 1)
                pool.wait_ge(part, 6 * m + 5)
                pool.tensor_tensor(rs[:, 0:n], ve[:, 0:n], half[:, 0:n], ALU.pow).then_inc(part, 1)
                pool.wait_ge(part, 6 * m + 6)
                pool.tensor_tensor(xn, xn, rows(rs), ALU.mult).then_inc(done, 1)

            def prep(phase, k, n):
                x = xg(n - GROUPS if isinstance(n, int) and n >= GROUPS else n)
                normalise(8 * k + n, eps_of(phase, n), GT, st_v, ag_p, x, XN[:], tp_pe, xn_p)

            def attention(phase, k):
                def body(g, p):
                    if has(g, 3, 2, PREPS[phase]):
                        prep(phase, k, g + 3)
                attention_walk(pool, body)

            def moe(phase, k, e):
                def body(g, p):
                    if has(g, 0):
                        pool.wait_ge(gate_v, NGV * (8 * e + g) + 4)
                        pool.tensor_tensor(ex[:, :, :].rearrange("p t e -> p (t e)"), euler[:],
                                           dl[:, :, :].rearrange("p t e -> p (t e)"), ALU.pow).then_inc(gexp_p, 1)
                    if has(g, 2, 2, PREPS[phase]):
                        prep(phase, k, g + 2)
                    if has(g, 0):
                        b, n = 8 * e + g, 3 * (8 * e + g)
                        pool.wait_ge(gate_v, NGV * b + NGV)
                        pool.tensor_tensor(GB, G[:].unsqueeze(3).to_broadcast([P, GT, EXP, C]),
                                           B2[e][:].unsqueeze(1).to_broadcast([P, GT, EXP, C]), ALU.mult).then_inc(gb_p, 1)
                        pool.wait_ge(gb_p, n + 1)
                        pool.tensor_tensor(GB[:, :, 0:2, :], GB[:, :, 0:2, :], GB[:, :, 2:4, :], ALU.add).then_inc(gb_p, 1)
                        pool.wait_ge(gb_p, n + 2)
                        pool.tensor_tensor(GB[:, :, 0, :], GB[:, :, 0, :], GB[:, :, 1, :], ALU.add).then_inc(gb_p, 1)
                        pool.wait_ge(gb_p, n + 3)
                        pool.wait_ge(comb_v, 4 * b + 4)
                        x = xg(g).rearrange("p (t c) -> p t c", t=GT)
                        pool.tensor_tensor(x, x, GB[:, :, 0, :], ALU.add).then_inc(xu[phase], 1)
                moe_walk(pool, body)

            def mixer2(g, p):
                if has(g, 0):
                    for j in range(4):
                        pool.wait_ge(z_a, 4 * g + j + 1)
                        after(pool, o_v, 4 * g)
                        pool.tensor_tensor(ZX[:, j, :], Z[:, j, :], XP[p][:, j, :, :].rearrange("p i f -> p (i f)"), ALU.add)\
                            .then_inc(zx_p, 1)
                if has(g, 3, 2, PREPS[4]):
                    prep(4, 3, g + 3)

            def mixer3(g, p):
                if has(g, 0):
                    for n, j in enumerate(BY_IMAGE):
                        pool.wait_ge(prod_v, 3 * (4 * g + n) + 3)
                        pool.wait_ge(pp_pe, 16 + 2 * g)
                        pool.tensor_tensor(OU[0:C, j // 2, j % 2, :], MA[:, j, :, :].rearrange("p r n -> p (r n)"),
                                           MB[:, j, :, :].rearrange("p r n -> p (r n)"), ALU.add).then_inc(y_p, 1)
                if has(g, 3, 2, PREPS[6]):
                    prep(6, 5, g + 3)

            prep(0, 0, 0)
            prep(0, 0, 1)
            for i in range(2):
                ins = pool.memset(PA[i], 0.0)
            ins.then_inc(ms_p, 1)
            for i in range(2):
                pool.memset(BW[i][:], 0.0)
                pool.memset(BB[i][:], 0.0)
            pool.memset(PO[0][:], 0.0)
            pool.memset(PWr[0][:], 0.0).then_inc(ms_p, 1)
            pool.memset(PF[:], 0.0).then_inc(ms_p, 1)
            attention(0, 0)
            for q in range(FG):
                normalise(q, EPS_T, FT, fst_v, fag_p, X[:, q * FT * C:(q + 1) * FT * C], FX, ft_pe, fxn_p)
            prep(2, 1, 0)
            prep(2, 1, 1)
            attention(2, 1)
            pool.wait_ge(wmoe, 16 * 12)
            moe(3, 2, 0)
            mixer_walk(pool, mixer2)
            moe(5, 4, 1)
            mixer_walk(pool, mixer3)
            moe(7, 6, 2)

        @block.scalar
        def _(act):
            with nc.allow_non_contiguous_dma(reason="small weights"):
                act.dma_start(ident[:], a["k_ident"]).then_inc(watt, 16)
                act.dma_start(raw[0:C, 0:3 * C], a["L0_conv_Wqkv"]).then_inc(watt, 16)
                act.wait_ge(ms_v, 1)
                act.dma_start(raw[C:C + 1, 0:3 * C], a["L0_conv_bqkv"].rearrange("(a n) -> a n", a=1)).then_inc(watt, 16)
                act.dma_start(EH, a["k_onehot"]).then_inc(watt, 16)
                act.dma_start(rel[:], a["L0_conv_rel_table"]).then_inc(watt, 16)
                act.dma_start(bm0[:], a["k_bm0"]).then_inc(watt, 16)
                act.dma_start(bm1[:], a["k_bm1"]).then_inc(watt, 16)
                act.dma_start(raw[0:C, 3 * C:6 * C], a["L1_conv_w_qkv"]).then_inc(watt, 16)
                act.dma_start(WM[0][0:C, :], a["L0_conv_Wm"]).then_inc(watt, 16)
                act.dma_start(WM[0][C:C + 1, :], a["L0_conv_bm"].rearrange("(a n) -> a n", a=1)).then_inc(watt, 16)
                act.dma_start(WM[1][0:C, :], a["L1_conv_w_out"]).then_inc(watt, 16)
                act.dma_start(WM[1][C:C + 1, :], a["L1_conv_b_out"].rearrange("(a n) -> a n", a=1)).then_inc(watt, 16)

            def prep_hi(m, p):
                act.wait_ge(tp_pe, m + 1)
                after(act, xt_used, m - 1)
                act.activation(XH[p][0:C, :], TB, ACT.Copy).then_inc(hi_a, 1)

            def ffn_hi(q):
                act.wait_ge(ft_pe, q + 1)
                act.activation(FH[0:C, :].rearrange("p (u n) -> p u n", u=2), PS[0:C, FT_BANKS[min(q, 1)], 0:3 * P], ACT.Copy)\
                   .then_inc(fh_a, 1)

            def attention(phase, ka):
                bs = 32 if ka == 0 else 64

                def body(g, p):
                    n, m = 8 * ka + g, 8 * ka + g
                    if ka == 0 and isinstance(g, int) and g == GROUPS - 1:
                        ffn_hi(0)
                    if has(g, 1) and ka == 1:
                        act.wait_ge(s_pe, n + 2)
                        after(act, nrm_v, n + 1)
                        rows = slice(0, bs)
                        S = PS[rows, 3:6, :].rearrange("p h (t j) -> p h t j", t=GT)[:, :, :, rows]
                        act.activation(SC[rows, :, :, 0:bs], S, ACT.Copy).then_inc(sc_a, 1)
                    if has(g, 0) and ka == 1:
                        after(act, pv_pe, n)
                        for h in range(2):
                            act.wait_ge(ptp_pe, 3 * g + h + 1)
                            act.activation(PT[:, h, :], bank(h), ACT.Copy).then_inc(pt_a, 1)
                    if has(g, 1) and ka == 1:
                        act.wait_ge(sub_v, n + 2)
                        act.activation(SC[:, :, :, 0:bs], SC[:, :, :, 0:bs], ACT.Exp).then_inc(exp_a, 1)
                    if has(g, 0):
                        act.wait_ge(pv_pe, n + 1)
                        after(act, wo_pe, n)
                        act.activation(OT[0:C, :], bank(6, 512, C), ACT.Copy).then_inc(ot_a, 1)
                    if has(g, 2):
                        act.wait_ge(q_pe, n + 3)
                        after(act, s_pe, n + 2)
                        act.activation(qT[0:C, :], bank(0, 512, C), ACT.Copy, scale=QSCALE).then_inc(q_a, 1)
                        act.wait_ge(k_pe, n + 3)
                        for h in range(HEADS):
                            rows = slice(h * DH, (h + 1) * DH)
                            ins = act.activation(kT[rows, h, :], PS[rows, 1, :], ACT.Copy)
                        ins.then_inc(k_a, 1)
                    if has(g, 1) and ka == 0:
                        act.wait_ge(sub_v, n + 2)
                        act.activation(SC[:, :, :, 0:bs], SC[:, :, :, 0:bs], ACT.Exp).then_inc(exp_a, 1)
                    if has(g, 1):
                        act.wait_ge(xt_used, m + 2)
                        act.activation(V[:].rearrange("p t c -> p (t c)"), bank(2, GT * C), ACT.Copy).then_inc(v_a, 1)
                    if has(g, 3, 2, PREPS[phase]):
                        prep_hi(m + 3, 1 - p)
                attention_walk(act, body)

            prep_hi(0, 0)
            prep_hi(1, 1)
            attention(0, 0)

            for q in range(-1, FG):
                if 0 <= q + 1 < FG:
                    for j in range(6):
                        c, u = j // 2, j % 2
                        act.wait_ge(fu_pe, 6 * (q + 1) + j + 1)
                        after(act, ge_a, 3 * q)
                        act.activation(Y1[(q + 1) % 2][:, c, u * 3 * P:(u + 1) * 3 * P], bank(j % 3, 3 * P), ACT.Identity,
                                       bias=b1c[:, c:c + 1]).then_inc(y1_a, 1)
                if q + 2 < FG:
                    ffn_hi(q + 2)
                if 0 <= q + 1 < FG:
                    for c in range(CH):
                        act.wait_ge(cl_v, 3 * (q + 1) + c + 1)
                        after(act, fd_pe, 2 * (q + 1))
                        act.activation(YH[:, c, :], Y1[(q + 1) % 2][:, c, :], ACT.Gelu, scale=qs[:, 0:1]).then_inc(ge_a, 1)

            prep_hi(8, 0)
            prep_hi(9, 1)
            attention(2, 1)

            def moe(phase, k, e):
                def gelus(b, p, lo, hi):
                    for c in range(lo, hi):
                        act.wait_ge(up_pe, CK * b + c + 1)
                        after(act, dn_pe, 4 * b - 4)
                        act.activation(H[p][:, c, :], bank(c % 4), ACT.Gelu).then_inc(gelu_a, 1)

                def body(g, p):
                    if has(g, 1):
                        gelus(8 * e + g + 1, 1 - p, 0, 9)
                    if has(g, 2, 2, PREPS[phase]):
                        prep_hi(8 * k + g + 2, p)
                    if has(g, 1):
                        gelus(8 * e + g + 1, 1 - p, 9, 12)
                moe_walk(act, body)

            def mix_relu(kc, k, g):
                s = 8 * kc + g + 1
                after(act, h_v, 2 * s)
                act.wait_ge(h_pe, s + 1)
                for i in range(2):
                    if i == 1:
                        act.wait_ge(xt_used, 8 * k + g + 2)
                    ts = slice(2 * i, 2 * i + 2)
                    act.activation(R[kc][:, ts, :], bank(4 + i, 2 * WID[kc]).rearrange("p (t m) -> p t m", t=2), ACT.Relu)\
                       .then_inc(r_a, 1)
                    if kc == 1:
                        act.wait_ge(r_a, 2 * s + i + 1)
                        act.activation(R[kc][:, ts, :], R[kc][:, ts, :], ACT.Square).then_inc(sq_a, 1)

            def mix_spectrum(kc, g, p):
                s = 8 * kc + g + 1
                for n, j in enumerate(BY_IMAGE):
                    c, i = j // 2, j % 2
                    act.wait_ge(dft_pe, 4 * s + n + 1)
                    if kc == 0:
                        after(act, zx_p, 4 * g)
                    else:
                        after(act, prod_v, 12 * g)
                    if kc == 0:
                        for h in range(2):
                            for r in range(2):
                                ins = act.activation(XP[1 - p][64 * r:64 * r + 64, 2 * c + h, i, :],
                                                     PS[64 * h:64 * h + 64, DB[kc][j], r * FR:(r + 1) * FR], ACT.Copy)
                        ins.then_inc(xf_a, 1)
                    else:
                        act.activation(XF[1 - p][:, c, :, i, :],
                                       bank(DB[kc][j], 2 * FR, C).rearrange("p (r f) -> p r f", r=2), ACT.Copy).then_inc(xf_a, 1)

            def mix_out(kc, g):
                s = 8 * kc + g
                for i in range(2):
                    act.wait_ge(pp_pe, 2 * s + i + 1)
                    after(act, id_pe, s)
                    act.activation(PSs[0:C, i, :], bank(PB[kc][i], 3 * C, C), ACT.Copy).then_inc(ps_a, 1)

            def mixer2(g, p):
                if has(g, 0):
                    for j in range(4):
                        act.wait_ge(m1_pe, 4 * g + j + 1)
                        after(act, m2_pe, 4 * g)
                        act.activation(O1[:, j, :], bank(j, 2 * FR), ACT.Relu, bias=BB[0][:, j:j + 1]).then_inc(o1_a, 1)
                if has(g, 1):
                    mix_relu(0, 3, g)
                if has(g, 0):
                    for j in range(4):
                        act.wait_ge(m2_pe, 4 * g + j + 1)
                        after(act, o_v, 4 * g)
                        act.activation(Z[:, j, :], bank((6, 0, 1, 2)[j], 2 * FR), ACT.Identity, bias=BB[1][:, j:j + 1])\
                           .then_inc(z_a, 1)
                if has(g, 1):
                    mix_spectrum(0, g, p)
                if has(g, 2, 2, PREPS[4]):
                    prep_hi(24 + g + 2, p)
                if has(g, 0):
                    mix_out(0, g)

            moe(3, 2, 0)
            mixer_walk(act, mixer2)
            moe(5, 4, 1)

            def routing_relu(i):
                act.wait_ge(f1_pe, i + 1)
                act.activation(hr[:], TB[0:24, 0:2], ACT.Relu, scale=1.0 / (HW * HW)).then_inc(rt_a, 1)
                act.wait_ge(rt_a, 2 * i + 1)
                act.activation(hq[:], hr[:], ACT.Square).then_inc(rt_a, 1)

            def routing_exp(i):
                act.wait_ge(rt_v, 5 * i + 3)
                act.activation(le[:], lg[:], ACT.Exp).then_inc(le_a, 1)

            def routing_hi(i, p):
                act.wait_ge(rt_pe, i + 1)
                after(act, w_pe, 4 * (i - 1))
                for row in (0, 64):
                    ins = act.activation(RT[p][row:row + NF, :, :].rearrange("p q c -> p (q c)"),
                                         TB[0:NF, 128:128 + 4 * C], ACT.Copy)
                ins.then_inc(rt_h, 1)

            for j in range(3):
                act.wait_ge(cw_pe, j + 1)
                act.activation(CW[:, j * FR:(j + 1) * FR], bank(j, FR, NF), ACT.Copy,
                               scale=-1.0 if j == 1 else 1.0).then_inc(cw_a, 1)
            for i in range(2):
                routing_relu(i)
                routing_exp(i)
                routing_hi(i, i)

            def mixer3(g, p):
                if has(g, 1):
                    mix_relu(1, 5, g)
                if has(g, 2, 2, PREPS[6]):
                    prep_hi(40 + g + 2, p)
                if has(g, 1):
                    mix_spectrum(1, g, p)
                if has(g, 2, 2):
                    routing_relu(g + 2)
                if has(g, 0):
                    mix_out(1, g)
                if has(g, 2, 2):
                    routing_exp(g + 2)
                    routing_hi(g + 2, p)
            mixer_walk(act, mixer3)
            moe(7, 6, 2)

        @block.vector
        def _(dve):
            for i in range(3):
                dve.memset(GWr[i][C:P, :], 0.0)
            dve.memset(raw[C:P, :], 0.0).then_inc(ms_v, 1)
            def halves(hi, lo, src, count):
                dve.tensor_copy(hi, src).then_inc(split_v, 1)
                dve.wait_ge(split_v, count + 1)
                dve.tensor_tensor(lo, src, hi.bitcast(F32), ALU.subtract).then_inc(split_v, 1)

            def prep_stats(m, n, prev, this):
                if isinstance(n, int) and n >= GROUPS:
                    dve.wait_ge(this, n - GROUPS + 1)
                    n = n - GROUPS
                elif isinstance(prev, tuple):
                    dve.wait_ge(*prev)
                else:
                    dve.wait_ge(prev, n + 1)
                after(dve, xn_p, m)
                for t in range(GT):
                    ins = dve.bn_stats(stats[:, t, :], xt(n, t))
                ins.then_inc(st_v, 1)

            def prep_lo(m, p, pool=None):
                dve.wait_ge(hi_a, m + 1)
                dve.tensor_tensor(XL[p][0:C, :], TB, XH[p][0:C, :].bitcast(F32), ALU.subtract).then_inc(lo_v, 1)
                if pool is not None:
                    after(dve, f1_pe, pool - 1)
                    dve.tensor_reduce(pl[:, p, :], TB.rearrange("p (i n) -> p i n", i=2), AX.X, ALU.add).then_inc(pool_v, 1)

            def x6(q):
                return X[:, q * FT * C:(q + 1) * FT * C].rearrange("p (t c) -> p t c", t=FT)

            def ffn_stats(q):
                after(dve, fxn_p, q)
                for t in range(FT):
                    ins = dve.bn_stats(stats[:, t, :], x6(q)[:, t, :])
                ins.then_inc(fst_v, 1)

            def ffn_lo(q):
                dve.wait_ge(fh_a, q + 1)
                dve.tensor_tensor(FL[0:C, :].rearrange("p (u n) -> p u n", u=2), PS[0:C, FT_BANKS[min(q, 1)], 0:3 * P],
                                  FH[0:C, :].bitcast(F32).rearrange("p (u n) -> p u n", u=2), ALU.subtract)\
                   .then_inc(fl_v, 1)

            def first_max(q, j):
                dve.wait_ge(y1_a, 6 * q + j + 1)
                dve.tensor_reduce(am[:, 0, j:j + 1], Y1[q % 2][:, j // 2, (j % 2) * 3 * P:(j % 2 + 1) * 3 * P],
                                  AX.X, ALU.max, apply_absolute_value=True).then_inc(ab_v, 1)

            def attention(phase, ka, prev):
                bs = 32 if ka == 0 else 64
                scv = SC[:, :, :, 0:bs].rearrange("p h t j -> p (h t) j")
                upd = xu[phase]

                def body(g, p):
                    n, m = 8 * ka + g, 8 * ka + g
                    prep = has(g, 3, 2, PREPS[phase])
                    if prep:
                        prep_stats(m + 3, g + 3, prev, upd)
                    if has(g, 1) and ka == 0:
                        dve.wait_ge(s_pe, n + 2)
                        after(dve, tr_v, g + 1)
                        for q in range(P // bs):
                            rows = slice(q * bs, (q + 1) * bs)
                            S = PS[rows, 3:6, :].rearrange("p h (t j) -> p h t j", t=GT)[:, :, :, rows]
                            ins = dve.tensor_tensor(SC[rows, :, :, 0:bs], S,
                                                    BI[rows, :, :].unsqueeze(2).to_broadcast([bs, HEADS, GT, bs]), ALU.add)
                        ins.then_inc(sc_r, 1)
                    if has(g, 1) and ka == 1:
                        dve.wait_ge(s_pe, n + 2)
                        after(dve, nrm_v, n + 1)
                        rows = slice(bs, P)
                        S = PS[rows, 3:6, :].rearrange("p h (t j) -> p h t j", t=GT)[:, :, :, rows]
                        dve.tensor_copy(SC[rows, :, :, 0:bs], S).then_inc(sc_r, 1)
                    if has(g, 0) and ka == 1:
                        dve.wait_ge(ptp_pe, 3 * g + 3)
                        after(dve, pv_pe, n)
                        dve.tensor_copy(PT[:, 2, :], bank(2)).then_inc(pt_v, 1)
                    if has(g, 1):
                        dve.wait_ge(sc_r, n + 2)
                        if ka == 1:
                            dve.wait_ge(sc_a, g + 2)
                        dve.tensor_reduce(mx[:], scv, AX.X, ALU.max).then_inc(mx_v, 1)
                        dve.wait_ge(mx_v, n + 2)
                        dve.tensor_tensor(scv, scv, mx[:].unsqueeze(2).to_broadcast([P, HEADS * GT, bs]), ALU.subtract)\
                           .then_inc(sub_v, 1)
                    if has(g, 1):
                        dve.wait_ge(exp_a, n + 2)
                        dve.tensor_reduce(sm[:], scv, AX.X, ALU.add).then_inc(sum_v, 1)
                        dve.wait_ge(sum_v, n + 2)
                        dve.reciprocal(rc[:], sm[:]).then_inc(rcp_v, 1)
                        dve.wait_ge(rcp_v, n + 2)
                        if ka == 1:
                            after(dve, ptp_pe, 3 * g + 3)
                            for q in range(P // bs):
                                rows = slice(q * bs, (q + 1) * bs)
                                ins = dve.tensor_tensor(PF[rows, :, :, rows], SC[rows, :, :, 0:bs],
                                                        rc[rows].rearrange("p (h t) -> p h t", h=HEADS).unsqueeze(3)
                                                        .to_broadcast([bs, HEADS, GT, bs]), ALU.mult)
                            ins.then_inc(nrm_v, 1)
                        else:
                            dve.tensor_tensor(scv, scv, rc[:].unsqueeze(2).to_broadcast([P, HEADS * GT, bs]), ALU.mult)\
                               .then_inc(nrm_v, 1)
                            dve.wait_ge(nrm_v, n + 2)
                            after(dve, pv_pe, g)
                            for q in range(P // bs):
                                rows = slice(q * bs, (q + 1) * bs)
                                ins = dve.transpose(PA[1 - p][rows, :, :].rearrange("p h (t j) -> p (h t) j", t=GT)[:, :, rows],
                                                    scv[rows])
                            ins.then_inc(tr_v, 1)
                    if prep:
                        prep_lo(m + 3, 1 - p)
                    if ka == 0 and isinstance(g, int) and g == GROUPS - 1:
                        for j in range(6):
                            first_max(0, j)
                    if has(g, 0):
                        dve.wait_ge(wo_pe, n + 1)
                        dve.tensor_tensor(xg(g), xg(g), bank(6, GT * C), ALU.add).then_inc(upd, 1)
                    if ka == 0 and isinstance(g, int):
                        if g == 5:
                            dve.wait_ge(xn_p, 8)
                            dve.wait_ge(xu[0], 2)
                            ffn_stats(0)
                        if g == 6:
                            ffn_lo(0)
                            ffn_stats(1)
                            expert_weights(0)
                    if ka == 1 and isinstance(g, int):
                        if g == 7:
                            mixer_weights()
                            expert_weights(1)
                attention_walk(dve, body)

            prep_stats(0, 0, (x_first, 16), None)
            for i in range(2):
                dve.memset(XH[i][C:P, :].bitcast(F32), 0.0)
                dve.memset(XL[i][C:P, :].bitcast(F32), 0.0)
            dve.memset(qT[C:P, :], 0.0)
            dve.memset(OT[C:C + 1, :], 1.0)
            dve.memset(onesf[:], 1.0).then_inc(ms_v, 1)
            dve.wait_ge(ms_v, 2)
            for i in range(2):
                ins = dve.memset(XH[i][C:C + 1, :].bitcast(F32), 1.0)
            ins.then_inc(ones_v, 1)
            prep_stats(1, 1, (x_first, 16), None)
            dve.wait_ge(watt, 16 * 12)
            for w in range(2):
                halves(WAh[w][:], WAl[w][:], raw[:, w * 3 * C:(w + 1) * 3 * C], 2 * w)
            prep_lo(0, 0)
            dve.memset(FH[C:P, :].bitcast(F32), 0.0)
            dve.memset(FL[C:P, :].bitcast(F32), 0.0)
            dve.memset(kT, 0.0).then_inc(ms_v, 1)
            prep_lo(1, 1)
            dve.wait_ge(bias_pe, 1)
            bp = bank(0, 16 * HEADS).rearrange("p (j h) -> p h j", h=HEADS)
            for k in range(2):
                cols = slice(16 * k, 16 * k + 16)
                ins = dve.tensor_tensor(BI[:, :, cols], bp, bm0[:, cols].unsqueeze(1).to_broadcast([P, HEADS, 16]), ALU.mult)
            ins.then_inc(bias_v, 1)
            dve.wait_ge(bias_v, 1)
            dve.tensor_tensor(BI[:], BI[:], bm1[:].unsqueeze(1).to_broadcast([P, HEADS, 32]), ALU.add).then_inc(bias_v, 1)
            dve.wait_ge(bias_v, 2)

            gs1, gs2 = HID // FG, C // FG
            dve.wait_ge(wt_pe, 1)
            dve.tensor_copy(w1t[:], bank(1, HID, C)).then_inc(wt_v, 1)
            dve.wait_ge(wt_pe, 2)
            dve.tensor_copy(w2t[:], bank(2, CH * C).rearrange("p (c o) -> p c o", c=CH)).then_inc(wt_v, 1)
            dve.wait_ge(wt_v, 2)
            dve.tensor_reduce(gsum[0:C, 0:FG], w1t[:, 0:FG * gs1].rearrange("p (g n) -> p g n", g=FG), AX.X, ALU.add)
            dve.tensor_reduce(gsum2[:, 0:FG], w2t[:, :, 0:FG * gs2].rearrange("p c (g n) -> p g c n", g=FG), AX.XY, ALU.add)\
               .then_inc(wt_v, 1)
            dve.memset(W1B[:].bitcast(F32), 0.0)
            dve.memset(W2B[:], 0.0).then_inc(wt_v, 1)
            dve.wait_ge(wt_pe, 3)
            dve.tensor_scalar(gmean[:, 0:FG], bank(3, FG), 1.0 / (gs1 * C), None, ALU.mult)
            dve.tensor_scalar(gmean[:, 8:8 + FG], bank(4, FG), 1.0 / (gs2 * HID), None, ALU.mult).then_inc(wt_v, 1)
            dve.wait_ge(wt_v, 5)
            s2 = sg2[:].rearrange("p (c o) -> p c o", c=CH)
            for g in range(FG):
                c1, c2 = slice(g * gs1, (g + 1) * gs1), slice(g * gs2, (g + 1) * gs2)
                dve.tensor_scalar(sg[0:C, c1], w1t[:, c1], gmean[0:C, g:g + 1], None, ALU.is_lt)
                ins = dve.tensor_scalar(s2[:, :, c2], w2t[:, :, c2], gmean[:, 8 + g:9 + g], None, ALU.is_lt)
            ins.then_inc(wt_v, 1)
            dve.wait_ge(wt_v, 6)
            for g in range(FG):
                c1, c2 = slice(g * gs1, (g + 1) * gs1), slice(g * gs2, (g + 1) * gs2)
                dve.scalar_tensor_tensor(W1B[0:C, c1], w1t[:, c1], gmean[0:C, g:g + 1], sg[0:C, c1], ALU.is_gt, ALU.subtract)
                ins = dve.scalar_tensor_tensor(W2B[:, :, c2], w2t[:, :, c2], gmean[:, 8 + g:9 + g], s2[:, :, c2],
                                               ALU.is_gt, ALU.subtract)
            ins.then_inc(wt_v, 1)

            def expert_weights(i):
                if i == 0:
                    dve.wait_ge(wmoe, 16 * 12)
                dve.wait_ge(wm_s, 32 * (i + 1))
                halves(M1h[i][:], M1l[i][:], raw[:], EW[i])
                halves(GW[i][:, 0:EXP], GW[i][:, EXP:], GWr[i][:], EW[i] + 2)

            def zero_rows(e, buffers):
                dve.wait_ge(dn_pe, 4 * GROUPS * (e + 1))
                for b in buffers:
                    ins = dve.memset(b[C:P], 0.0)
                ins.then_inc(pad_v, 1)

            def mixer_weights():
                dve.memset(PO[1][C:P], 0.0)
                dve.memset(GDFT[C:P], 0.0)
                for i in range(2):
                    dve.memset(RT[i][:].rearrange("p q c -> p (q c)").bitcast(F32), 0.0)
                dve.memset(CWS[:].bitcast(F32), 0.0)
                dve.wait_ge(wfft, 16 * NWFFT)
                for i in range(2):
                    halves(PWh[i][:], PWl[i][:], PWr[i][:], MW + 3 * i)
                    dve.tensor_scalar(BW[i][64:P, :, 0:64], BW[i][64:P, :, 0:64], -1.0, None, ALU.mult).then_inc(split_v, 1)

            dve.wait_ge(ms_p, 4)
            attention(0, 0, (xin, 16 * 3))

            dve.wait_ge(xu[0], GROUPS)
            dve.wait_ge(ms_p, 6)

            def second_scale(r):
                dve.wait_ge(g2_pe, 2 * r + 2)
                dve.tensor_scalar(qe[:, 1:2], PS[:, 7, 384:385], QEPS, None, ALU.add).then_inc(qs2_v, 1)
                dve.wait_ge(qs2_v, 3 * r + 1)
                dve.reciprocal(qr[:, 1:2], qe[:, 1:2])
                dve.tensor_scalar(ql[:, 1, 0:1], qe[:, 1:2], QCLIP / QB, None, ALU.mult)
                dve.tensor_scalar(ql[:, 1, 1:2], qe[:, 1:2], -QCLIP / QB, None, ALU.mult).then_inc(qs2_v, 1)
                dve.wait_ge(qs2_v, 3 * r + 2)
                dve.tensor_scalar(qs[:, 1:2], qr[:, 1:2], QB, None, ALU.mult).then_inc(qs2_v, 1)

            for q in range(-1, FG + 1):
                r, first, output = q - 1, 0 <= q + 1 < FG, 0 <= q < FG
                for j in range(6):
                    if 0 < q + 1 < FG:
                        first_max(q + 1, j)
                    if r >= 0 and j == 2:
                        dve.wait_ge(g2_pe, 2 * r + 1)
                        dve.tensor_reduce(gmx[:, 1:2], PS[0:1, 7, 256:256 + P], AX.X, ALU.max).then_inc(gm2_v, 1)
                    if r >= 0 and j == 4:
                        second_scale(r)
                if first:
                    dve.wait_ge(ab_v, 6 * (q + 2))
                    dve.tensor_reduce(am1[:, 0:1], am[:, 0, :], AX.X, ALU.max).then_inc(gm1_v, 1)
                if r >= 0:
                    dve.tensor_scalar(Y2[:], Y2[:], ql[:, 1, 0:1], ql[:, 1, 1:2], ALU.min, ALU.max).then_inc(y2_v, 1)
                    dve.wait_ge(qs2_v, 3 * r + 3)
                    dve.wait_ge(y2_v, 3 * r + 3)
                    dve.scalar_tensor_tensor(x6(r), Y2[:], qs[:, 1:2], x6(r), ALU.mult, ALU.add).then_inc(xu[1], 1)
                if q + 3 < FG:
                    ffn_stats(q + 3)
                if first:
                    dve.wait_ge(g1_pe, 2 * (q + 1) + 1)
                    dve.tensor_reduce(gmx[:, 0:1], PS[0:1, 7, 0:P], AX.X, ALU.max).then_inc(gm1_v, 1)
                    dve.wait_ge(g1_pe, 2 * (q + 1) + 2)
                    dve.tensor_scalar(qe[:, 0:1], PS[:, 7, P:P + 1], QEPS, None, ALU.add).then_inc(qs1_v, 1)
                    dve.wait_ge(qs1_v, 3 * (q + 1) + 1)
                    dve.reciprocal(qr[:, 0:1], qe[:, 0:1])
                    dve.tensor_scalar(ql[:, 0, 0:1], qe[:, 0:1], QCLIP / QB, None, ALU.mult)
                    dve.tensor_scalar(ql[:, 0, 1:2], qe[:, 0:1], -QCLIP / QB, None, ALU.mult).then_inc(qs1_v, 1)
                    dve.wait_ge(qs1_v, 3 * (q + 1) + 2)
                    after(dve, ge_a, 3 * (q + 1))
                    dve.tensor_scalar(qs[:, 0:1], qr[:, 0:1], QB, None, ALU.mult).then_inc(qs1_v, 1)
                    for c in range(CH):
                        y = Y1[(q + 1) % 2][:, c, :]
                        dve.tensor_scalar(y, y, ql[:, 0, 0:1], ql[:, 0, 1:2], ALU.min, ALU.max).then_inc(cl_v, 1)
                if q + 2 < FG:
                    ffn_lo(q + 2)
                if output:
                    after(dve, xu[1], q)
                    for u in range(2):
                        dve.wait_ge(fd_pe, 2 * q + u + 1)
                        dve.tensor_tensor(Y2[:, 3 * u:3 * u + 3, :], bank(3 + u, 3 * C).rearrange("p (t c) -> p t c", t=3),
                                          b2bc[:].unsqueeze(1).to_broadcast([P, 3, C]), ALU.add).then_inc(y2_v, 1)
                    dve.wait_ge(y2_v, 3 * q + 2)
                    dve.tensor_reduce(am1[:, 1:2], Y2[:], AX.XY, ALU.max, apply_absolute_value=True).then_inc(gm2_v, 1)
                if FG - 2 <= q < FG:
                    dve.wait_ge(fxn_p, FG)
                    prep_stats(8 + q - (FG - 2), q - (FG - 2), (xu[1], 2), None)

            for i in range(2):
                prep_lo(8 + i, i)
            attention(2, 1, (xu[1], FG))

            def gating_head(b, m):
                dve.wait_ge(xt_used, m + 1)
                dve.tensor_copy(gs[:].rearrange("p t e -> p (t e)"), bank(6, GT * 2 * EXP)).then_inc(gate_v, 1)
                dve.wait_ge(gate_v, NGV * b + 1)
                sc = gs[:, :, 0:EXP]
                dve.tensor_tensor(sc, sc, gs[:, :, EXP:], ALU.add).then_inc(gate_v, 1)
                dve.wait_ge(gate_v, NGV * b + 2)
                dve.tensor_reduce(smx[:], sc, AX.X, ALU.max).then_inc(gate_v, 1)
                dve.wait_ge(gate_v, NGV * b + 3)
                dve.tensor_tensor(dl[:], sc, smx[:].unsqueeze(2).to_broadcast([P, GT, EXP]), ALU.subtract).then_inc(gate_v, 1)

            def gating_tail(b):
                exr = ex[:].unsqueeze(3).to_broadcast([P, GT, EXP, EXP])
                exc = ex[:].unsqueeze(2).to_broadcast([P, GT, EXP, EXP])
                dve.wait_ge(gexp_p, b + 1)
                dve.tensor_tensor(cg[:], exc, exr, ALU.is_gt)
                dve.tensor_tensor(ce[:], exc, exr, ALU.is_ge)
                dve.tensor_reduce(s0[:], ex[:], AX.X, ALU.add).then_inc(gate_v, 1)
                dve.wait_ge(gate_v, NGV * b + 5)
                dve.tensor_tensor(cg[:], cg[:], tie[:, 0, :, :].unsqueeze(1).to_broadcast([P, GT, EXP, EXP]), ALU.mult)
                dve.tensor_tensor(ce[:], ce[:], tie[:, 1, :, :].unsqueeze(1).to_broadcast([P, GT, EXP, EXP]), ALU.mult)\
                   .then_inc(gate_v, 1)
                dve.wait_ge(gate_v, NGV * b + 6)
                dve.tensor_tensor(cg[:], cg[:], ce[:], ALU.add).then_inc(gate_v, 1)
                dve.wait_ge(gate_v, NGV * b + 7)
                dve.tensor_reduce(rk[:], cg[:], AX.X, ALU.add).then_inc(gate_v, 1)
                dve.wait_ge(gate_v, NGV * b + 8)
                dve.scalar_tensor_tensor(me[:], rk[:], 2.0, ex[:], ALU.is_lt, ALU.mult).then_inc(gate_v, 1)
                dve.wait_ge(gate_v, NGV * b + 9)
                dve.tensor_reduce(s1[:], me[:], AX.X, ALU.add).then_inc(gate_v, 1)
                dve.wait_ge(gate_v, NGV * b + 10)
                dve.scalar_tensor_tensor(s1[:], s0[:], 1e-9, s1[:], ALU.mult, ALU.add).then_inc(gate_v, 1)
                dve.wait_ge(gate_v, NGV * b + 11)
                dve.reciprocal(s0[:], s1[:]).then_inc(gate_v, 1)
                dve.wait_ge(gate_v, NGV * b + 12)
                dve.tensor_tensor(G[:], me[:], s0[:].unsqueeze(2).to_broadcast([P, GT, EXP]), ALU.mult).then_inc(gate_v, 1)
                dve.wait_ge(gate_v, NGV * b + 13)

            def combine(b, g, t):
                dve.wait_ge(dn_pe, 4 * b + t + 1)
                for e in range(EXP):
                    if e > 0:
                        dve.wait_ge(part_v, 3 * (4 * b + t) + e)
                    ins = dve.scalar_tensor_tensor(xt(g, t), bank(4 + t % 2)[:, e * C:(e + 1) * C], G[:, t, e:e + 1],
                                                   xt(g, t), ALU.mult, ALU.add)
                    if e < EXP - 1:
                        ins.then_inc(part_v, 1)
                ins.then_inc(comb_v, 1)

            def moe(phase, k, e, pool_next=False):
                def body(g, p):
                    b, m = 8 * e + g, 8 * k + g
                    prep = has(g, 2, 2, PREPS[phase])
                    if has(g, 0):
                        gating_head(b, m)
                    if prep:
                        prep_stats(m + 2, g + 2, xu[phase - 1], xu[phase])
                    if has(g, 0):
                        gating_tail(b)
                    if has(g, 0):
                        for t in range(2):
                            combine(b, g, t)
                    if prep:
                        prep_lo(m + 2, p, g + 2 - GROUPS if pool_next and isinstance(g, int) and g + 2 >= GROUPS else None)
                    if has(g, 0):
                        for t in range(2, 4):
                            combine(b, g, t)
                moe_walk(dve, body)

            moe(3, 2, 0)

            def mix_h(kc, g):
                s = 8 * kc + g + 1
                after(dve, dft_pe, 4 * s)
                for i in range(2):
                    ts = slice(2 * i, 2 * i + 2)
                    if kc == 0:
                        dve.wait_ge(r_a, 2 * s + i + 1)
                        dve.tensor_tensor(R[kc][:, ts, :], R[kc][:, ts, :], R[kc][:, ts, :], ALU.mult).then_inc(sq_v, 1)
                        dve.wait_ge(sq_v, 2 * s + i + 1)
                    else:
                        dve.wait_ge(sq_a, 2 * g + 2 + i + 1)
                    dve.tensor_scalar(HH[kc][:, ts, :], R[kc][:, ts, :], SBc[kc][:, 0:1], SBc[kc][:, 1:2], ALU.mult, ALU.add)\
                       .then_inc(h_v, 1)

            def mix_x(kc, g, upd):
                dve.wait_ge(id_pe, 8 * kc + g + 1)
                dve.tensor_tensor(xg(g), xg(g), bank(IB[kc], GT * C), ALU.add).then_inc(upd, 1)

            def mixer2(g, p):
                m = 24 + g
                prep = has(g, 2, 2, PREPS[4])
                if has(g, 1):
                    mix_h(0, g)
                if has(g, 0):
                    after(dve, pp_pe, 2 * g)
                    for j in range(4):
                        c, h = j // 2, j % 2
                        dve.wait_ge(z_a, 4 * g + j + 1)
                        dve.tensor_scalar(CL[:, j, :], Z[:, j, :], LAMBDA, -LAMBDA, ALU.min, ALU.max).then_inc(c_v, 1)
                        dve.wait_ge(c_v, 4 * g + j + 1)
                        dve.wait_ge(zx_p, 4 * g + j + 1)
                        for r in range(2):
                            ins = dve.tensor_tensor(OU[64 * h:64 * h + 64, c, :, r * FR:(r + 1) * FR],
                                                    ZX[64 * r:64 * r + 64, j, :].rearrange("p (i f) -> p i f", i=2),
                                                    CL[64 * r:64 * r + 64, j, :].rearrange("p (i f) -> p i f", i=2), ALU.subtract)
                        ins.then_inc(o_v, 1)
                if prep:
                    prep_lo(m + 2, p)
                if has(g, 3, 2, PREPS[4]):
                    prep_stats(m + 3, g + 3, xu[3], xu[4])
                if has(g, 0):
                    mix_x(0, g, xu[4])
                if isinstance(g, int) and g == 5:
                    expert_weights(2)
            zero_rows(0, [PSs])
            mixer_walk(dve, mixer2)
            moe(5, 4, 1, pool_next=True)

            def routing(i):
                dve.wait_ge(rt_a, 2 * i + 2)
                dve.tensor_scalar(hh[:], hq[:], msb[:, 0:1], msb[:, 1:2], ALU.mult, ALU.add).then_inc(rt_v, 1)
                dve.wait_ge(f2_pe, i + 1)
                L = TB[:, 16:16 + 4 * NF].rearrange("p (f c i) -> p f c i", f=NF, c=2)
                dve.tensor_reduce(lmx[:], L.rearrange("p f c i -> p c i f"), AX.X, ALU.max).then_inc(rt_v, 1)
                dve.wait_ge(rt_v, 5 * i + 2)
                dve.tensor_tensor(lg[:], L, lmx[:].unsqueeze(1).to_broadcast([C, NF, 2, 2]), ALU.subtract).then_inc(rt_v, 1)
                dve.wait_ge(le_a, i + 1)
                dve.tensor_reduce(lsum[:], le[:].rearrange("p f c i -> p c i f"), AX.X, ALU.add).then_inc(rt_v, 1)
                dve.wait_ge(rt_v, 5 * i + 4)
                dve.reciprocal(lrc[:], lsum[:]).then_inc(rt_v, 1)
                dve.wait_ge(rt_v, 5 * i + 5)
                after(dve, rt_pe, i)
                dve.tensor_tensor(RTm[:].rearrange("p c i f -> p f c i"), le[:],
                                  lrc[:].unsqueeze(1).to_broadcast([C, NF, 2, 2]), ALU.mult).then_inc(rt_m, 1)

            def routing_out(i, p):
                dve.wait_ge(rt_h, i + 1)
                dve.tensor_tensor(RT[p][32:32 + NF, :, :].rearrange("p q c -> p (q c)"), TB[0:NF, 128:128 + 4 * C],
                                  RT[p][0:NF, :, :].rearrange("p q c -> p (q c)").bitcast(F32), ALU.subtract).then_inc(rt_x, 1)

            dve.wait_ge(cw_a, 3)
            for row in (0, 32):
                ins = dve.tensor_copy(CWS[row:row + NF, :], CW[:])
            ins.then_inc(cw_v, 1)
            dve.wait_ge(cw_v, 1)
            dve.tensor_tensor(CWS[64:64 + NF, :], CW[:], CWS[0:NF, :].bitcast(F32), ALU.subtract).then_inc(cw_v, 1)
            for i in range(2):
                routing(i)
                routing_out(i, i)

            def mixer3(g, p):
                m = 40 + g
                prep = has(g, 2, 2, PREPS[6])

                def lo_and_sums():
                    prep_lo(m + 2, p, g + 2 if has(g, 2, 2) else None)
                if has(g, 1):
                    mix_h(1, g)
                if has(g, 0):
                    for n, j in enumerate(BY_IMAGE):
                        if n == 2 and prep:
                            lo_and_sums()
                        c, i = j // 2, j % 2
                        W = bank(j, 3 * FR, C).rearrange("p (r f) -> p r f", r=3)
                        dve.wait_ge(w_pe, 4 * g + n + 1)
                        dve.wait_ge(xf_a, 32 + 4 * g + n + 1)
                        after(dve, y_p, 4 * g)
                        dve.tensor_tensor(MA[:, j, :, :], XF[p][:, c, :, i, :], W[:, 0:1, :].to_broadcast([C, 2, FR]), ALU.mult)\
                           .then_inc(prod_v, 1)
                        dve.tensor_tensor(MB[:, j, 0, :], XF[p][:, c, 1, i, :], W[:, 1, :], ALU.mult).then_inc(prod_v, 1)
                        dve.tensor_tensor(MB[:, j, 1, :], XF[p][:, c, 0, i, :], W[:, 2, :], ALU.mult).then_inc(prod_v, 1)
                elif prep:
                    lo_and_sums()
                if has(g, 3, 2, PREPS[6]):
                    prep_stats(m + 3, g + 3, xu[5], xu[6])
                if has(g, 2, 2):
                    routing(g + 2)
                if has(g, 0):
                    mix_x(1, g, xu[6])
                if has(g, 2, 2):
                    routing_out(g + 2, p)
            zero_rows(1, [OU, PSs])
            mixer_walk(dve, mixer3)
            moe(7, 6, 2)

        @block.tensor
        def _(pe):
            def three(o, wh, wl, xh, xl):
                pe.matmul(o, wh, xh, start=True, stop=False)
                pe.matmul(o, wh, xl, start=False, stop=False)
                return pe.matmul(o, wl, xh, start=False, stop=True)

            def prep_turn(m, windows=False, extra=None):
                pe.wait_ge(xn_p, m + 1)
                after(pe, lo_v, m)
                if extra:
                    after(pe, *extra)
                for t in range(GT):
                    o = TB[:, t * P:(t + 1) * P]
                    if windows:
                        o = o.rearrange("p (h r c) -> p r h c", h=2, r=8)
                    ins = pe.transpose(o, XN[:, t, :], ident[:])
                ins.then_inc(tp_pe, 1)

            def weight_sums():
                pe.wait_ge(wt_v, 3)
                pe.matmul(PS[:, 3, 0:FG], onesf[0:C, :], gsum[0:C, 0:FG], start=True, stop=True)
                pe.matmul(PS[:, 4, 0:FG], onesf[:], gsum2[:, 0:FG], start=True, stop=True).then_inc(wt_pe, 1)
                pe.wait_ge(wt_v, 5)

            def ffn_turn(q):
                pe.wait_ge(fxn_p, q + 1)
                after(pe, fl_v, q)
                for t in range(FT):
                    ins = pe.transpose(PS[0:C, FT_BANKS[min(q, 1)].start + t // 3, (t % 3) * P:(t % 3 + 1) * P], FX[:, t, :], ident[:])
                ins.then_inc(ft_pe, 1)

            def ffn_up(q, j):
                c, u = j // 2, j % 2
                if j == 0:
                    pe.wait_ge(fl_v, q + 1)
                after(pe, y1_a, 6 * q + j - 2)
                w, us = W1B[:, c * P:(c + 1) * P], slice(u * 3 * P, (u + 1) * 3 * P)
                pe.matmul(bank(j % 3, 3 * P), w, FH[:, us], start=True, stop=False)
                pe.matmul(bank(j % 3, 3 * P), w, FL[:, us], start=False, stop=True).then_inc(fu_pe, 1)

            def attention(phase, ka):
                wh, wl = WAh[ka], WAl[ka]

                def body(g, p):
                    n, m = 8 * ka + g, 8 * ka + g
                    more = has(g, 1)
                    if ka == 0 and isinstance(g, int) and g == GROUPS - 1:
                        pe.wait_ge(q_a, GROUPS)
                        pe.wait_ge(k_a, GROUPS)
                        ffn_turn(0)
                    if has(g, 0):
                        pe.wait_ge(v_a, n + 1)
                    if more:
                        pe.wait_ge(q_a, n + 2)
                        pe.wait_ge(k_a, n + 2)
                        for t in range(GT):
                            for h in range(HEADS):
                                ts = slice(t * P, (t + 1) * P)
                                ins = pe.matmul(PS[:, 3 + h, ts], qT[:, ts], kT[:, h, ts], start=True, stop=True)
                        ins.then_inc(s_pe, 1)
                    if has(g, 0) and ka == 1:
                        pe.wait_ge(nrm_v, n + 1)
                        pe.wait_ge(q_a, n + 2 if more else n + 1)
                        pe.wait_ge(k_a, n + 2 if more else n + 1)
                        for h in range(HEADS):
                            for t in range(GT):
                                ins = pe.transpose(PS[:, h, t * P:(t + 1) * P], PF[:, h, t, :], ident[:])
                            ins.then_inc(ptp_pe, 1)
                    if has(g, 0):
                        if ka == 0:
                            pe.wait_ge(tr_v, g + 1)
                        else:
                            pe.wait_ge(pt_a, 2 * g + 2)
                            pe.wait_ge(pt_v, g + 1)
                        weights = PT if ka == 1 else PA[p]
                        after(pe, xu[phase], g)
                        for t in range(GT):
                            for h in range(HEADS):
                                rows = slice(h * DH, (h + 1) * DH)
                                o = PS[rows, 6, t * P:(t + 1) * P]
                                if ka == 1:
                                    o = o.rearrange("p (r h c) -> p h r c", h=2, r=8)
                                ins = pe.matmul(o, V[:, t, rows], weights[:, h, t * P:(t + 1) * P], start=True, stop=True)
                        ins.then_inc(pv_pe, 1)
                    if has(g, 2):
                        xh, xl = XH[p], XL[p]
                        pe.wait_ge(lo_v, m + 3)
                        three(bank(0, 512, C), wh[:, 0:C], wl[:, 0:C], xh[:], xl[:]).then_inc(q_pe, 1)
                        three(bank(1, 512, C), wh[:, C:2 * C], wl[:, C:2 * C], xh[:], xl[:]).then_inc(k_pe, 1)
                    if ka == 0 and isinstance(g, int) and g == -2:
                        weight_sums()
                    if more:
                        xh, xl = XH[1 - p], XL[1 - p]
                        for t in range(GT):
                            ts = slice(t * P, (t + 1) * P)
                            ins = three(PS[:, 2, t * C:(t + 1) * C], xh[:, ts], xl[:, ts], wh[:, 2 * C:], wl[:, 2 * C:])
                        ins.then_inc(xt_used, 1)
                    if has(g, 3, 2, PREPS[phase]):
                        prep_turn(m + 3, ka == 1 and has(g, 3))
                    if ka == 0 and isinstance(g, int) and g == GROUPS - 1:
                        pe.wait_ge(wt_v, 7)
                        for j in range(6):
                            ffn_up(0, j)
                    if has(g, 0):
                        pe.wait_ge(ot_a, n + 1)
                        for t in range(GT):
                            ins = pe.matmul(PS[:, 6, t * C:(t + 1) * C], OT[:, t * P:(t + 1) * P], WM[ka][:],
                                            start=True, stop=True)
                        ins.then_inc(wo_pe, 1)
                attention_walk(pe, body)

            pe.wait_ge(watt, 16 * 12)
            prep_turn(0)
            for j in range(16):
                ins = pe.matmul(PS[:, 0, j * HEADS:(j + 1) * HEADS], EH[:, j, :], rel[:], start=True, stop=True)
            ins.then_inc(bias_pe, 1)
            prep_turn(1)
            pe.wait_ge(wffn, 16 * 4)
            for c in range(CH):
                ins = pe.transpose(PS[0:C, 1, c * P:(c + 1) * P], w1raw[:, c, :], ident[:])
            ins.then_inc(wt_pe, 1)
            for c in range(CH):
                ins = pe.transpose(PS[:, 2, c * C:(c + 1) * C], w2raw[:, c * P:(c + 1) * P], ident[0:C, 0:C])
            ins.then_inc(wt_pe, 1)
            pe.wait_ge(split_v, 4)
            pe.wait_ge(bias_v, 2)
            pe.wait_ge(wt_v, 1)
            pe.wait_ge(ms_v, 3)
            pe.wait_ge(ones_v, 1)
            attention(0, 0)

            pe.wait_ge(xu[0], GROUPS)

            def down(lo, hi):
                for t in range(lo, hi):
                    for c in range(CH):
                        ins = pe.matmul(PS[:, 3 + t // 3, (t % 3) * C:(t % 3 + 1) * C], YH[:, c, t * P:(t + 1) * P],
                                        W2B[:, c, :], start=c == 0, stop=c == CH - 1)
                return ins

            def second_max(r):
                pe.wait_ge(gm2_v, 2 * r + 1)
                pe.wait_ge(qs1_v, 3 * min(r + 1, FG - 1) + 1)
                pe.transpose(PS[0:1, 7, 256:256 + P], am1[:, 1:2], ident[:]).then_inc(g2_pe, 1)

            def second_scale(r):
                pe.wait_ge(gm2_v, 2 * r + 2)
                pe.matmul(PS[:, 7, 384:385], onesf[0:1, :], gmx[:, 1:2], start=True, stop=True).then_inc(g2_pe, 1)

            for q in range(-1, FG + 1):
                r = q - 1
                for j in range(6):
                    if 0 < q + 1 < FG:
                        ffn_up(q + 1, j)
                    if r >= 0 and j == 2:
                        second_max(r)
                    if r >= 0 and j == 4:
                        second_scale(r)
                if q + 2 < FG:
                    ffn_turn(q + 2)
                if 0 <= q + 1 < FG:
                    pe.wait_ge(gm1_v, 2 * (q + 1) + 1)
                    after(pe, qs2_v, 3 * (q - 1) + 1)
                    pe.transpose(PS[0:1, 7, 0:P], am1[:, 0:1], ident[:]).then_inc(g1_pe, 1)
                if 0 <= q < FG:
                    pe.wait_ge(ge_a, 3 * q + 3)
                    after(pe, y2_v, 3 * q)
                    down(0, 2)
                if 0 <= q + 1 < FG:
                    pe.wait_ge(gm1_v, 2 * (q + 1) + 2)
                    pe.matmul(PS[:, 7, P:P + 1], onesf[0:1, :], gmx[:, 0:1], start=True, stop=True).then_inc(g1_pe, 1)
                if 0 <= q < FG:
                    down(2, 3).then_inc(fd_pe, 1)
                    down(3, 6).then_inc(fd_pe, 1)
            pe.wait_ge(qs2_v, 3 * (FG - 1) + 1)
            prep_turn(8, True)
            prep_turn(9, True)
            attention(2, 1)

            def moe(phase, k, e, busy):
                def up(b, p, lo, hi):
                    for c in range(lo, hi):
                        if isinstance(b, int) and b == 8 * e and c == busy:
                            pe.wait_ge(xu[phase - 1], GROUPS)
                        after(pe, gelu_a, CK * b + c - 3)
                        cs = slice(c * P, (c + 1) * P)
                        three(bank(c % 4), M1h[e][:, cs], M1l[e][:, cs], XH[p][:], XL[p][:]).then_inc(up_pe, 1)

                def gate(b, p):
                    after(pe, gate_v, NGV * b - NGV + 1)
                    for t in range(GT):
                        ts, o = slice(t * P, (t + 1) * P), 2 * t * EXP
                        pe.matmul(PS[:, 6, o:o + 2 * EXP], XH[p][:, ts], GW[e][:], start=True, stop=False)
                        ins = pe.matmul(PS[:, 6, o:o + EXP], XL[p][:, ts], GW[e][:, 0:EXP], start=False, stop=True)
                    ins.then_inc(xt_used, 1)

                def down(b, g, p, t):
                    Y = bank(4 + t % 2, EXP * C)
                    if t == 0:
                        pe.wait_ge(gelu_a, CK * b + CK)
                    after(pe, comb_v, 4 * b + t - 1)
                    for x in range(EXP):
                        for c in range(CH):
                            j = x * CH + c
                            ins = pe.matmul(Y[:, x * C:(x + 1) * C], H[p][:, j, t * P:(t + 1) * P], M2[e][:, j, :],
                                            start=c == 0, stop=c == CH - 1)
                    ins.then_inc(dn_pe, 1)

                def body(g, p):
                    b, m = 8 * e + g, 8 * k + g
                    if has(g, 1):
                        pe.wait_ge(lo_v, m + 2)
                    for t in range(GT):
                        if has(g, 1):
                            up(b + 1, 1 - p, 3 * t, 3 * t + 3)
                        if has(g, 0):
                            down(b, g, p, t)
                        if t == 1 and has(g, 2, 2, PREPS[phase]):
                            prep_turn(m + 2)
                    if has(g, 1):
                        if isinstance(g, int) and g == -1:
                            pe.wait_ge(xu[phase - 1], GROUPS)
                        gate(b + 1, 1 - p)
                moe_walk(pe, body)

            pe.wait_ge(split_v, 8)
            moe(3, 2, 0, 6)

            def mix_h(kc, k, g, p):
                m = 8 * k + g
                pe.wait_ge(lo_v, m + 2)
                for t in range(GT):
                    ts = slice(t * P, (t + 1) * P)
                    ins = three(PS[:, 4 + t // 2, (t % 2) * WID[kc]:(t % 2 + 1) * WID[kc]], XH[1 - p][0:C, ts], XL[1 - p][0:C, ts],
                                PWh[kc][:], PWl[kc][:])
                    if t == 1:
                        ins.then_inc(h_pe, 1)
                ins.then_inc(xt_used, 1)

            def mix_dft(kc, g):
                s = 8 * kc + g + 1
                for j in BY_IMAGE:
                    c, i = j // 2, j % 2
                    pe.wait_ge(h_v, 2 * s + i + 1)
                    if kc == 0 and j == 3:
                        after(pe, z_a, 4 * g + 1)
                    if kc == 1 and j == 3:
                        after(pe, prod_v, 12 * g + 3)
                    for kk in range(2):
                        w = WID[kc] // 2
                        ins = pe.matmul(bank(DB[kc][j], 2 * FR, w), HH[kc][:, 2 * i + kk, c * w:(c + 1) * w], FDFT[:, kk, :],
                                        start=kk == 0, stop=kk == 1)
                    ins.then_inc(dft_pe, 1)

            def mix_channels(kc, g):
                if isinstance(g, int) and g == 0:
                    pe.wait_ge(pad_v, kc + 1)
                for i in range(2):
                    if kc == 1:
                        pe.wait_ge(y_p, 4 * g + 2 * i + 2)
                    for n in range(3):
                        for c in range(2):
                            ins = pe.matmul(PS[0:C, PB[kc][i], n * C:(n + 1) * C], OU[:, c, i, n * C:(n + 1) * C],
                                            PO[kc][:, c, :], start=c == 0, stop=c == 1)
                    ins.then_inc(pp_pe, 1)

            def mix_tokens(kc, g):
                s = 8 * kc + g
                for i in range(2):
                    pe.wait_ge(ps_a, 2 * s + i + 1)
                    for kk in range(2):
                        t = 2 * i + kk
                        for n in range(3):
                            ins = pe.matmul(PS[:, IB[kc], t * C:(t + 1) * C], GDFT[:, n, kk * P:(kk + 1) * P],
                                            PSs[:, i, n * C:(n + 1) * C], start=n == 0, stop=n == 2)
                ins.then_inc(id_pe, 1)

            def block_mlp(w, src, banks, done, g=0):
                for j in range(4):
                    if banks[j] == IB[0] and w == 0:
                        after(pe, xu[4], g)
                    pe.matmul(bank(banks[j], 2 * FR), BW[w][:, j, :], src[:, j], start=True, stop=True).then_inc(done, 1)

            def mixer2(g, p):
                if has(g, 0):
                    pe.wait_ge(xf_a, 4 * g + 4)
                    block_mlp(0, XP[p].rearrange("p q i f -> p q (i f)"), (0, 1, 2, 3), m1_pe, g)
                if has(g, 1):
                    mix_h(0, 3, g, p)
                if has(g, 0):
                    pe.wait_ge(o1_a, 4 * g + 4)
                    block_mlp(1, O1, (6, 0, 1, 2), m2_pe)
                if has(g, 1):
                    mix_dft(0, g)
                if has(g, 2, 2, PREPS[4]):
                    prep_turn(24 + g + 2)
                if has(g, 0):
                    pe.wait_ge(o_v, 4 * g + 4)
                    mix_channels(0, g)
                    mix_tokens(0, g)
            pe.wait_ge(xu[3], GROUPS)
            pe.wait_ge(split_v, 14)
            mixer_walk(pe, mixer2)
            pe.wait_ge(split_v, 18)
            moe(5, 4, 1, IB[0])

            pe.wait_ge(xu[5], GROUPS)
            cwv = cwx[:].rearrange("p (f r) -> p f r", r=2)
            for j in range(3):
                pe.matmul(bank(j, FR, NF), cwv[:, :, min(j, 1)], RB[:], start=True, stop=True).then_inc(cw_pe, 1)

            def route_in(i, p):
                pe.wait_ge(pool_v, i + 1)
                pe.matmul(TB[0:24, 0:2], fc1[:], pl[:, p, :], start=True, stop=True).then_inc(f1_pe, 1)

            def route_logits(i):
                pe.wait_ge(rt_v, 5 * i + 1)
                for f in range(NF):
                    for c in range(2):
                        n = 16 + (f * 2 + c) * 2
                        w = f * MED + c * C
                        ins = pe.matmul(TB[:, n:n + 2], fc2[:, w:w + C], hh[:], start=True, stop=True)
                ins.then_inc(f2_pe, 1)

            def route_turn(i):
                pe.wait_ge(rt_m, i + 1)
                for q in range(4):
                    ins = pe.transpose(TB[0:NF, 128 + q * C:128 + (q + 1) * C], RTm[:, q // 2, q % 2, :], ident[0:C, 0:C])
                ins.then_inc(rt_pe, 1)

            for i in range(2):
                after(pe, rt_x, i)
                route_in(i, i)
                route_logits(i)
                route_turn(i)
            pe.wait_ge(cw_v, 2)

            def mixer3(g, p):
                if has(g, 0):
                    pe.wait_ge(xf_a, 32 + 4 * g + 4)
                if has(g, 1):
                    mix_h(1, 5, g, p)
                if has(g, 0):
                    pe.wait_ge(rt_x, g + 1)
                    pe.wait_ge(xf_a, 32 + 4 * g + 4)
                    for j in BY_IMAGE:
                        if j == 2:
                            after(pe, ps_a, 16 + 2 * g)
                        if j == 3:
                            after(pe, xu[6], g)
                        pe.matmul(bank(j, 3 * FR, C), RT[p][:, j, :], CWS[:], start=True, stop=True).then_inc(w_pe, 1)
                if has(g, 2, 2, PREPS[6]):
                    prep_turn(40 + g + 2, False, (rt_x, g + 2 if has(g, 2, 2, 8) else GROUPS))
                if has(g, 1):
                    mix_dft(1, g)
                if has(g, 2, 2):
                    route_in(g + 2, p)
                if has(g, 0):
                    mix_channels(1, g)
                if has(g, 2, 2):
                    route_logits(g + 2)
                if has(g, 0):
                    mix_tokens(1, g)
                if has(g, 2, 2):
                    route_turn(g + 2)
            mixer_walk(pe, mixer3)
            pe.wait_ge(split_v, 22)
            moe(7, 6, 2, IB[1])


def shape_constants():
    k = {"k_ident": np.eye(P)}
    i = np.arange(P)
    col = np.arange(32)
    same = ((i[:, None] % 32) // 16 == col[None, :] // 16).astype(np.float64)
    k["k_bm0"], k["k_bm1"] = same, (same - 1) * BIG
    e = np.arange(EXP)
    tie = np.stack([e[None, :] > e[:, None], e[None, :] < e[:, None]])
    k["k_tie"] = np.broadcast_to(tie[None], (P, 2, EXP, EXP))
    c = np.stack(np.meshgrid(np.arange(4), np.arange(4), indexing="ij")).reshape(2, -1)
    d = (c[:, :, None] - c[:, None, :] + 3).transpose(1, 2, 0)
    idx = d[..., 0] * 7 + d[..., 1]
    k["k_onehot"] = (idx[i % 16][None].transpose(0, 2, 1) == np.arange(49)[:, None, None])
    h, w = np.divmod(np.arange(HW * HW), HW)
    ky, kx = np.divmod(np.arange(FR), WF)
    th = 2 * np.pi * ((h[:, None] * ky[None] + w[:, None] * kx[None]) % HW) / HW
    fwd = np.concatenate([np.cos(th), -np.sin(th)], 1) / HW
    k["k_dft"] = fwd.reshape(2, P, 2 * FR).transpose(1, 0, 2)
    twice = np.where((kx == 0) | (kx == HW // 2), 1.0, 2.0)[:, None]
    inv = np.concatenate([np.cos(th).T * twice, -np.sin(th).T * twice]) / HW
    k["k_idft"] = inv.reshape(3, C, HW * HW).transpose(1, 0, 2)

    def cubic(old, new):
        A, m = -0.75, np.zeros((new, old))
        pos = np.arange(new, dtype=np.float32) * np.float32((old - 1) / (new - 1))
        i0 = np.floor(pos).astype(int)
        fr = (pos - i0.astype(np.float32)).astype(np.float64)
        for o in (-1, 0, 1, 2):
            t = np.abs(fr - o)
            w1 = ((A + 2) * t - (A + 3)) * t * t + 1
            w2 = A * (((t - 5) * t + 8) * t - 4)
            wt = np.where(t <= 1, w1, np.where(t < 2, w2, 0))
            for n in range(new):
                m[n, np.clip(i0[n] + o, 0, old - 1)] += wt[n]
        return m
    k["k_bicubic"] = np.kron(cubic(14, HW), cubic(8, WF)).T
    return {n: np.ascontiguousarray(v, dtype=np.float32) for n, v in k.items()}


def kernel(**inputs):
    import concourse.bacc as bacc
    from concourse.bass_utils import run_bass_kernel_spmd

    nc = bacc.Bacc("TRN2", target_bir_lowering=False, num_devices=1)
    arrays = {n: np.ascontiguousarray(v) for n, v in inputs.items()}
    arrays["x"] = arrays["x"].reshape(TOK, C)
    arrays.update(shape_constants())
    aps = {n: nc.dram_tensor(n, v.shape, mybir.dt.from_np(v.dtype), kind="ExternalInput").ap() for n, v in arrays.items()}
    out = nc.dram_tensor("out", (TOK, C), F32, kind="ExternalOutput").ap()
    program(nc, aps, out)
    r = run_bass_kernel_spmd(nc, [arrays], core_ids=[0])
    return r.results[0]["out"].reshape(IMGS, HW, HW, C)
```
